# Optimizing a Trainium2 kernel written in Bass

```python
import numpy as np
import jax
import jax.numpy as jnp

def _softmax(x, axis=-1):
    return jax.nn.softmax(x, axis=axis)

def _gelu(x):
    return jax.nn.gelu(x, approximate=True)

def _silu(x):
    return jax.nn.silu(x)

def _sigmoid(x):
    return jax.nn.sigmoid(x)

def _layernorm(x, axis=-1, eps=1e-05):
    m = jnp.mean(x, axis=axis, keepdims=True)
    v = jnp.var(x, axis=axis, keepdims=True)
    return (x - m) / jnp.sqrt(v + eps)

def _scatter_add(tgt, idx, src, axis=0):
    return tgt.at[idx].add(src)

def _segment_sum(src, seg, n):
    return jax.ops.segment_sum(src, seg, n)
kernel_name = 'mk_gnn_resnorm_d4_gnn_r64_4387b3'

def setup_inputs(seed: int=0):
    np.random.seed(seed)
    _w = jnp.asarray

    def _rec_inputs():
        import jax
        import jax.numpy as jnp
        _gk = jax.random.key(seed)
        x = -0.0005121 + 1.001 * jax.random.normal(jax.random.fold_in(_gk, 1), (100000, 32), jnp.float32)
        src = jax.random.randint(jax.random.fold_in(_gk, 2), (25000,), 0, 100000, jnp.int32)
        dst = jax.random.randint(jax.random.fold_in(_gk, 3), (25000,), 0, 100000, jnp.int32)
        _o = jnp.argsort(dst, stable=True)
        src = src[_o]
        dst = dst[_o]
        edge_attr_10 = jax.random.uniform(jax.random.fold_in(_gk, 12), (25000, 10), jnp.float32, 0.0, 0.999998)
        edge_attr_3 = 0.00158508 + 0.999651 * jax.random.normal(jax.random.fold_in(_gk, 13), (25000, 3), jnp.float32)
        edge_weight = jax.random.uniform(jax.random.fold_in(_gk, 14), (25000,), jnp.float32, 0.0, 0.999997)
        return (x, src, dst, edge_attr_10, edge_attr_3, edge_weight)
    x, src, dst, edge_attr_10, edge_attr_3, edge_weight = _rec_inputs()

    def _L0_gnn_setup():
        import jax, jax.numpy as jnp
        import numpy as np
        ALPHA = 0.1
        K = 10
        key = jax.random.key(seed)
        k1, k2, k3 = jax.random.split(key, 3)
        N, E, D = (100000, 25000, 32)
        feat = jax.random.normal(k1, (N, D), dtype=jnp.float32)
        src = jax.random.randint(k2, (E,), 0, N)
        dst = jax.random.randint(k3, (E,), 0, N)
        return {'feat': feat, 'src': src, 'dst': dst}
    _L0_gnn_all = _L0_gnn_setup()
    _L0_gnn_in = {k: v for k, v in _L0_gnn_all.items() if k in ()}
    del _L0_gnn_all

    def _L1_gnn_setup():
        import jax, jax.numpy as jnp
        import numpy as np
        SQRT3 = 3.0 ** 0.5

        def _mlp(emb, w1, w2):
            h = jax.nn.relu(emb @ w1 / jnp.sqrt(jnp.float32(w1.shape[0])))
            return h @ w2 / jnp.sqrt(jnp.float32(w2.shape[0]))
        key = jax.random.key(seed)
        ks = jax.random.split(key, 10)
        N, E = (10000, 2500)
        x = jax.random.normal(ks[0], (N, 32), jnp.float32)
        edge_src = jax.random.randint(ks[1], (E,), 0, N)
        edge_dst = jax.random.randint(ks[2], (E,), 0, N)
        edge_vec = jax.random.normal(ks[3], (E, 3), jnp.float32)
        emb = jax.random.uniform(ks[4], (E, 10), jnp.float32)
        norm = jax.random.uniform(ks[5], (E,), jnp.float32)
        fc1_w1 = jax.random.normal(ks[6], (10, 16), jnp.float32)
        fc1_w2 = jax.random.normal(ks[7], (16, 512), jnp.float32)
        fc2_w1 = jax.random.normal(ks[8], (10, 16), jnp.float32)
        fc2_w2 = jax.random.normal(ks[9], (16, 384), jnp.float32)
        return dict(x=x, edge_src=edge_src, edge_dst=edge_dst, edge_vec=edge_vec, emb=emb, norm=norm, num_nodes=N, fc1_w1=fc1_w1, fc1_w2=fc1_w2, fc2_w1=fc2_w1, fc2_w2=fc2_w2)
    _L1_gnn_all = _L1_gnn_setup()
    _L1_gnn_in = {k: v for k, v in _L1_gnn_all.items() if k in ('fc1_w1', 'fc1_w2', 'fc2_w1', 'fc2_w2')}
    del _L1_gnn_all

    def _L2_gnn_setup():
        import jax, jax.numpy as jnp
        import numpy as np
        N_NODES = 100000
        N_EDGES = 25000
        D_FEAT = 32
        key = jax.random.key(seed)
        k1, k2, k3 = jax.random.split(key, 3)
        x = jax.random.normal(k1, (N_NODES, D_FEAT), dtype=jnp.float32)
        edge_row = jax.random.randint(k2, (N_EDGES,), 0, N_NODES, dtype=jnp.int64)
        edge_col = jax.random.randint(k3, (N_EDGES,), 0, N_NODES, dtype=jnp.int64)
        return {'x': x, 'edge_row': edge_row, 'edge_col': edge_col}
    _L2_gnn_all = _L2_gnn_setup()
    _L2_gnn_in = {k: v for k, v in _L2_gnn_all.items() if k in ()}
    del _L2_gnn_all

    def _L3_gnn_setup():
        import jax, jax.numpy as jnp
        import numpy as np
        NEG_SLOPE = 0.2

        def _cheb(src, dst, n, x, norm, re_norm, W, b):

            def prop(h):
                return norm * jax.ops.segment_sum((h * norm)[src], dst, num_segments=n)
            X0 = x
            X1 = -re_norm * prop(X0) + X0 * (re_norm - 1.0)
            X2 = -2.0 * re_norm * prop(X1) + X1 * 2.0 * (re_norm - 1.0) - X0
            Xt = jnp.concatenate([X0, X1, X2], axis=1)
            return jax.nn.relu(Xt @ W.T + b)

        def _gatv2(src, dst, n, x, Wsrc, bsrc, Wdst, bdst, attn, bias):
            H, D = (attn.shape[1], attn.shape[2])
            fs = (x @ Wsrc.T + bsrc).reshape(n, H, D)
            fd = (x @ Wdst.T + bdst).reshape(n, H, D)
            e = jax.nn.leaky_relu(fs[src] + fd[dst], NEG_SLOPE)
            logits = jnp.sum(e * attn, axis=-1)
            m = jax.ops.segment_max(logits, dst, num_segments=n)
            m = jnp.where(jnp.isfinite(m), m, 0.0)
            ex = jnp.exp(logits - m[dst])
            s = jax.ops.segment_sum(ex, dst, num_segments=n)
            a = ex / s[dst]
            rst = jax.ops.segment_sum(a[:, :, None] * fs[src], dst, num_segments=n)
            return rst + bias.reshape(1, H, D)
        key = jax.random.key(seed)
        ks = jax.random.split(key, 8)
        N, E, Dm, K, Hh = (100000, 25000, 32, 3, 1)
        return {'user_embed': jax.random.normal(ks[0], (N, Dm), jnp.float32), 'src': jax.random.randint(ks[1], (E,), 0, N), 'dst': jax.random.randint(ks[2], (E,), 0, N), 'laplacian_lambda_max': jnp.ones((1,), jnp.float32), 'cheb_W': jax.random.normal(ks[3], (Dm, K * Dm), jnp.float32) * 0.1, 'cheb_b': jnp.zeros((Dm,), jnp.float32), 'gat_Wsrc': jax.random.normal(ks[4], (Hh * Dm, Dm), jnp.float32) * 0.1, 'gat_bsrc': jnp.zeros((Hh * Dm,), jnp.float32), 'gat_Wdst': jax.random.normal(ks[5], (Hh * Dm, Dm), jnp.float32) * 0.1, 'gat_bdst': jnp.zeros((Hh * Dm,), jnp.float32), 'gat_attn': jax.random.normal(ks[6], (1, Hh, Dm), jnp.float32) * 0.1, 'gat_bias': jnp.zeros((Hh * Dm,), jnp.float32)}
    _L3_gnn_all = _L3_gnn_setup()
    _L3_gnn_in = {k: v for k, v in _L3_gnn_all.items() if k in ('laplacian_lambda_max', 'cheb_W', 'cheb_b', 'gat_Wsrc', 'gat_bsrc', 'gat_Wdst', 'gat_bdst', 'gat_attn', 'gat_bias')}
    del _L3_gnn_all
    return {'x': x, 'src': src, 'dst': dst, 'edge_attr_10': edge_attr_10, 'edge_attr_3': edge_attr_3, 'edge_weight': edge_weight, 'L1_gnn_fc1_w1': _L1_gnn_in['fc1_w1'], 'L1_gnn_fc1_w2': _L1_gnn_in['fc1_w2'], 'L1_gnn_fc2_w1': _L1_gnn_in['fc2_w1'], 'L1_gnn_fc2_w2': _L1_gnn_in['fc2_w2'], 'L3_gnn_laplacian_lambda_max': _L3_gnn_in['laplacian_lambda_max'], 'L3_gnn_cheb_W': _L3_gnn_in['cheb_W'], 'L3_gnn_cheb_b': _L3_gnn_in['cheb_b'], 'L3_gnn_gat_Wsrc': _L3_gnn_in['gat_Wsrc'], 'L3_gnn_gat_bsrc': _L3_gnn_in['gat_bsrc'], 'L3_gnn_gat_Wdst': _L3_gnn_in['gat_Wdst'], 'L3_gnn_gat_bdst': _L3_gnn_in['gat_bdst'], 'L3_gnn_gat_attn': _L3_gnn_in['gat_attn'], 'L3_gnn_gat_bias': _L3_gnn_in['gat_bias']}

def reference(x, src, dst, edge_attr_10, edge_attr_3, edge_weight, L1_gnn_fc1_w1, L1_gnn_fc1_w2, L1_gnn_fc2_w1, L1_gnn_fc2_w2, L3_gnn_laplacian_lambda_max, L3_gnn_cheb_W, L3_gnn_cheb_b, L3_gnn_gat_Wsrc, L3_gnn_gat_bsrc, L3_gnn_gat_Wdst, L3_gnn_gat_bdst, L3_gnn_gat_attn, L3_gnn_gat_bias):
    import jax
    import jax.numpy as jnp

    def _L0_gnn_ref(feat, src, dst):
        import jax, jax.numpy as jnp
        import numpy as np
        ALPHA = 0.1
        K = 10
        N = feat.shape[0]
        deg = jax.ops.segment_sum(jnp.ones_like(dst, dtype=feat.dtype), dst, num_segments=N)
        norm = jnp.where(deg > 0, deg ** (-0.5), 0.0)[:, None]
        feat_0 = feat

        def step(h, _):
            h = h * norm
            h = jax.ops.segment_sum(h[src], dst, num_segments=N)
            h = h * norm
            h = (1.0 - ALPHA) * h + ALPHA * feat_0
            return (h, None)
        h, _ = jax.lax.scan(step, feat, None, length=K)
        return h

    def _L1_gnn_ref(x, edge_src, edge_dst, edge_vec, emb, norm, num_nodes, fc1_w1, fc1_w2, fc2_w1, fc2_w2):
        import jax, jax.numpy as jnp
        import numpy as np
        SQRT3 = 3.0 ** 0.5

        def _mlp(emb, w1, w2):
            h = jax.nn.relu(emb @ w1 / jnp.sqrt(jnp.float32(w1.shape[0])))
            return h @ w2 / jnp.sqrt(jnp.float32(w2.shape[0]))
        E = edge_vec.shape[0]
        r = edge_vec / jnp.linalg.norm(edge_vec, axis=1, keepdims=True)
        sh1 = SQRT3 * r
        xs, xd = (x[edge_src], x[edge_dst])
        s1 = jnp.concatenate([xs[:, :8], xd[:, :8]], axis=1)
        v1 = jnp.concatenate([xs[:, 8:].reshape(E, 8, 3), xd[:, 8:].reshape(E, 8, 3)], axis=1)
        w = _mlp(emb, fc1_w1, fc1_w2)
        Wss = w[:, 0:128].reshape(E, 16, 8)
        Wvv = w[:, 128:256].reshape(E, 16, 8)
        Wsv = w[:, 256:384].reshape(E, 16, 8)
        Wvs = w[:, 384:512].reshape(E, 16, 8)
        a1 = 1.0 / jnp.sqrt(32.0)
        vdot1 = jnp.einsum('euk,ek->eu', v1, sh1) / SQRT3
        s_t = a1 * (jnp.einsum('eu,euw->ew', s1, Wss) + jnp.einsum('eu,euw->ew', vdot1, Wvv))
        v_t = a1 * (jnp.einsum('eu,euw->ew', s1, Wsv)[:, :, None] * sh1[:, None, :] + jnp.einsum('euk,euw->ewk', v1, Wvs))
        w2 = _mlp(emb, fc2_w1, fc2_w2)
        Ass = w2[:, 0:64].reshape(E, 8, 8)
        Avv = w2[:, 64:128].reshape(E, 8, 8)
        Bss = w2[:, 128:192].reshape(E, 8, 8)
        Bvv = w2[:, 192:256].reshape(E, 8, 8)
        Csv = w2[:, 256:320].reshape(E, 8, 8)
        Cvs = w2[:, 320:384].reshape(E, 8, 8)
        a2 = 1.0 / jnp.sqrt(16.0)
        vdot2 = jnp.einsum('euk,ek->eu', v_t, sh1) / SQRT3
        scal = a2 * (jnp.einsum('eu,euw->ew', s_t, Ass) + jnp.einsum('eu,euw->ew', vdot2, Avv))
        gates = a2 * (jnp.einsum('eu,euw->ew', s_t, Bss) + jnp.einsum('eu,euw->ew', vdot2, Bvv))
        vecs = a2 * (jnp.einsum('eu,euw->ew', s_t, Csv)[:, :, None] * sh1[:, None, :] + jnp.einsum('euk,euw->ewk', v_t, Cvs))
        edge_out = jnp.concatenate([jnp.tanh(scal), (vecs * jnp.tanh(gates)[:, :, None]).reshape(E, 24)], axis=1)
        edge_out = edge_out * norm[:, None]
        return jax.ops.segment_sum(edge_out, edge_dst, num_segments=num_nodes)

    def _L2_gnn_ref(x, edge_row, edge_col):
        import jax, jax.numpy as jnp
        import numpy as np
        N_NODES = 100000
        N_EDGES = 25000
        D_FEAT = 32
        n = x.shape[0]
        deg = jax.ops.segment_sum(jnp.ones(edge_row.shape[0], dtype=x.dtype), edge_row, num_segments=n)
        norm = jax.lax.rsqrt(1.0 + deg)[:, None]
        xs = norm * x
        agg = jax.ops.segment_sum(xs[edge_col], edge_row, num_segments=n)
        return norm * (agg + xs)

    def _L3_gnn_ref(user_embed, src, dst, laplacian_lambda_max, cheb_W, cheb_b, gat_Wsrc, gat_bsrc, gat_Wdst, gat_bdst, gat_attn, gat_bias):
        import jax, jax.numpy as jnp
        import numpy as np
        NEG_SLOPE = 0.2

        def _cheb(src, dst, n, x, norm, re_norm, W, b):

            def prop(h):
                return norm * jax.ops.segment_sum((h * norm)[src], dst, num_segments=n)
            X0 = x
            X1 = -re_norm * prop(X0) + X0 * (re_norm - 1.0)
            X2 = -2.0 * re_norm * prop(X1) + X1 * 2.0 * (re_norm - 1.0) - X0
            Xt = jnp.concatenate([X0, X1, X2], axis=1)
            return jax.nn.relu(Xt @ W.T + b)

        def _gatv2(src, dst, n, x, Wsrc, bsrc, Wdst, bdst, attn, bias):
            H, D = (attn.shape[1], attn.shape[2])
            fs = (x @ Wsrc.T + bsrc).reshape(n, H, D)
            fd = (x @ Wdst.T + bdst).reshape(n, H, D)
            e = jax.nn.leaky_relu(fs[src] + fd[dst], NEG_SLOPE)
            logits = jnp.sum(e * attn, axis=-1)
            m = jax.ops.segment_max(logits, dst, num_segments=n)
            m = jnp.where(jnp.isfinite(m), m, 0.0)
            ex = jnp.exp(logits - m[dst])
            s = jax.ops.segment_sum(ex, dst, num_segments=n)
            a = ex / s[dst]
            rst = jax.ops.segment_sum(a[:, :, None] * fs[src], dst, num_segments=n)
            return rst + bias.reshape(1, H, D)
        n = user_embed.shape[0]
        deg = jax.ops.segment_sum(jnp.ones((src.shape[0],), user_embed.dtype), dst, num_segments=n)
        norm = jnp.clip(deg, 1.0, None)[:, None] ** (-0.5)
        re_norm = 2.0 / laplacian_lambda_max
        h = _cheb(src, dst, n, user_embed, norm, re_norm, cheb_W, cheb_b)
        h = _cheb(src, dst, n, h, norm, re_norm, cheb_W, cheb_b)
        out = _gatv2(src, dst, n, h, gat_Wsrc, gat_bsrc, gat_Wdst, gat_bdst, gat_attn, gat_bias)
        return out[:, 0, :]
    x = _layernorm(x + _L0_gnn_ref(x, src, dst), axis=-1)
    x = _layernorm(x + _L1_gnn_ref(x, src, dst, edge_attr_3, edge_attr_10, edge_weight, 100000, L1_gnn_fc1_w1, L1_gnn_fc1_w2, L1_gnn_fc2_w1, L1_gnn_fc2_w2), axis=-1)
    x = _layernorm(x + _L2_gnn_ref(x, src, dst), axis=-1)
    x = _layernorm(x + _L3_gnn_ref(x, src, dst, L3_gnn_laplacian_lambda_max, L3_gnn_cheb_W, L3_gnn_cheb_b, L3_gnn_gat_Wsrc, L3_gnn_gat_bsrc, L3_gnn_gat_Wdst, L3_gnn_gat_bdst, L3_gnn_gat_attn, L3_gnn_gat_bias), axis=-1)
    return x

_drawn_inputs = setup_inputs


def setup_inputs(seed=0):
    import zlib

    import numpy as np

    out = dict(_drawn_inputs(seed))
    spreads = {'L3_gnn_cheb_b': (0.0, 0.378),
     'L3_gnn_gat_bsrc': (0.0, 0.1),
     'L3_gnn_gat_bdst': (0.0, 0.8),
     'L3_gnn_gat_bias': (0.0, 0.1)}
    factors = {'edge_attr_10': 2.918,
     'edge_attr_3': 3.297,
     'edge_weight': 4.014,
     'L3_gnn_gat_Wdst': 4.178}
    for name, (base, spread) in spreads.items():
        noise = np.random.default_rng([zlib.crc32(name.encode()), seed]).standard_normal(out[name].shape)
        drawn = base * np.exp(spread * noise) if base else spread * noise
        out[name] = jnp.asarray(drawn.astype(out[name].dtype))
    for name, factor in factors.items():
        out[name] = (out[name] * factor).astype(out[name].dtype)
    return out
```

```python
import concourse.bass as bass
from concourse import mybir
from contextlib import ExitStack


def gnn_resnorm_kernel(nc, x, dst_ext, src_idx, ea10_t, ea3, ew, w1cat, fc1_w2, fc2_w2, lam,
                       cheb_wt, cheb_b, wsrc_t, bsrc, wdst_t, bdst, attn, gat_bias, out):
    fp32, i32, u8 = mybir.dt.float32, mybir.dt.int32, mybir.dt.uint8
    ALU = mybir.AluOpType
    ACT = mybir.ActivationFunctionType
    AX = mybir.AxisListType.X

    N, F = x.shape
    P = 128
    K = src_idx.shape[1]
    EP = P * K
    KF = K * F
    NONE = 200000
    EPS = 1e-5
    BIG = 1e30
    NP, NR = 125, N // 125
    ND = 10
    RC = NR // ND
    GC = 7
    KG = K // GC
    T1 = 7
    N1 = K // T1
    LC = 14
    LW = KF // LC
    H = w1cat.shape[1]
    HIN = w1cat.shape[0]
    W1C, W2C = fc1_w2.shape[1], fc2_w2.shape[1]
    WC = W1C + W2C
    S3 = 3.0 ** 0.5
    L0_ROUNDS = 10
    L1_LINKS = 14

    node_tab = nc.dram_tensor("node_tab", [N, 3], fp32).ap()
    out_tab = nc.dram_tensor("out_tab", [N + P, F], fp32).ap()
    ids_tab = nc.dram_tensor("ids_tab", [P, 4 * K], fp32).ap()
    agg_tab = nc.dram_tensor("agg_tab", [EP, F], fp32).ap()
    x3_tab = nc.dram_tensor("x3_tab", [P, KF], fp32).ap()

    ctx = ExitStack()
    with ctx:
        def sb(name, shape, dt=fp32):
            return ctx.enter_context(nc.sbuf_tensor(name, shape, dt))

        def sem(name):
            return ctx.enter_context(nc.semaphore(name))

        XS, XD, G, A, B, C = (sb(n, [P, KF]) for n in ("XS", "XD", "G", "A", "B", "C"))
        mask_f = sb("mask_f", [P, KF + 4], u8)
        U = sb("U", [P, 3 * T1 * P])
        r3 = sb("r3", [P, K * 3])
        last = sb("last", [P, K])
        m_first = sb("m_first", [P, K])
        m_last = sb("m_last", [P, K])
        ewt = sb("ewt", [P, K])
        live = sb("live", [P, K])
        norms = sb("norms", [P, 4, K])
        n3s, n2s, n3d, n2d = (norms[:, i, :] for i in range(4))
        n3live = sb("n3live", [P, K])
        cs1 = sb("cs1", [P, K])
        idx_last = sb("idx_last", [P, K], i32)
        ptr = sb("ptr", [P, K], i32)
        s1, s2, s3 = (sb(n, [P, K]) for n in ("s1", "s2", "s3"))
        ident = sb("ident", [P, P])
        M = sb("M", [P, P])
        MT = sb("MT", [P, P])
        cr = sb("cr", [P, F])
        tick = sb("tick", [P, 8])
        c_bias = sb("c_bias", [P, F])
        c_attn = sb("c_attn", [P, F])
        cols = sb("cols", [P, 8])
        cb, bs_c, bd_c, lam_c, nre, rm1, rm2, nre2 = (cols[:, i:i + 1] for i in range(8))

        dst_i = U[:, 0:K + 2].bitcast(i32)
        src_i = U[:, 200:200 + K].bitcast(i32)
        node_row = U[:, 400:400 + 3 * K].rearrange("p (k c) -> p k c", c=3)
        ids = U[:, 1024:1024 + 4 * K]
        src_g, dst_g, add_to = (U[:, 1024 + K * i:1024 + K * (i + 1)].bitcast(i32) for i in range(3))
        srcf = U[:, 1024 + 3 * K:1024 + 4 * K]
        d = U[:, 2004:2004 + K + 2]
        spare = U[:, 2210:2211]
        bcm = U[:, 2220:2220 + P]
        RN = NR
        fp16, bf16 = mybir.dt.float16, mybir.dt.bfloat16
        iota_c = G[:, 0:400].bitcast(fp16)
        iota_p = G[:, 400:464].bitcast(fp16)
        hot_c = [G[:, 464 + 400 * u:864 + 400 * u].bitcast(bf16) for u in range(2)]
        hot_p = [G[:, 1264 + 64 * u:1328 + 64 * u].bitcast(bf16) for u in range(2)]
        stage = G[0:NP, 1392:1392 + 3 * RN].rearrange("p (c w) -> p c w", w=3)
        iota_i = G[:, 1392:1392 + RN].bitcast(i32)
        iota_q = G[:, 2192:2192 + P].bitcast(i32)
        zeros = G[:, 3792:3792 + 1024]
        node_d = G[:, 4944:4944 + 3 * K]
        node_s = G[:, 5532:5532 + 3 * K]
        diag = sb("diag", [P, P])
        ones = sb("ones", [P, P])
        ea = [U[0:HIN, T1 * P * u:T1 * P * (u + 1)] for u in range(2)]
        hid = U[0:H, 2 * T1 * P:3 * T1 * P]
        BD = [U[:, P * i:P * (i + 1)] for i in range(5)]
        Wa, Wb, Wc = (U[:, P * i:P * (i + 1)] for i in range(5, 8))
        w1_sb = sb("w1_sb", [HIN, 2 * H])
        in48 = sb("in48", [P, T1, 48])
        vt = sb("vt", [P, T1, 3, 8])
        sums = sb("sums", [P, T1, 8, 8])
        gates = sb("gates", [P, K, 8])
        w2_sb = G[0:H, KF - WC:KF]

        psW = ctx.enter_context(nc.psum_tensor("psW", [P, 2, 1024], fp32))
        psH = ctx.enter_context(nc.psum_tensor("psH", [P, 1024], fp32))
        psC = ctx.enter_context(nc.psum_tensor("psC", [P, 512], fp32))

        def row(t):
            return t[:, 0:KF].rearrange("p (k f) -> p k f", f=F)

        def row_t(t):
            return t[:, 0:KF].rearrange("p (k f) -> p f k", f=F)

        def fm(t):
            return t[:, 0:KF].rearrange("p (f k) -> p f k", k=K)

        def over_f(s):
            return s.unsqueeze(2).broadcast_to([P, s.shape[1], F])

        def over_f_fm(s):
            return s.unsqueeze(1).broadcast_to([P, F, s.shape[1]])

        s_idx = sem("s_idx")
        s_small = sem("s_small")
        s_wts = sem("s_wts")
        s_w2 = sem("s_w2")
        iota_done = sem("iota_done")
        dst_g_ready = sem("dst_g_ready")
        idx_last_ready = sem("idx_last_ready")
        bc_ready = sem("bc_ready")
        bc_done = sem("bc_done")
        c_iota = sem("c_iota")
        hots_ready = sem("hots_ready")
        hist_mm = sem("hist_mm")
        stage_ready = sem("stage_ready")
        zeros_ready = sem("zeros_ready")
        node_stored = sem("node_stored")
        out_zeroed = sem("out_zeroed")
        node_d_got = sem("node_d_got")
        node_row_ready = sem("node_row_ready")
        node_scattered = sem("node_scattered")
        diag_ready = sem("diag_ready")
        same_done = sem("same_done")
        ids_ready = sem("ids_ready")
        ids_stored = sem("ids_stored")
        ids_back = sem("ids_back")
        equal_ready = sem("equal_ready")
        merged_mm = sem("merged_mm")
        merged_ready = sem("merged_ready")
        added = sem("added")
        out_s_got = sem("out_s_got")
        out_d_got = sem("out_d_got")
        dense_go = sem("dense_go")
        sums_in = sem("sums_in")
        sums_used = sem("sums_used")
        ptr_ready = sem("ptr_ready")
        hist_done = sem("hist_done")
        xd_got = sem("xd_got")
        xs_got = sem("xs_got")
        node_s_got = sem("node_s_got")
        x_in = [sem(f"x_in{i}") for i in range(2)]
        dense_ready = sem("dense_ready")
        dense_stored = [sem(f"dense_stored{i}") for i in range(2)]
        dve_step = sem("dve_step")
        var_ready = sem("var_ready")
        std_ready = sem("std_ready")
        scan_done = sem("scan_done")
        carry_done = sem("carry_done")
        table_ready = sem("table_ready")
        table_stored = sem("table_stored")
        got = [sem(f"got{i}") for i in range(GC)]
        ticked = sem("ticked")
        w1_blank = sem("w1_blank")
        w2_free = sem("w2_free")
        ea_in = [sem(f"ea_in{i}") for i in range(2)]
        hid_mm = sem("hid_mm")
        hid_ready = sem("hid_ready")
        wts_mm = sem("wts_mm")
        wts_ready = sem("wts_ready")
        l1_used = [sem(f"l1_used{i}") for i in range(2)]
        l1_tanh = sem("l1_tanh")
        wts_blank = sem("wts_blank")
        x3_ready = sem("x3_ready")
        x3_spilled = sem("x3_spilled")
        xd_free = sem("xd_free")
        x3_back = sem("x3_back")
        lin_in = sem("lin_in")
        lin_mm = sem("lin_mm")
        lin_out = sem("lin_out")
        ex_in = sem("ex_in")
        ex_out = sem("ex_out")
        res_ready = sem("res_ready")
        res_stored = sem("res_stored")

        x_v = x.rearrange("(p c r) f -> p c (r f)", p=NP, c=ND)
        out_v = out.rearrange("(p c r) f -> p c (r f)", p=NP, c=ND)
        agg_v = agg_tab.rearrange("(p k) f -> p (k f)", p=P)
        sum_v = out_tab[0:N, :].rearrange("(p c r) f -> p c (r f)", p=NP, c=ND)
        node_v = node_tab.rearrange("(p c r) w -> p c (r w)", p=NP, c=ND)
        DX = [B[0:NP, u * RC * F:(u + 1) * RC * F] for u in range(2)]
        DN = [B[0:NP, 2 * RC * F + u * RC * 3:2 * RC * F + (u + 1) * RC * 3] for u in range(2)]
        DS = C[0:NP, 0:RC * F]
        DQ = C[0:NP, RC * F:2 * RC * F]

        block = ctx.enter_context(nc.Block())

        @block.sync
        def _(sp):
            sp.dma_start(dst_i, dst_ext).then_inc(s_idx, 16)
            sp.dma_start(src_i, src_idx).then_inc(s_idx, 16)
            sp.dma_start(c_bias[:], gat_bias.unsqueeze(0).broadcast_to([P, F])).then_inc(s_small, 16)
            sp.dma_start(c_attn[:], attn.unsqueeze(0).broadcast_to([P, F])).then_inc(s_small, 16)
            sp.dma_start(lam_c, lam.unsqueeze(0).broadcast_to([P, 1])).then_inc(s_small, 16)
            for i in range(4):
                for c, v in ((cb, cheb_b), (bs_c, bsrc), (bd_c, bdst)):
                    sp.dma_start(c[F * i:F * (i + 1), :], v.unsqueeze(1)).then_inc(s_small, 16)
            sp.wait_ge(w1_blank, 1)
            sp.dma_start(w1_sb[:, 0:H], w1cat).then_inc(s_small, 16)
            sp.dma_start(ewt[:], ew).then_inc(s_small, 16)
            sp.dma_start(r3[:], ea3).then_inc(s_small, 16)
            sp.wait_ge(zeros_ready, 1)
            sp.dma_start(out_tab[0:N, :].rearrange("(p a r) f -> p a (r f)", p=NP, a=25),
                         zeros[0:NP, :].unsqueeze(1).broadcast_to([NP, 25, 1024])).then_inc(out_zeroed, 16)
            sp.dma_start(out_tab[N:N + P, :], zeros[:, 0:F]).then_inc(out_zeroed, 16)
            sp.wait_ge(stage_ready, 1)
            sp.dma_start(node_tab.rearrange("(p c) w -> p (c w)", p=NP),
                         stage.rearrange("p c w -> p (c w)")).then_inc(node_stored, 16)
            def store_table(r):
                sp.wait_ge(table_ready, r + 1)
                sp.dma_start(agg_v, A[:]).then_inc(table_stored, 16)

            sp.wait_ge(ids_ready, 1)
            sp.dma_start(ids_tab, ids).then_inc(ids_stored, 16)
            with sp.Fori(0, L0_ROUNDS) as i:
                store_table(i)
            sp.wait_ge(w2_free, 1)
            sp.dma_start(w2_sb[0:H // 2, 0:W1C], fc1_w2).then_inc(s_w2, 16)
            sp.dma_start(w2_sb[H // 2:H, W1C:WC], fc2_w2).then_inc(s_w2, 16)
            for u in range(2):
                sp.dma_start(ea[u], ea10_t[:, u * T1 * P:(u + 1) * T1 * P]).then_inc(ea_in[u], 16)
            with sp.Fori(0, N1 // 2 - 1) as i:
                for u in range(2):
                    sp.wait_ge(hid_mm, i * 2 + u + 1)
                    sp.dma_start(ea[u], ea10_t[:, bass.ds((i * 2 + 2 + u) * (T1 * P), T1 * P)]).then_inc(ea_in[u], 16)
            store_table(L0_ROUNDS)
            sp.wait_ge(wts_blank, 1)
            for q in range(4):
                sl = slice(F * q, F * (q + 1))
                for i in range(3):
                    sp.dma_start(BD[i][sl, sl], cheb_wt[F * i:F * (i + 1), :]).then_inc(s_wts, 16)
                sp.dma_start(BD[3][sl, sl], wsrc_t).then_inc(s_wts, 16)
                sp.dma_start(BD[4][sl, sl], wdst_t).then_inc(s_wts, 16)
            sp.wait_ge(ids_stored, 16)
            sp.dma_start(ids, ids_tab).then_inc(ids_back, 16)
            sp.wait_ge(added, 16 * K)
            sp.wait_ge(dense_go, 1)

            def load_dense(t):
                u = t % 2
                sp.dma_start(DX[u], x_v[:, t, :]).then_inc(x_in[u], 16)
                sp.dma_start(DN[u], node_v[:, t, :]).then_inc(x_in[u], 16)

            for t in range(2):
                load_dense(t)
            for t in range(ND):
                if t:
                    sp.wait_ge(sums_used, t)
                sp.dma_start(DS, sum_v[:, t, :]).then_inc(sums_in, 16)
                if t:
                    sp.wait_ge(dense_ready, t)
                    sp.dma_start(out_v[:, t - 1, :], DX[(t - 1) % 2]).then_inc(dense_stored[(t - 1) % 2], 16)
                    if t + 1 < ND:
                        sp.wait_ge(dense_stored[(t - 1) % 2], 16 * ((t - 1) // 2 + 1))
                        load_dense(t + 1)
            sp.wait_ge(dense_ready, ND)
            sp.dma_start(out_v[:, ND - 1, :], DX[(ND - 1) % 2]).then_inc(dense_stored[(ND - 1) % 2], 16)
            sp.wait_ge(x3_ready, 1)
            sp.dma_start(x3_tab, XD[:]).then_inc(x3_spilled, 16)
            for r in range(4):
                store_table(L0_ROUNDS + 1 + r)
            sp.wait_ge(xd_free, 1)
            sp.dma_start(XD[:], x3_tab).then_inc(x3_back, 16)
            sp.wait_ge(res_stored, 16 * K)
            for u in range(2):
                sp.wait_ge(dense_stored[u], 16 * (ND // 2))

        @block.gpsimd
        def _(pool):
            for j, (sm, n) in enumerate(((hist_mm, 2), (hid_ready, 1), (wts_ready, 1), (l1_used[0], 1),
                                         (l1_used[1], 1), (ticked, 1))):
                nc.gpsimd.memset(tick[:, j:j + 1], 0.0).then_inc(sm, n)
            nc.gpsimd.memset(ident[:], 1.0).then_inc(iota_done, 1)
            nc.gpsimd.iota(iota_i, [[1, RN]], base=0, channel_multiplier=0).then_inc(c_iota, 1)
            nc.gpsimd.iota(iota_q, [[1, P]], base=0, channel_multiplier=0).then_inc(c_iota, 1)
            nc.gpsimd.iota(node_row[:, :, 0].bitcast(i32), [[1, K]], base=0, channel_multiplier=K).then_inc(c_iota, 1)
            nc.gpsimd.iota(spare.bitcast(i32), [[1, 1]], base=N, channel_multiplier=1).then_inc(c_iota, 1)
            nc.gpsimd.memset(zeros, 0.0).then_inc(zeros_ready, 1)
            nc.gpsimd.memset(ones[:], 1.0).then_inc(iota_done, 1)
            nc.gpsimd.memset(M[:], 1.0).then_inc(iota_done, 1)
            nc.gpsimd.memset(MT[:], 1.0).then_inc(iota_done, 1)
            pool.wait_ge(iota_done, 4)
            nc.gpsimd.affine_select(ident[:], ident[:], [[-1, P]], ALU.is_equal, 0.0, base=0,
                                    channel_multiplier=1).then_inc(iota_done, 1)
            nc.gpsimd.affine_select(M[:], M[:], [[1, P]], ALU.is_gt, 0.0, base=0,
                                    channel_multiplier=-1).then_inc(iota_done, 1)
            nc.gpsimd.affine_select(MT[:], MT[:], [[-1, P]], ALU.is_gt, 0.0, base=0,
                                    channel_multiplier=1).then_inc(iota_done, 1)

            def gather(dst, table, idx, bound, k, w=F):
                return nc.gpsimd.indirect_dma_start(dst[:, k * w:(k + 1) * w], None, table,
                                                    bass.IndirectOffsetOnAxis(idx[:, k:k + 1], 0),
                                                    bounds_check=bound, oob_is_err=False)

            def scatter(table, src, idx, k, w=F):
                return nc.gpsimd.indirect_dma_start(table, bass.IndirectOffsetOnAxis(idx[:, k:k + 1], 0),
                                                    src[:, k * w:(k + 1) * w], None, bounds_check=N - 1,
                                                    oob_is_err=False)

            pool.wait_ge(dst_g_ready, 2)
            for k in range(K):
                gather(XD, x, dst_g, N - 1, k).then_inc(xd_got, 16)
            for k in range(K):
                gather(XS, x, src_g, N - 1, k).then_inc(xs_got, 16)
            pool.wait_ge(node_stored, 16)
            for k in range(K):
                gather(node_d, node_tab, dst_g, N - 1, k, 3).then_inc(node_d_got, 16)
            pool.wait_ge(node_row_ready, 1)
            for k in range(K):
                scatter(node_tab, U[:, 400:400 + 3 * K], idx_last, k, 3).then_inc(node_scattered, 16)
            pool.wait_ge(node_scattered, 16 * K)
            for k in range(K):
                gather(node_s, node_tab, src_g, N - 1, k, 3).then_inc(node_s_got, 16)
            pool.wait_ge(ptr_ready, 1)

            def gather_round(r):
                pool.wait_ge(ticked, r + 1)
                pool.wait_ge(table_stored, r * 16 + 16)
                nc.gpsimd.tensor_tensor(tick[:, 5:6], ident[:, 0:1], ident[:, 0:1], ALU.add).then_inc(ticked, 1)
                for k in range(K):
                    gather(G, agg_tab, ptr, EP - 1, k).then_inc(got[k // KG], 16)

            with pool.Fori(0, L0_ROUNDS + 1) as r:
                gather_round(r)
            pool.wait_ge(ids_back, 16)
            pool.wait_ge(out_zeroed, 32)
            for k in range(K):
                pool.wait_ge(merged_ready, k + 1)
                if k:
                    pool.wait_ge(added, 16 * k)
                nc.gpsimd.indirect_dma_start(out_tab, bass.IndirectOffsetOnAxis(add_to[:, k:k + 1], 0),
                                             C[:, k * F:(k + 1) * F], None, bounds_check=N + P - 1,
                                             oob_is_err=True, compute_op=ALU.add).then_inc(added, 16)
            pool.wait_ge(added, 16 * K)
            for k in range(K):
                gather(G, out_tab, src_g, N - 1, k).then_inc(out_s_got, 16)
            for k in range(K):
                gather(A, out_tab, dst_g, N - 1, k).then_inc(out_d_got, 16)
            with pool.Fori(L0_ROUNDS + 1, L0_ROUNDS + 5) as r:
                gather_round(r)
            for u in range(2):
                pool.wait_ge(dense_stored[u], 16 * (ND // 2))
            pool.wait_ge(res_ready, 1)
            for k in range(K):
                scatter(out, A, idx_last, k).then_inc(res_stored, 16)

        @block.tensor
        def _(pe):
            pe.wait_ge(zeros_ready, 1)
            zb = zeros.bitcast(bf16)
            for o, w in ((0, 512), (512, RN - 512)):
                nc.tensor.matmul(psW[:, 0, o:o + w], zb[:, 0:P], zb[:, 0:w], start=True, stop=False,
                                 skip_group_check=True)
            with pe.Fori(0, K // 2) as i:
                for u in range(2):
                    pe.wait_ge(hots_ready, i * 2 + u + 1)
                    nc.tensor.matmul(psW[:, 0, 0:512], hot_p[u][:, 0:P], hot_c[u][:, 0:512], start=False,
                                     stop=False, skip_group_check=True)
                    nc.tensor.matmul(psW[:, 0, 512:RN], hot_p[u][:, 0:P], hot_c[u][:, 512:RN], start=False,
                                     stop=False, skip_group_check=True).then_inc(hist_mm, 1)
            for o, w in ((0, 512), (512, RN - 512)):
                mm = nc.tensor.matmul(psW[:, 0, o:o + w], zb[:, 0:P], zb[:, 0:w], start=False, stop=True,
                                      skip_group_check=True)
            mm.then_inc(hist_done, 1)
            pe.wait_ge(iota_done, 7)
            with pe.Fori(0, K) as k:
                pe.wait_ge(diag_ready, k + 1)
                nc.tensor.matmul(psC[:, 0:P], ones[:], diag[:], start=True, stop=True).then_inc(same_done, 1)
            for t in range(2):
                pe.wait_ge(bc_ready, t + 1)
                nc.tensor.matmul(psC[:, P * t:P * (t + 1)], bcm, ident[:], start=True, stop=True).then_inc(bc_done, 1)

            def carry(q, src, matrix, width=F):
                pe.wait_ge(scan_done, q + 1)
                rhs = fm(src)[:, :, K - 1] if matrix is M else fm(src)[:, :, 0]
                nc.tensor.matmul(psC[:, 0:F], matrix[:], rhs, start=True, stop=True).then_inc(carry_done, 1)

            def carry1(q, src, lhs):
                pe.wait_ge(scan_done, q + 1)
                nc.tensor.matmul(psC[:, 0:src.shape[1]], lhs, src, start=True, stop=True).then_inc(carry_done, 1)

            carry1(0, s1[:, K - 1:K], M[:])
            with pe.Fori(0, L0_ROUNDS) as i:
                carry(i + 1, B, M)
            carry(L0_ROUNDS + 1, B, MT)
            pe.wait_ge(s_small, 16 * 18)
            pe.wait_ge(s_w2, 32)
            with pe.Fori(0, N1 // 2) as i:
                for u in range(2):
                    n = i * 2 + u
                    pe.wait_ge(ea_in[u], i * 16 + 16)
                    pe.wait_ge(hid_ready, n + 1)
                    nc.tensor.matmul(psH[0:2 * H, 0:512], w1_sb[:], ea[u][:, 0:512], start=True, stop=True)
                    nc.tensor.matmul(psH[0:2 * H, 512:T1 * P], w1_sb[:], ea[u][:, 512:T1 * P],
                                     start=True, stop=True).then_inc(hid_mm, 1)
                    pe.wait_ge(hid_ready, n + 2)
                    for t in range(T1):
                        m = i * (2 * T1) + (u * T1 + t)
                        slot = (u * T1 + t) % 2
                        pe.wait_ge(wts_ready, m + 1 if (u, t) == (0, 0) else m)
                        nc.tensor.matmul(psW[:, slot, 0:W1C], hid[:, t * P:(t + 1) * P], w2_sb[:, 0:W1C],
                                         start=True, stop=True)
                        nc.tensor.matmul(psW[:, slot, 512:512 + W2C], hid[:, t * P:(t + 1) * P],
                                         w2_sb[:, W1C:WC], start=True, stop=True).then_inc(wts_mm, 1)
            carry(L0_ROUNDS + 2, C, M)
            carry(L0_ROUNDS + 3, C, MT)
            with pe.Fori(0, K) as k:
                pe.wait_ge(diag_ready, k + (K + 1))
                nc.tensor.matmul(psC[:, 0:P], ones[:], diag[:], start=True, stop=True).then_inc(same_done, 1)
                pe.wait_ge(equal_ready, k + 1)
                nc.tensor.matmul(psC[:, P:P + F], B[:, 0:P], A[:, bass.ds(k * F, F)], start=True, stop=True).then_inc(merged_mm, 1)

            def linear(n, pairs):
                pe.wait_ge(lin_in, n + 1)
                for c in range(LC):
                    g = n * LC + c
                    if g >= 4:
                        pe.wait_ge(lin_out, g - 3)
                    o = psW[:, (g // 2) % 2, 512 * (g % 2):512 * (g % 2) + LW]
                    for i, (t, w) in enumerate(pairs):
                        mm = nc.tensor.matmul(o, w, t[:, c * LW:(c + 1) * LW], start=(i == 0),
                                              stop=(i == len(pairs) - 1))
                    mm.then_inc(lin_mm, 1)

            for layer in range(2):
                q = L0_ROUNDS + 4 + 2 * layer
                carry(q, B, M)
                linear(4 * layer, [(C, Wa), (A, Wb)])
                linear(4 * layer + 1, [(C, Wa), (XS, Wb)])
                carry(q + 1, B, M)
                linear(4 * layer + 2, [(C, Wc), (XD, ident[:])])
                linear(4 * layer + 3, [(C, Wc), (XS, ident[:])])
            linear(8, [(C, BD[3])])
            linear(9, [(C, BD[4])])
            q = L0_ROUNDS + 8
            carry(q, B, MT)
            carry1(q + 1, ident[:], A[:, 0:P])
            carry1(q + 2, s1[:, 0:1], MT[:])
            carry1(q + 3, s1[:, K - 1:K], M[:])
            carry(q + 4, B, M)

        @block.scalar
        def _(act):
            nstd = [0]

            def sqrt(t):
                act.wait_ge(var_ready, nstd[0] + 1)
                nc.scalar.activation(t, t, ACT.Sqrt).then_inc(std_ready, 1)
                nstd[0] += 1

            sqrt(s2[:])
            sqrt(norms[:].rearrange("p a k -> p (a k)"))
            sqrt(s2[:])
            sqrt(s2[:])
            with act.Fori(0, N1 // 2) as i:
                for u in range(2):
                    n = i * 2 + u
                    W = (B, C)[u][:, 0:T1 * WC].rearrange("p (t w) -> p t w", w=WC)
                    act.wait_ge(hid_mm, n + 1)
                    nc.scalar.activation(hid, psH[0:H, 0:T1 * P], ACT.Relu, scale=float(HIN) ** -0.5).then_inc(hid_ready, 1)
                    act.wait_ge(l1_used[u], i + 1)
                    for t in range(T1):
                        m = i * (2 * T1) + (u * T1 + t)
                        slot = (u * T1 + t) % 2
                        act.wait_ge(wts_mm, m + 1)
                        nc.scalar.activation(W[:, t, 0:W1C], psW[:, slot, 0:W1C], ACT.Copy,
                                             scale=0.25 / 32.0 ** 0.5)
                        nc.scalar.activation(W[:, t, W1C:WC], psW[:, slot, 512:512 + W2C], ACT.Copy,
                                             scale=0.25 / 4.0).then_inc(wts_ready, 1)
            act.wait_ge(wts_blank, 1)
            nc.scalar.activation(row(A)[:, :, 0:8], row(A)[:, :, 0:8], ACT.Tanh)
            nc.scalar.activation(gates[:], gates[:], ACT.Tanh).then_inc(l1_tanh, 1)
            sqrt(s2[:])
            sqrt(s2[:])
            for t in range(ND):
                sqrt(s1[0:NP, 0:2 * RC])
                sqrt(s1[0:NP, 0:RC])
                sqrt(s1[0:NP, 0:RC])
            sqrt(s2[:])
            sqrt(s2[:])

            def take(n, dst, func, bias=None):
                for c in range(LC):
                    g = n * LC + c
                    act.wait_ge(lin_mm, g + 1)
                    o = psW[:, (g // 2) % 2, 512 * (g % 2):512 * (g % 2) + LW]
                    if bias is None:
                        nc.scalar.activation(dst[:, c * LW:(c + 1) * LW], o, func).then_inc(lin_out, 1)
                    else:
                        nc.scalar.activation(dst[:, c * LW:(c + 1) * LW], o, func, bias=bias).then_inc(lin_out, 1)

            act.wait_ge(x3_spilled, 16)
            for layer in range(2):
                take(4 * layer, XD, ACT.Identity, cb)
                take(4 * layer + 1, XS, ACT.Identity, cb)
                take(4 * layer + 2, B, ACT.Relu)
                take(4 * layer + 3, B, ACT.Relu)
            take(8, B, ACT.Identity, bs_c)
            take(9, B, ACT.Identity, bd_c)
            act.wait_ge(ex_in, 1)
            nc.scalar.activation(s2[:], s2[:], ACT.Exp).then_inc(ex_out, 1)
            sqrt(s2[:])

        @block.vector
        def _(dve):
            v = nc.vector
            steps = [0]
            loop = [None, 0]

            def link(ins):
                steps[0] += 1
                ins.then_inc(dve_step, 1)
                n = steps[0]
                dve.wait_ge(dve_step, n if loop[0] is None else loop[0] * loop[1] + n)

            nstd = [0]

            def root(ins):
                ins.then_inc(var_ready, 1)
                nstd[0] += 1
                dve.wait_ge(std_ready, nstd[0])

            v.memset(w1_sb[:], 0.0).then_inc(w1_blank, 1)
            dve.wait_ge(s_idx, 32)
            v.tensor_copy(d, dst_i)
            link(v.tensor_copy(srcf, src_i))
            v.tensor_scalar(dst_g, d[:, 1:K + 1], float(N - 1), None, ALU.min).then_inc(dst_g_ready, 1)
            v.tensor_scalar(src_g, srcf, float(N - 1), None, ALU.min).then_inc(dst_g_ready, 1)
            link(v.tensor_tensor(last[:], d[:, 1:K + 1], d[:, 2:K + 2], ALU.not_equal))
            link(v.tensor_scalar(s1[:], d[:, 1:K + 1], float(-NONE), None, ALU.add))
            link(v.tensor_tensor(s1[:], s1[:], last[:], ALU.mult))
            link(v.tensor_scalar(idx_last[:], s1[:], float(NONE), None, ALU.add))
            link(v.tensor_tensor(s2[:], d[:, 1:K + 1], d[:, 0:K], ALU.is_equal))
            link(v.memset(s2[:, 0:1], 0.0))
            link(v.memset(mask_f[:], 0))
            link(v.tensor_copy(fm(mask_f), over_f_fm(s2[:])))
            link(v.tensor_scalar(m_first[:], d[:, 1:K + 1], d[:, 1:2], None, ALU.is_equal))
            link(v.tensor_scalar(m_last[:], d[:, 1:K + 1], d[:, K:K + 1], None, ALU.is_equal))

            dve.wait_ge(c_iota, 4)
            v.tensor_copy(iota_c, iota_i)
            v.tensor_copy(iota_p, iota_q)
            v.tensor_copy(node_row[:, :, 0], node_row[:, :, 0].bitcast(i32))
            link(v.tensor_copy(spare, spare.bitcast(i32)))
            link(v.tensor_scalar(s3[:].bitcast(i32), srcf, 1.0 / RN, None, ALU.mult))
            link(v.tensor_copy(s2[:], s3[:].bitcast(i32)))
            link(v.scalar_tensor_tensor(s1[:], s2[:], float(-RN), srcf, ALU.mult, ALU.add))
            for test, by in ((ALU.is_lt, -1.0), (ALU.is_ge, 1.0)):
                link(v.tensor_scalar(s3[:], s1[:], 0.0 if by < 0 else float(RN), None, test))
                link(v.scalar_tensor_tensor(s2[:], s3[:], by, s2[:], ALU.mult, ALU.add))
                link(v.scalar_tensor_tensor(s1[:], s3[:], -by * RN, s1[:], ALU.mult, ALU.add))
            with dve.Fori(0, K // 2) as i:
                for u in range(2):
                    col = bass.ds(i * 2 + u, 1)
                    dve.wait_ge(hist_mm, i * 2 + u + 1)
                    v.tensor_scalar(hot_p[u][:, 0:P], iota_p[:, 0:P], s2[:, col], None, ALU.is_equal)
                    v.tensor_scalar(hot_c[u][:, 0:RN], iota_c[:, 0:RN], s1[:, col], None,
                                    ALU.is_equal).then_inc(hots_ready, 1)
            dve.wait_ge(hist_done, 1)
            link(v.memset(stage[:, :, 0:2], 0.0))
            link(v.memset(stage[:, :, 0:1], float(NONE)))
            v.tensor_copy(stage[:, :, 2], psW[0:NP, 0, 0:RN]).then_inc(stage_ready, 1)

            dve.wait_ge(iota_done, 7)
            base = steps[0]
            with dve.Fori(0, K) as k:
                loop[0], loop[1] = k, 1
                v.tensor_scalar(diag[:], ident[:], srcf[:, bass.ds(k, 1)], None, ALU.mult).then_inc(diag_ready, 1)
                dve.wait_ge(same_done, k + 1)
                link(v.scalar_tensor_tensor(bcm, psC[:, 0:P], srcf[:, bass.ds(k, 1)], MT[:], ALU.is_equal, ALU.mult,
                                            accum_out=s3[:, bass.ds(k, 1)]))
            loop[0] = None
            steps[0] = base + K
            link(v.tensor_scalar(s1[:], srcf, float(N), None, ALU.is_lt))
            link(v.scalar_tensor_tensor(s3[:], s3[:], 0.0, s1[:], ALU.is_equal, ALU.mult))
            link(v.scalar_tensor_tensor(s1[:], srcf, spare, s3[:], ALU.subtract, ALU.mult))
            v.tensor_scalar(add_to, s1[:], spare, None, ALU.add).then_inc(ids_ready, 1)
            dve.wait_ge(ids_ready, 1)

            v.tensor_copy(bcm, d[:, 1:2].broadcast_to([P, P])).then_inc(bc_ready, 1)
            dve.wait_ge(bc_done, 1)
            v.tensor_copy(bcm, d[:, K:K + 1].broadcast_to([P, P])).then_inc(bc_ready, 1)
            dve.wait_ge(bc_done, 2)
            link(v.scalar_tensor_tensor(M[:], psC[:, 0:P], d[:, K:K + 1], M[:], ALU.is_equal, ALU.mult))
            link(v.scalar_tensor_tensor(MT[:], psC[:, P:2 * P], d[:, 1:2], MT[:], ALU.is_equal, ALU.mult))

            def fix(j, m):
                dve.wait_ge(carry_done, j + 1)
                link(v.tensor_copy(cr[:, 0:1], psC[:, 0:1]))
                link(v.scalar_tensor_tensor(s1[:], m[:], cr[:, 0:1], s1[:], ALU.mult, ALU.add))

            link(v.memset(s2[:], 1.0))
            v.tensor_tensor_scan(s1[:], mask_f[:, 0:K], s2[:], 0.0, ALU.mult, ALU.add).then_inc(scan_done, 1)
            dve.wait_ge(scan_done, 1)
            fix(0, m_first)
            link(v.tensor_copy(node_row[:, :, 1], s1[:]))
            link(v.tensor_scalar(n3d, s1[:], 1.0, None, ALU.max))

            dve.wait_ge(s_small, 16 * 18)
            link(v.reciprocal(rm2, lam_c))
            link(v.tensor_scalar(nre, rm2, -2.0, None, ALU.mult))
            link(v.tensor_scalar(rm1, rm2, 2.0, -1.0, ALU.mult, ALU.add))
            link(v.tensor_scalar(nre2, nre, 2.0, None, ALU.mult))
            link(v.tensor_scalar(rm2, rm1, 2.0, None, ALU.mult))

            r3v = r3[:].rearrange("p (k c) -> p k c", c=3)
            q3 = C[:, 0:3 * K].rearrange("p (k c) -> p k c", c=3)
            link(v.tensor_tensor(q3, r3v, r3v, ALU.mult))
            root(v.tensor_reduce(s2[:], q3, AX, ALU.add))
            link(v.reciprocal(s2[:], s2[:]))
            link(v.tensor_tensor(r3v, r3v, s2[:].unsqueeze(2).broadcast_to([P, K, 3]), ALU.mult))

            def take_carry(q):
                dve.wait_ge(carry_done, q + 1)
                link(v.tensor_copy(cr[:], psC[:, 0:F]))

            def segment_sums(q, msg, acc, res):
                v.tensor_tensor_scan(acc[:], mask_f[:, 0:KF], msg[:], 0.0, ALU.mult, ALU.add).then_inc(scan_done, 1)
                dve.wait_ge(scan_done, q + 1)
                take_carry(q)
                for f in range(F):
                    o = v.scalar_tensor_tensor(row(res)[:, :, f], m_first[:], cr[:, f:f + 1], fm(acc)[:, f, :],
                                               ALU.mult, ALU.add)
                return o

            def spread(q, msg, acc):
                v.tensor_tensor_scan(acc[:, ::-1], mask_f[:, 1:KF + 1][:, ::-1], msg[:, ::-1], 0.0,
                                     ALU.mult, ALU.add).then_inc(scan_done, 1)
                dve.wait_ge(scan_done, q + 1)
                take_carry(q)
                for f in range(F):
                    o = v.scalar_tensor_tensor(fm(acc)[:, f, :], m_last[:], cr[:, f:f + 1], fm(acc)[:, f, :],
                                               ALU.mult, ALU.add)
                link(o)

            def layernorm(X, Q):
                link(v.tensor_reduce(s1[:], row(X), AX, ALU.add))
                link(v.tensor_scalar(s1[:], s1[:], -1.0 / F, None, ALU.mult))
                link(v.tensor_tensor(row(X), row(X), over_f(s1[:]), ALU.add))
                link(v.tensor_tensor(row(Q), row(X), row(X), ALU.mult))
                link(v.tensor_reduce(s2[:], row(Q), AX, ALU.add))
                root(v.tensor_scalar(s2[:], s2[:], 1.0 / F, EPS, ALU.mult, ALU.add))
                link(v.reciprocal(s2[:], s2[:]))
                return v.tensor_tensor(row(X), row(X), over_f(s2[:]), ALU.mult)

            def gathered(r, c=GC - 1):
                for g in range(c + 1) if c == GC - 1 else [c]:
                    dve.wait_ge(got[g], r * (16 * KG) + 16 * KG)

            nd, ns = (t.rearrange("p (k c) -> p k c", c=3) for t in (node_d, node_s))
            dve.wait_ge(node_d_got, 16 * K)
            link(v.tensor_scalar(n2d, nd[:, :, 2], 1.0, None, ALU.add))
            v.tensor_copy(node_row[:, :, 2], nd[:, :, 2]).then_inc(node_row_ready, 1)
            dve.wait_ge(node_s_got, 16 * K)
            v.tensor_copy(ptr[:], ns[:, :, 0]).then_inc(ptr_ready, 1)
            link(v.tensor_scalar(live[:], ns[:, :, 0], float(EP), None, ALU.is_lt))
            link(v.tensor_scalar(n3s, ns[:, :, 1], 1.0, None, ALU.max))
            root(v.tensor_scalar(n2s, ns[:, :, 2], 1.0, None, ALU.add))
            link(v.reciprocal(norms[:], norms[:]))
            link(v.tensor_tensor(n3live[:], n3s, live[:], ALU.mult))
            link(v.tensor_tensor(cs1[:], n3live[:], n3live[:], ALU.mult))
            link(v.tensor_scalar(cs1[:], cs1[:], 0.9, None, ALU.mult))
            dve.wait_ge(node_stored, 16)
            dve.wait_ge(out_zeroed, 32)
            link(v.memset(G[:], 1.0))

            dve.wait_ge(xs_got, 16 * K)
            link(v.tensor_tensor(fm(A), row_t(XS), over_f_fm(n3live[:]), ALU.mult))
            link(v.tensor_scalar(C[:], A[:], 0.1, None, ALU.mult))
            base = steps[0]
            PASS = 1 + 2 * GC
            with dve.Fori(0, L0_ROUNDS - 1) as i:
                loop[0], loop[1] = i, PASS
                segment_sums(i + 1, A, B, A).then_inc(table_ready, 1)
                for c in range(GC):
                    gathered(i, c)
                    ks = slice(c * KG, (c + 1) * KG)
                    link(v.tensor_tensor(fm(A)[:, :, ks], row_t(G)[:, :, ks], over_f_fm(cs1[:, ks]), ALU.mult))
                    link(v.tensor_tensor(fm(A)[:, :, ks], fm(A)[:, :, ks], fm(C)[:, :, ks], ALU.add))
            assert steps[0] == base + PASS
            loop[0] = None
            steps[0] = base + PASS * (L0_ROUNDS - 1)
            R = L0_ROUNDS
            segment_sums(R, A, B, A).then_inc(table_ready, 1)
            dve.wait_ge(table_ready, R)
            dve.wait_ge(xd_got, 16 * K)
            link(v.tensor_tensor(s1[:], n3d, last[:], ALU.mult))
            link(v.tensor_scalar(s1[:], s1[:], 0.9, None, ALU.mult))
            link(v.tensor_tensor(fm(C), row_t(A), over_f_fm(s1[:]), ALU.mult))
            spread(R + 1, C, B)
            link(v.scalar_tensor_tensor(row_t(XD), row_t(XD), 1.1, fm(B), ALU.mult, ALU.add))
            link(layernorm(XD, C))
            gathered(R - 1)
            link(v.tensor_scalar(s1[:], n3live[:], 0.9, None, ALU.mult))
            link(v.tensor_tensor(row(C), row(G), over_f(s1[:]), ALU.mult))
            link(v.scalar_tensor_tensor(XS[:], XS[:], 1.1, C[:], ALU.mult, ALU.add))
            link(layernorm(XS, C))

            dve.wait_ge(ids_stored, 16)
            link(v.memset(U[:], 0.0))
            v.memset(w2_sb, 0.0).then_inc(w2_free, 1)
            PR = G[:, 0:T1 * 96 * 8].rearrange("p (t u w) -> p t u w", u=96, w=8)
            PF = G[:, 0:T1 * 96 * 8].rearrange("p (g u w) -> p g w u", u=16, w=8)
            P2 = G[:, 0:T1 * 64 * 8].rearrange("p (t u w) -> p t u w", u=64, w=8)
            P2F = G[:, 0:T1 * 64 * 8].rearrange("p (g u w) -> p g w u", u=8, w=8)
            base = steps[0]
            with dve.Fori(0, N1 // 2) as i:
                loop[0], loop[1] = i, 2 * L1_LINKS
                for u in range(2):
                    k0 = i * (2 * T1) + u * T1
                    W = (B, C)[u][:, 0:T1 * WC].rearrange("p (t w) -> p t w", w=WC)
                    Wm = W[:, :, 0:W1C].rearrange("p t (u w) -> p t u w", w=8)
                    Wn = W[:, :, W1C:WC].rearrange("p t (u w) -> p t u w", w=8)
                    xs = row(XS)[:, bass.ds(k0, T1), :]
                    xd = row(XD)[:, bass.ds(k0, T1), :]
                    rr = r3v[:, bass.ds(k0, T1), :]
                    for j, z in enumerate((xs, xd)):
                        v.tensor_copy(in48[:, :, 8 * j:8 * j + 8], z[:, :, 0:8])
                        v.tensor_copy(in48[:, :, 32 + 8 * j:40 + 8 * j], z[:, :, 0:8])
                        vr = G[:, 0:T1 * 24].rearrange("p (t v c) -> p t v c", v=8, c=3)
                        link(v.tensor_tensor(vr, z[:, :, 8:F].rearrange("p t (v c) -> p t v c", c=3),
                                             rr.unsqueeze(2).broadcast_to([P, T1, 8, 3]), ALU.mult))
                        link(v.tensor_reduce(in48[:, :, 16 + 8 * j:24 + 8 * j], vr, AX, ALU.add))
                    dve.wait_ge(wts_ready, i * (2 * T1) + ((u + 1) * T1 + 1))
                    v.tensor_tensor(PR[:, :, 0:48, :], Wm[:, :, 0:48, :],
                                    in48[:].unsqueeze(3).broadcast_to([P, T1, 48, 8]), ALU.mult)
                    for c in range(3):
                        for j, z in enumerate((xs, xd)):
                            vec = z[:, :, 8:F].rearrange("p t (v c) -> p t v c", c=3)[:, :, :, c]
                            o = v.tensor_tensor(PR[:, :, 48 + 16 * c + 8 * j:56 + 16 * c + 8 * j, :],
                                                Wm[:, :, 48 + 8 * j:56 + 8 * j, :],
                                                vec.unsqueeze(3).broadcast_to([P, T1, 8, 8]), ALU.mult)
                    link(o)
                    S6 = sums[:].rearrange("p t g w -> p (t g) w")[:, 0:T1 * 6, :]
                    link(v.tensor_reduce(S6, PF, AX, ALU.add))
                    S6 = S6.rearrange("p (t g) w -> p t g w", g=6)
                    for j in (0, 16, 32):
                        v.tensor_tensor(in48[:, :, j:j + 8], S6[:, :, 0, :], S6[:, :, 1, :], ALU.add)
                    for c in range(3):
                        o = v.tensor_tensor(vt[:, :, c, :], S6[:, :, 2, :],
                                            rr[:, :, c:c + 1].broadcast_to([P, T1, 8]), ALU.mult)
                    link(o)
                    link(v.scalar_tensor_tensor(vt[:], vt[:], S3, S6[:, :, 3:6, :], ALU.mult, ALU.add))
                    pv = G[:, 0:T1 * 24].rearrange("p (t c w) -> p t c w", c=3, w=8)
                    link(v.tensor_tensor(pv, vt[:], rr.unsqueeze(3).broadcast_to([P, T1, 3, 8]), ALU.mult))
                    for j in (8, 24):
                        o = v.tensor_reduce(in48[:, :, j:j + 8], pv.rearrange("p t c w -> p t w c"), AX, ALU.add)
                    link(o)
                    v.tensor_tensor(P2[:, :, 0:40, :], Wn[:, :, 0:40, :],
                                    in48[:, :, 0:40].unsqueeze(3).broadcast_to([P, T1, 40, 8]), ALU.mult)
                    for c in range(3):
                        o = v.tensor_tensor(P2[:, :, 40 + 8 * c:48 + 8 * c, :], Wn[:, :, 40:48, :],
                                            vt[:, :, c, :].unsqueeze(3).broadcast_to([P, T1, 8, 8]), ALU.mult)
                    o.then_inc(l1_used[u], 1)
                    dve.wait_ge(l1_used[u], i + 2)
                    link(v.tensor_reduce(sums[:].rearrange("p t g w -> p (t g) w"), P2F, AX, ALU.add))
                    a = row(A)[:, bass.ds(k0, T1), :]
                    v.tensor_tensor(a[:, :, 0:8], sums[:, :, 0, :], sums[:, :, 1, :], ALU.add)
                    v.tensor_tensor(gates[:, bass.ds(k0, T1), :], sums[:, :, 2, :], sums[:, :, 3, :], ALU.add)
                    for c in range(3):
                        o = v.tensor_tensor(vt[:, :, c, :], sums[:, :, 4, :],
                                            rr[:, :, c:c + 1].broadcast_to([P, T1, 8]), ALU.mult)
                    link(o)
                    link(v.scalar_tensor_tensor(vt[:], vt[:], S3, sums[:, :, 5:8, :], ALU.mult, ALU.add))
                    link(v.tensor_copy(a[:, :, 8:F].rearrange("p t (w c) -> p t c w", c=3), vt[:]))
            assert steps[0] == base + 2 * L1_LINKS, steps[0] - base
            loop[0] = None
            steps[0] = base + 2 * L1_LINKS * (N1 // 2)
            v.memset(U[:], 0.0).then_inc(wts_blank, 1)
            dve.wait_ge(l1_tanh, 1)
            av = row(A)[:, :, 8:F].rearrange("p k (w c) -> p k w c", c=3)
            link(v.tensor_tensor(av, av, gates[:].unsqueeze(3).broadcast_to([P, K, 8, 3]), ALU.mult))
            link(v.tensor_tensor(fm(B), row_t(A), over_f_fm(ewt[:]), ALU.mult))
            segment_sums(R + 2, B, C, A).then_inc(table_ready, 1)
            dve.wait_ge(table_ready, R + 1)
            link(v.tensor_tensor(fm(B), row_t(A), over_f_fm(last[:]), ALU.mult))
            spread(R + 3, B, C)
            link(v.tensor_tensor(row_t(XD), row_t(XD), fm(C), ALU.add))
            link(layernorm(XD, B))
            gathered(R)
            link(v.tensor_tensor(row(C), row(G), over_f(live[:]), ALU.mult))

            dve.wait_ge(ids_back, 16)
            link(v.tensor_scalar(s1[:], srcf, float(N), None, ALU.is_lt))
            link(v.tensor_tensor(s1[:], s1[:], n2d, ALU.mult))
            link(v.tensor_tensor(XS[:], XS[:], C[:], ALU.add))
            link(v.tensor_tensor(row(A), row(XD), over_f(s1[:]), ALU.mult))
            base = steps[0]
            bcq = B[:, 0:P]
            with dve.Fori(0, K) as k:
                loop[0], loop[1] = k, 0
                v.tensor_scalar(diag[:], ident[:], srcf[:, bass.ds(k, 1)], None, ALU.mult).then_inc(diag_ready, 1)
                dve.wait_ge(same_done, k + (K + 1))
                v.tensor_scalar(bcq, psC[:, 0:P], srcf[:, bass.ds(k, 1)], None, ALU.is_equal).then_inc(equal_ready, 1)
                dve.wait_ge(merged_mm, k + 1)
                v.tensor_copy(C[:, bass.ds(k * F, F)], psC[:, P:P + F]).then_inc(merged_ready, 1)
            loop[0] = None
            link(layernorm(XS, B))
            v.tensor_copy(cr[:, 0:1], c_bias[:, 0:1]).then_inc(dense_go, 1)
            Q = DQ.rearrange("p (r f) -> p r f", f=F)
            S = DS.rearrange("p (r f) -> p r f", f=F)
            z1, z4 = s1[0:NP, 0:RC], s1[0:NP, RC:2 * RC]
            z2, z3 = s2[0:NP, 0:RC], s3[0:NP, 0:RC]

            def wide(z):
                return z.unsqueeze(2).broadcast_to([NP, RC, F])

            for t in range(ND):
                X = DX[t % 2].rearrange("p (r f) -> p r f", f=F)
                deg = DN[t % 2].rearrange("p (r w) -> p r w", w=3)[:, :, 2]

                def centre():
                    link(v.tensor_reduce(z1, X, AX, ALU.add))
                    link(v.tensor_scalar(z1, z1, -1.0 / F, None, ALU.mult))
                    link(v.tensor_tensor(X, X, wide(z1), ALU.add))

                def squares():
                    link(v.tensor_tensor(Q, X, X, ALU.mult))
                    link(v.tensor_reduce(z2, Q, AX, ALU.add))

                dve.wait_ge(x_in[t % 2], 32 * (t // 2 + 1))
                centre()
                squares()
                link(v.tensor_scalar(z2, z2, 1.0 / F, None, ALU.mult))
                link(v.tensor_scalar(z1, z2, 1.21, EPS, ALU.mult, ALU.add))
                link(v.reciprocal(z1, z1))
                link(v.tensor_scalar(z1, z1, 1.21, None, ALU.mult))
                link(v.tensor_tensor(z2, z2, z1, ALU.mult))
                link(v.tensor_scalar(z3, z2, EPS, None, ALU.add))
                link(v.reciprocal(z3, z3))
                link(v.tensor_tensor(z1, z1, z3, ALU.mult))
                link(v.tensor_scalar(z4, deg, 1.0, None, ALU.add))
                link(v.reciprocal(z4, z4))
                root(v.tensor_scalar(z3, z4, 1.0, None, ALU.add))
                link(v.tensor_tensor(z1, z1, z3, ALU.mult))
                link(v.tensor_tensor(X, X, wide(z1), ALU.mult))
                dve.wait_ge(sums_in, 16 * (t + 1))
                link(v.tensor_tensor(S, S, wide(z4), ALU.mult))
                v.tensor_tensor(X, X, S, ALU.add).then_inc(sums_used, 1)
                dve.wait_ge(sums_used, t + 1)
                for layer in (2, 3):
                    centre()
                    squares()
                    root(v.tensor_scalar(z1, z2, 1.0 / F, EPS, ALU.mult, ALU.add))
                    link(v.reciprocal(z1, z1))
                    o = v.tensor_tensor(X, X, wide(z1), ALU.mult)
                    if layer == 2:
                        link(o)
                        link(v.tensor_tensor(X, X, c_bias[0:NP, :].unsqueeze(1).broadcast_to([NP, RC, F]), ALU.add))
                o.then_inc(dense_ready, 1)
                dve.wait_ge(dense_ready, t + 1)
            for u in range(2):
                dve.wait_ge(dense_stored[u], 16 * (ND // 2))
            for X, own, n, got_sm in ((XS, G, n2s, out_s_got), (XD, A, n2d, out_d_got)):
                link(v.tensor_tensor(row(C), row(X), over_f(n), ALU.mult))
                dve.wait_ge(got_sm, 16 * K)
                link(v.tensor_tensor(C[:], C[:], own[:], ALU.add))
                link(v.tensor_tensor(row(C), row(C), over_f(n), ALU.mult))
                link(v.tensor_tensor(X[:], X[:], C[:], ALU.add))
                if X is XS:
                    link(layernorm(X, C))
            layernorm(XD, C).then_inc(x3_ready, 1)
            dve.wait_ge(x3_ready, 1)

            dve.wait_ge(s_wts, 16 * 20)
            link(v.tensor_tensor(Wa, BD[0], BD[2], ALU.subtract))
            link(v.scalar_tensor_tensor(Wb, BD[2], rm2, BD[1], ALU.mult, ALU.add))
            link(v.tensor_scalar(Wc, BD[2], nre2, None, ALU.mult))
            for layer in range(2):
                r = R + 1 + 2 * layer
                q = R + 4 + 2 * layer
                n = 4 * layer
                link(v.tensor_tensor(fm(A), row_t(XS), over_f_fm(n3s), ALU.mult))
                segment_sums(q, A, B, A).then_inc(table_ready, 1)
                dve.wait_ge(table_ready, r + 1)
                link(v.tensor_tensor(row(B), row(A), over_f(n3d), ALU.mult))
                link(v.tensor_scalar(B[:], B[:], nre, None, ALU.mult))
                link(v.scalar_tensor_tensor(B[:], XD[:], rm1, B[:], ALU.mult, ALU.add))
                link(v.transpose(C[:], XD[:]))
                dve.wait_ge(table_stored, 16 * (r + 1))
                v.transpose(A[:], B[:]).then_inc(lin_in, 1)
                dve.wait_ge(lin_in, n + 1)
                gathered(r)
                link(v.tensor_tensor(row(B), row(G), over_f(n3live[:]), ALU.mult))
                link(v.tensor_scalar(B[:], B[:], nre, None, ALU.mult))
                link(v.scalar_tensor_tensor(B[:], XS[:], rm1, B[:], ALU.mult, ALU.add))
                dve.wait_ge(lin_out, LC * (n + 1))
                link(v.transpose(C[:], XS[:]))
                v.transpose(XS[:], B[:]).then_inc(lin_in, 1)
                link(v.tensor_tensor(fm(A), row_t(B), over_f_fm(n3s), ALU.mult))
                segment_sums(q + 1, A, B, A).then_inc(table_ready, 1)
                dve.wait_ge(table_ready, r + 2)
                link(v.tensor_tensor(row(B), row(A), over_f(n3d), ALU.mult))
                dve.wait_ge(lin_out, LC * (n + 2))
                v.transpose(C[:], B[:]).then_inc(lin_in, 1)
                dve.wait_ge(lin_out, LC * (n + 3))
                link(v.transpose(XD[:], B[:]))
                gathered(r + 1)
                link(v.tensor_tensor(row(A), row(G), over_f(n3live[:]), ALU.mult))
                v.transpose(C[:], A[:]).then_inc(lin_in, 1)
                dve.wait_ge(lin_out, LC * (n + 4))
                link(v.transpose(XS[:], B[:]))

            for n, X in ((8, XS), (9, XD)):
                v.transpose(C[:], X[:]).then_inc(lin_in, 1)
                dve.wait_ge(lin_out, LC * (n + 1))
                link(v.transpose(X[:], B[:]))
            q = R + 8
            link(v.tensor_tensor(fm(A), row_t(XD), over_f_fm(last[:]), ALU.mult))
            spread(q, A, B)
            link(v.tensor_tensor(row_t(XD), row_t(XS), fm(B), ALU.add))
            link(v.scalar_tensor_tensor(XD[:], XD[:], 0.2, XD[:], ALU.mult, ALU.max))
            v.tensor_tensor(row(A), row(XD), c_attn[:].unsqueeze(1).broadcast_to([P, K, F]), ALU.mult).then_inc(xd_free, 1)
            dve.wait_ge(xd_free, 1)
            link(v.tensor_reduce(s3[:], row(A), AX, ALU.add))
            msk = mask_f[:, 0:K]
            link(v.tensor_scalar(s1[:], msk, BIG, -BIG, ALU.mult, ALU.add))
            link(v.tensor_tensor_scan(s2[:], s1[:], s3[:], -BIG, ALU.add, ALU.max))
            v.tensor_copy(A[:, 0:P], s2[:, K - 1:K].broadcast_to([P, P])).then_inc(scan_done, 1)
            link(v.tensor_scalar(A[:, P:2 * P], MT[:], BIG, -BIG, ALU.mult, ALU.add))
            dve.wait_ge(carry_done, q + 2)
            link(v.tensor_tensor(A[:, P:2 * P], A[:, P:2 * P], psC[:, 0:P], ALU.add))
            link(v.tensor_reduce(cr[:, 0:1], A[:, P:2 * P], AX, ALU.max))
            link(v.tensor_scalar(s1[:], m_first[:], BIG, -BIG, ALU.mult, ALU.add))
            link(v.scalar_tensor_tensor(s1[:], m_first[:], cr[:, 0:1], s1[:], ALU.mult, ALU.add))
            link(v.tensor_tensor(s2[:], s2[:], s1[:], ALU.max))
            link(v.tensor_tensor(s2[:], s2[:], last[:], ALU.mult))
            v.tensor_tensor_scan(s1[:, ::-1], mask_f[:, 1:K + 1][:, ::-1], s2[:, ::-1], 0.0,
                                 ALU.mult, ALU.add).then_inc(scan_done, 1)
            dve.wait_ge(scan_done, q + 3)

            fix(q + 2, m_last)
            v.tensor_tensor(s2[:], s3[:], s1[:], ALU.subtract).then_inc(ex_in, 1)
            dve.wait_ge(ex_out, 1)
            v.tensor_tensor_scan(s1[:], msk, s2[:], 0.0, ALU.mult, ALU.add).then_inc(scan_done, 1)
            dve.wait_ge(scan_done, q + 4)
            fix(q + 3, m_first)
            link(v.tensor_scalar(s1[:], s1[:], 1e-6, None, ALU.max))
            link(v.reciprocal(s3[:], s1[:]))
            link(v.tensor_tensor(fm(A), row_t(XS), over_f_fm(s2[:]), ALU.mult))
            link(segment_sums(q + 4, A, B, A))
            link(v.tensor_tensor(row(A), row(A), over_f(s3[:]), ALU.mult))
            link(v.tensor_tensor(row(A), row(A), c_bias[:].unsqueeze(1).broadcast_to([P, K, F]), ALU.add))
            dve.wait_ge(x3_back, 16)
            link(v.tensor_tensor(A[:], A[:], XD[:], ALU.add))
            layernorm(A, C).then_inc(res_ready, 1)


def kernel(x, src, dst, edge_attr_10, edge_attr_3, edge_weight, L1_gnn_fc1_w1, L1_gnn_fc1_w2, L1_gnn_fc2_w1,
           L1_gnn_fc2_w2, L3_gnn_laplacian_lambda_max, L3_gnn_cheb_W, L3_gnn_cheb_b, L3_gnn_gat_Wsrc,
           L3_gnn_gat_bsrc, L3_gnn_gat_Wdst, L3_gnn_gat_bdst, L3_gnn_gat_attn, L3_gnn_gat_bias):
    import numpy as np
    import concourse.bacc as bacc
    from concourse.bass_utils import run_bass_kernel_spmd

    P, E = 128, src.shape[0]
    K = -(-E // P)
    pad = P * K - E

    def padded(a, value):
        a = np.asarray(a)
        return np.concatenate([a, np.full((pad,) + a.shape[1:], value, a.dtype)])

    def tiles(a, value):
        return np.ascontiguousarray(padded(a, value).reshape(P, -1))

    d = np.concatenate([np.full(1, -1, np.int32), padded(dst, 200000), np.full(1, -2, np.int32)])
    dst_ext = np.stack([d[p * K:p * K + K + 2] for p in range(P)])
    ea10 = padded(edge_attr_10, 0).reshape(P, K, -1)
    arrays = {
        "x": np.asarray(x),
        "dst_ext": dst_ext,
        "src_idx": tiles(src, 200000),
        "ea10_t": np.ascontiguousarray(ea10.transpose(2, 1, 0).reshape(ea10.shape[2], K * P)),
        "ea3": tiles(edge_attr_3, 1),
        "ew": tiles(edge_weight, 0),
        "w1cat": np.concatenate([np.asarray(L1_gnn_fc1_w1), np.asarray(L1_gnn_fc2_w1)], axis=1),
        "fc1_w2": np.asarray(L1_gnn_fc1_w2),
        "fc2_w2": np.asarray(L1_gnn_fc2_w2),
        "lam": np.asarray(L3_gnn_laplacian_lambda_max),
        "cheb_wt": np.ascontiguousarray(np.asarray(L3_gnn_cheb_W).T),
        "cheb_b": np.asarray(L3_gnn_cheb_b),
        "wsrc_t": np.ascontiguousarray(np.asarray(L3_gnn_gat_Wsrc).T),
        "bsrc": np.asarray(L3_gnn_gat_bsrc),
        "wdst_t": np.ascontiguousarray(np.asarray(L3_gnn_gat_Wdst).T),
        "bdst": np.asarray(L3_gnn_gat_bdst),
        "attn": np.asarray(L3_gnn_gat_attn).reshape(-1),
        "gat_bias": np.asarray(L3_gnn_gat_bias),
    }
    nc = bacc.Bacc("TRN2", target_bir_lowering=False, num_devices=1)
    aps = [nc.dram_tensor(f"in_{n}", a.shape, mybir.dt.from_np(a.dtype), kind="ExternalInput").ap()
           for n, a in arrays.items()]
    out = nc.dram_tensor("out_rows", x.shape, mybir.dt.float32, kind="ExternalOutput").ap()
    gnn_resnorm_kernel(nc, *aps, out)
    r = run_bass_kernel_spmd(nc, [{f"in_{n}": a for n, a in arrays.items()}], core_ids=[0])
    return r.results[0]["out_rows"]
```

```python
import concourse.bass as bass
from concourse import mybir
from contextlib import ExitStack


def gnn_resnorm_kernel(nc, x, dst_ext, src_idx, ea10_t, ea3, ew, w1cat, fc1_w2, fc2_w2, lam,
                       cheb_wt, cheb_b, wsrc_t, bsrc, wdst_t, bdst, attn, gat_bias, out):
    fp32, i32, u8 = mybir.dt.float32, mybir.dt.int32, mybir.dt.uint8
    ALU = mybir.AluOpType
    ACT = mybir.ActivationFunctionType
    AX = mybir.AxisListType.X

    N, F = x.shape
    P = 128
    K = src_idx.shape[1]
    EP = P * K
    KF = K * F
    NONE = 200000
    EPS = 1e-5
    BIG = 1e30
    NP, NR = 125, N // 125
    ND = 10
    SPANS = ((0, 4), (4, 6), (6, 8), (8, 10))
    RC = NR // ND
    GC = 7
    KG = K // GC
    T1 = 7
    N1 = K // T1
    LC = 14
    LW = KF // LC
    H = w1cat.shape[1]
    HIN = w1cat.shape[0]
    W1C, W2C = fc1_w2.shape[1], fc2_w2.shape[1]
    WC = W1C + W2C
    S3 = 3.0 ** 0.5
    L0_ROUNDS = 10
    KC = 64
    FEW_MAX = KC
    XS_FIRST = 56
    XS_FILL = -(-(K - XS_FIRST) // (L0_ROUNDS - 1))
    EC = P * KC
    KCF = KC * F
    PACK = 32768
    L1_LINKS = 14

    node_tab = nc.dram_tensor("node_tab", [N, 2], fp32).ap()
    deg_tab = nc.dram_tensor("deg_tab", [N, 1], fp32).ap()
    out_tab = nc.dram_tensor("out_tab", [N + P, F], fp32).ap()
    few_tab = nc.dram_tensor("few_tab", [EC, F], fp32).ap()
    few_pos = nc.dram_tensor("few_pos", [EP, 1], fp32).ap()
    ids_tab = nc.dram_tensor("ids_tab", [P, 4 * K], fp32).ap()
    agg_tab = nc.dram_tensor("agg_tab", [EP, F], fp32).ap()
    x3_tab = nc.dram_tensor("x3_tab", [P, KF], fp32).ap()

    ctx = ExitStack()
    with ctx:
        def sb(name, shape, dt=fp32):
            return ctx.enter_context(nc.sbuf_tensor(name, shape, dt))

        def sem(name):
            return ctx.enter_context(nc.semaphore(name))

        gates = sb("gates", [P, K, 8])
        XS, XD, G, A, B, C = (sb(n, [P, KF]) for n in ("XS", "XD", "G", "A", "B", "C"))
        mask_f = sb("mask_f", [P, KF + 4], u8)
        U = sb("U", [P, 3 * T1 * P])
        r3 = sb("r3", [P, K * 3])
        last = sb("last", [P, K])
        m_first = sb("m_first", [P, K])
        m_last = sb("m_last", [P, K])
        ewt = sb("ewt", [P, K])
        live = sb("live", [P, K])
        norms = sb("norms", [P, 4, K])
        n3s, n3d, n2s, n2d = (norms[:, i, :] for i in range(4))
        n3live = sb("n3live", [P, K])
        cs1 = sb("cs1", [P, K])
        idx_last = sb("idx_last", [P, K], i32)
        ptr = sb("ptr", [P, K], i32)
        s1, s2, s3 = (sb(n, [P, K]) for n in ("s1", "s2", "s3"))
        ident = sb("ident", [P, P])
        M = sb("M", [P, P])
        MT = sb("MT", [P, P])
        cr = sb("cr", [P, F])
        flag = sb("flag", [1, 1], i32)
        tick = sb("tick", [P, 8])
        c_bias = sb("c_bias", [P, F])
        c_attn = sb("c_attn", [P, F])
        cols = sb("cols", [P, 8])
        cb, bs_c, bd_c, lam_c, nre, rm1, rm2, nre2 = (cols[:, i:i + 1] for i in range(8))

        dst_i = U[:, 0:K + 2].bitcast(i32)
        src_i = U[:, 200:200 + K].bitcast(i32)
        node_row = U[:, 400:400 + 2 * K].rearrange("p (k c) -> p k c", c=2)
        ids = U[:, 1024:1024 + 4 * K]
        src_g, dst_g, add_to = (U[:, 1024 + K * i:1024 + K * (i + 1)].bitcast(i32) for i in range(3))
        srcf = U[:, 1024 + 3 * K:1024 + 4 * K]
        d = U[:, 2004:2004 + K + 2]
        seg_last = U[:, 2360:2360 + K]
        spare = U[:, 2210:2211]
        bcm = U[:, 2220:2220 + P]
        RN = NR
        fp16, bf16 = mybir.dt.float16, mybir.dt.bfloat16
        iota_c = G[:, 0:400].bitcast(fp16)
        iota_p = G[:, 400:464].bitcast(fp16)
        hot_c = [G[:, 464 + 400 * u:864 + 400 * u].bitcast(bf16) for u in range(2)]
        hot_p = [G[:, 1264 + 64 * u:1328 + 64 * u].bitcast(bf16) for u in range(2)]
        stage = G[0:NP, 1392:1392 + RN]
        iota_i = G[:, 1392:1392 + RN].bitcast(i32)
        iota_q = G[:, 2192:2192 + P].bitcast(i32)
        zeros = G[:, 3792:3792 + 1024]
        node_s = G[:, 5532:5532 + 2 * K]
        blank = A[0:NP, 0:2 * RN].rearrange("p (c w) -> p c w", w=2)
        few_w, few_acc, few_row = (B[:, KCF * i:KCF * (i + 1)] for i in range(3))
        few_g, few_c0 = (C[:, KCF * i:KCF * (i + 1)] for i in range(2))
        few_mask = C[:, 2 * KCF:2 * KCF + KCF // 4].bitcast(u8)
        gt = gates[:].rearrange("p k w -> p (k w)")
        MF = gt[:, 0:P]
        (f_key, f_int, f_ptr, f_edge, f_dst, f_seg, f_deg, f_live, f_same, f_place, f_pos, f_m1, f_cs1, f_end,
         f_tmp, f_next, f_src, f_low) = (gt[:, P + KC * i:P + KC * (i + 1)] for i in range(18))
        f_one = gt[:, P + 18 * KC:P + 18 * KC + 8]
        diag = sb("diag", [P, P])
        ones = sb("ones", [P, P])
        ea = [U[0:HIN, T1 * P * u:T1 * P * (u + 1)] for u in range(2)]
        hid = U[0:H, 2 * T1 * P:3 * T1 * P]
        BD = [U[:, P * i:P * (i + 1)] for i in range(5)]
        Wa, Wb, Wc = (U[:, P * i:P * (i + 1)] for i in range(5, 8))
        w1_sb = sb("w1_sb", [HIN, 2 * H])
        in48 = sb("in48", [P, T1, 48])
        vt = sb("vt", [P, T1, 3, 8])
        sums = sb("sums", [P, T1, 8, 8])
        w2_sb = G[0:H, KF - WC:KF]

        psW = ctx.enter_context(nc.psum_tensor("psW", [P, 2, 1024], fp32))
        psH = ctx.enter_context(nc.psum_tensor("psH", [P, 1024], fp32))
        psC = ctx.enter_context(nc.psum_tensor("psC", [P, 512], fp32))

        def row(t):
            return t[:, 0:KF].rearrange("p (k f) -> p k f", f=F)

        def row_t(t):
            return t[:, 0:KF].rearrange("p (k f) -> p f k", f=F)

        def fm(t):
            return t[:, 0:KF].rearrange("p (f k) -> p f k", k=K)

        def over_f(s):
            return s.unsqueeze(2).broadcast_to([P, s.shape[1], F])

        def over_f_fm(s):
            return s.unsqueeze(1).broadcast_to([P, F, s.shape[1]])

        s_idx = sem("s_idx")
        s_small = sem("s_small")
        s_wts = sem("s_wts")
        s_w2 = sem("s_w2")
        iota_done = sem("iota_done")
        dst_g_ready = sem("dst_g_ready")
        idx_last_ready = sem("idx_last_ready")
        bc_ready = sem("bc_ready")
        bc_done = sem("bc_done")
        c_iota = sem("c_iota")
        hots_ready = sem("hots_ready")
        hist_mm = sem("hist_mm")
        stage_ready = sem("stage_ready")
        zeros_ready = sem("zeros_ready")
        node_stored = sem("node_stored")
        out_zeroed = sem("out_zeroed")
        blank_ready = sem("blank_ready")
        deg_stored = sem("deg_stored")
        deg_idx_ready = sem("deg_idx_ready")
        deg_got = sem("deg_got")
        node_row_ready = sem("node_row_ready")
        node_scattered = sem("node_scattered")
        diag_ready = sem("diag_ready")
        same_done = sem("same_done")
        ids_ready = sem("ids_ready")
        ids_stored = sem("ids_stored")
        ids_back = sem("ids_back")
        equal_ready = sem("equal_ready")
        merged_mm = sem("merged_mm")
        merged_ready = sem("merged_ready")
        added = sem("added")
        out_s_got = [sem(f"out_s_got{i}") for i in range(GC)]
        out_d_got = sem("out_d_got")
        dense_go = sem("dense_go")
        sums_in = sem("sums_in")
        sums_used = sem("sums_used")
        ptr_ready = sem("ptr_ready")
        hist_done = sem("hist_done")
        xd_got = sem("xd_got")
        xs_got = sem("xs_got")
        node_s_got = sem("node_s_got")
        x_in = [sem(f"x_in{i}") for i in range(2)]
        dense_ready = sem("dense_ready")
        dense_stored = [sem(f"dense_stored{i}") for i in range(2)]
        dve_step = sem("dve_step")
        var_ready = sem("var_ready")
        std_ready = sem("std_ready")
        scan_done = sem("scan_done")
        carry_done = sem("carry_done")
        table_ready = sem("table_ready")
        table_stored = sem("table_stored")
        got = [sem(f"got{i}") for i in range(GC)]
        ticked = sem("ticked")
        few_zeroed = sem("few_zeroed")
        mode_ready = sem("mode_ready")
        count_ready = sem("count_ready")
        count_done = sem("count_done")
        g_step = sem("g_step")
        f_step = sem("f_step")
        g_scan = sem("g_scan")
        g_carry = sem("g_carry")
        g_table = sem("g_table")
        g_stored = sem("g_stored")
        f_seg_ready = sem("f_seg_ready")
        f_seg_put = sem("f_seg_put")
        f_pos_got = sem("f_pos_got")
        f_pos_ready = sem("f_pos_ready")
        f_first_ready = sem("f_first_ready")
        f_first_done = sem("f_first_done")
        f_x_got = sem("f_x_got")
        f_scan = sem("f_scan")
        f_carry = sem("f_carry")
        f_table = sem("f_table")
        f_stored = sem("f_stored")
        f_exit = sem("f_exit")
        f_put = sem("f_put")
        f_back = sem("f_back")
        c_far = sem("c_far")
        g_got = [sem(f"g_got{i}") for i in range(GC)]
        f_got = [sem(f"f_got{i}") for i in range(2)]
        w1_blank = sem("w1_blank")
        w2_free = sem("w2_free")
        ea_in = [sem(f"ea_in{i}") for i in range(2)]
        hid_mm = sem("hid_mm")
        hid_ready = sem("hid_ready")
        wts_mm = sem("wts_mm")
        wts_ready = sem("wts_ready")
        l1_used = [sem(f"l1_used{i}") for i in range(2)]
        l1_tanh = sem("l1_tanh")
        wts_blank = sem("wts_blank")
        x3_ready = sem("x3_ready")
        x3_spilled = sem("x3_spilled")
        xd_free = sem("xd_free")
        x3_back = sem("x3_back")
        lin_in = sem("lin_in")
        lin_part = sem("lin_part")
        lin_mm = sem("lin_mm")
        lin_out = sem("lin_out")
        ex_in = sem("ex_in")
        ex_out = sem("ex_out")
        res_ready = sem("res_ready")
        res_stored = sem("res_stored")

        x_v = x.rearrange("(p c r) f -> p c (r f)", p=NP, c=ND)
        out_v = out.rearrange("(p c r) f -> p c (r f)", p=NP, c=ND)
        agg_v = agg_tab.rearrange("(p k) f -> p (k f)", p=P)
        sum_v = out_tab[0:N, :].rearrange("(p c r) f -> p c (r f)", p=NP, c=ND)
        node_v = deg_tab.rearrange("(p c r) w -> p c (r w)", p=NP, c=ND)
        DX = [B[0:NP, u * RC * F:(u + 1) * RC * F] for u in range(2)]
        DN = [B[0:NP, 2 * RC * F + u * RC:2 * RC * F + (u + 1) * RC] for u in range(2)]
        DS = A[0:NP, 0:RC * F]
        DQ = A[0:NP, RC * F:2 * RC * F]

        block = ctx.enter_context(nc.Block())

        @block.sync
        def _(sp):
            sp.dma_start(dst_i, dst_ext).then_inc(s_idx, 16)
            sp.dma_start(src_i, src_idx).then_inc(s_idx, 16)
            sp.dma_start(c_bias[:], gat_bias.unsqueeze(0).broadcast_to([P, F])).then_inc(s_small, 16)
            sp.dma_start(c_attn[:], attn.unsqueeze(0).broadcast_to([P, F])).then_inc(s_small, 16)
            sp.dma_start(lam_c, lam.unsqueeze(0).broadcast_to([P, 1])).then_inc(s_small, 16)
            for i in range(4):
                for c, v in ((cb, cheb_b), (bs_c, bsrc), (bd_c, bdst)):
                    sp.dma_start(c[F * i:F * (i + 1), :], v.unsqueeze(1)).then_inc(s_small, 16)
            sp.wait_ge(w1_blank, 1)
            sp.dma_start(w1_sb[:, 0:H], w1cat).then_inc(s_small, 16)
            sp.dma_start(ewt[:], ew).then_inc(s_small, 16)
            sp.dma_start(r3[:], ea3).then_inc(s_small, 16)
            sp.wait_ge(blank_ready, 2)
            sp.dma_start(node_tab.rearrange("(p c) w -> p (c w)", p=NP),
                         blank.rearrange("p c w -> p (c w)")).then_inc(node_stored, 16)
            sp.wait_ge(zeros_ready, 1)
            sp.dma_start(out_tab[0:N, :].rearrange("(p a r) f -> p a (r f)", p=NP, a=25),
                         zeros[0:NP, :].unsqueeze(1).broadcast_to([NP, 25, 1024])).then_inc(out_zeroed, 16)
            sp.dma_start(out_tab[N:N + P, :], zeros[:, 0:F]).then_inc(out_zeroed, 16)
            sp.dma_start(few_pos.rearrange("(p k) o -> p (k o)", p=P), zeros[:, 0:K]).then_inc(few_zeroed, 16)
            sp.dma_start(agg_tab.rearrange("(p a r) f -> p a (r f)", p=P, a=7),
                         zeros[:, 0:KF // 7].unsqueeze(1).broadcast_to([P, 7, KF // 7])).then_inc(few_zeroed, 16)
            sp.wait_ge(stage_ready, 1)
            sp.dma_start(deg_tab.rearrange("(p c) w -> p (c w)", p=NP), stage).then_inc(deg_stored, 16)
            def store_table(r):
                sp.wait_ge(table_ready, r + 1)
                sp.dma_start(agg_v, A[:]).then_inc(table_stored, 16)

            sp.wait_ge(ids_ready, 1)
            sp.dma_start(ids_tab, ids).then_inc(ids_stored, 16)
            sp.wait_ge(mode_ready, 1)
            few = sp.value_load(flag[0:1, 0:1], min_val=0, max_val=1)
            with sp.If(few > 0):
                with sp.Fori(0, L0_ROUNDS - 1) as i:
                    sp.wait_ge(f_table, i + 1)
                    sp.dma_start(few_tab.rearrange("(p k) f -> p (k f)", p=P), few_row).then_inc(f_stored, 16)
                sp.wait_ge(f_put, 16 * KC)
                sp.dma_start(A[:], agg_v).then_inc(f_back, 16)
            with sp.Else():
                with sp.Fori(0, L0_ROUNDS - 1) as i:
                    sp.wait_ge(g_table, i + 1)
                    sp.dma_start(agg_v, A[:]).then_inc(g_stored, 16)
                store_table(0)
            sp.wait_ge(w2_free, 1)
            sp.dma_start(w2_sb[0:H // 2, 0:W1C], fc1_w2).then_inc(s_w2, 16)
            sp.dma_start(w2_sb[H // 2:H, W1C:WC], fc2_w2).then_inc(s_w2, 16)
            for u in range(2):
                sp.dma_start(ea[u], ea10_t[:, u * T1 * P:(u + 1) * T1 * P]).then_inc(ea_in[u], 16)
            with sp.Fori(0, N1 // 2 - 1) as i:
                for u in range(2):
                    sp.wait_ge(hid_mm, i * 2 + u + 1)
                    sp.dma_start(ea[u], ea10_t[:, bass.ds((i * 2 + 2 + u) * (T1 * P), T1 * P)]).then_inc(ea_in[u], 16)
            store_table(1)
            sp.wait_ge(wts_blank, 1)
            for q in range(4):
                sl = slice(F * q, F * (q + 1))
                for i in range(3):
                    sp.dma_start(BD[i][sl, sl], cheb_wt[F * i:F * (i + 1), :]).then_inc(s_wts, 16)
                sp.dma_start(BD[3][sl, sl], wsrc_t).then_inc(s_wts, 16)
                sp.dma_start(BD[4][sl, sl], wdst_t).then_inc(s_wts, 16)
            sp.wait_ge(ids_stored, 16)
            sp.dma_start(ids, ids_tab).then_inc(ids_back, 16)

            def load_dense(t):
                u = t % 2
                sp.dma_start(DX[u], x_v[:, t, :]).then_inc(x_in[u], 16)
                sp.dma_start(DN[u], node_v[:, t, :]).then_inc(x_in[u], 16)

            def dense_span(w):
                sp.wait_ge(dense_go, w + 1)
                t0, t1 = SPANS[w]
                for t in range(t0, min(t0 + 2, t1)):
                    load_dense(t)
                for t in range(t0, t1):
                    if t > t0:
                        sp.wait_ge(sums_used, t)
                    sp.dma_start(DS, sum_v[:, t, :]).then_inc(sums_in, 16)
                    if t > t0:
                        sp.wait_ge(dense_ready, t)
                        sp.dma_start(out_v[:, t - 1, :], DX[(t - 1) % 2]).then_inc(dense_stored[(t - 1) % 2], 16)
                        if t + 1 < t1:
                            sp.wait_ge(dense_stored[(t - 1) % 2], 16 * ((t - 1) // 2 + 1))
                            load_dense(t + 1)
                sp.wait_ge(dense_ready, t1)
                sp.dma_start(out_v[:, t1 - 1, :], DX[(t1 - 1) % 2]).then_inc(dense_stored[(t1 - 1) % 2], 16)

            sp.wait_ge(added, 16 * K)
            dense_span(0)
            sp.wait_ge(x3_ready, 1)
            sp.dma_start(x3_tab, XD[:]).then_inc(x3_spilled, 16)
            for r in range(4):
                store_table(2 + r)
                if 1 + r < len(SPANS):
                    dense_span(1 + r)
            sp.wait_ge(xd_free, 1)
            sp.dma_start(XD[:], x3_tab).then_inc(x3_back, 16)
            sp.wait_ge(res_stored, 16 * K)
            for u in range(2):
                sp.wait_ge(dense_stored[u], 16 * (ND // 2))

        @block.gpsimd
        def _(pool):
            for j, (sm, n) in enumerate(((hist_mm, 2), (hid_ready, 1), (wts_ready, 1), (l1_used[0], 1),
                                         (l1_used[1], 1), (ticked, 1))):
                nc.gpsimd.memset(tick[:, j:j + 1], 0.0).then_inc(sm, n)
            nc.gpsimd.memset(blank[:, :, 0], float(NONE)).then_inc(blank_ready, 1)
            nc.gpsimd.memset(blank[:, :, 1], 0.0).then_inc(blank_ready, 1)
            nc.gpsimd.memset(ident[:], 1.0).then_inc(iota_done, 1)
            nc.gpsimd.iota(iota_i, [[1, RN]], base=0, channel_multiplier=0).then_inc(c_iota, 1)
            nc.gpsimd.iota(iota_q, [[1, P]], base=0, channel_multiplier=0).then_inc(c_iota, 1)
            nc.gpsimd.iota(node_row[:, :, 0].bitcast(i32), [[1, K]], base=0, channel_multiplier=K).then_inc(c_iota, 1)
            nc.gpsimd.iota(f_place.bitcast(i32), [[1, KC]], base=1, channel_multiplier=KC).then_inc(c_iota, 1)
            nc.gpsimd.memset(MF, 1.0).then_inc(c_far, 1)
            nc.gpsimd.iota(spare.bitcast(i32), [[1, 1]], base=N, channel_multiplier=1).then_inc(c_iota, 1)
            nc.gpsimd.memset(zeros, 0.0).then_inc(zeros_ready, 1)
            nc.gpsimd.memset(ones[:], 1.0).then_inc(iota_done, 1)
            nc.gpsimd.memset(M[:], 1.0).then_inc(iota_done, 1)
            nc.gpsimd.memset(MT[:], 1.0).then_inc(iota_done, 1)
            pool.wait_ge(iota_done, 4)
            nc.gpsimd.affine_select(ident[:], ident[:], [[-1, P]], ALU.is_equal, 0.0, base=0,
                                    channel_multiplier=1).then_inc(iota_done, 1)
            nc.gpsimd.affine_select(M[:], M[:], [[1, P]], ALU.is_gt, 0.0, base=0,
                                    channel_multiplier=-1).then_inc(iota_done, 1)
            pool.wait_ge(c_far, 1)
            nc.gpsimd.affine_select(MF, MF, [[1, P]], ALU.is_gt, 0.0, base=0, channel_multiplier=-1).then_inc(c_far, 1)
            nc.gpsimd.affine_select(MT[:], MT[:], [[-1, P]], ALU.is_gt, 0.0, base=0,
                                    channel_multiplier=1).then_inc(iota_done, 1)

            def gather(dst, table, idx, bound, k, w=F):
                return nc.gpsimd.indirect_dma_start(dst[:, k * w:(k + 1) * w], None, table,
                                                    bass.IndirectOffsetOnAxis(idx[:, k:k + 1], 0),
                                                    bounds_check=bound, oob_is_err=False)

            def scatter(table, src, idx, k, w=F):
                return nc.gpsimd.indirect_dma_start(table, bass.IndirectOffsetOnAxis(idx[:, k:k + 1], 0),
                                                    src[:, k * w:(k + 1) * w], None, bounds_check=N - 1,
                                                    oob_is_err=False)

            pool.wait_ge(node_stored, 16)
            pool.wait_ge(node_row_ready, 1)
            for k in range(K):
                scatter(node_tab, U[:, 400:400 + 2 * K], idx_last, k, 2).then_inc(node_scattered, 16)
            pool.wait_ge(node_scattered, 16 * K)
            pool.wait_ge(dst_g_ready, 2)
            for k in range(K):
                gather(node_s, node_tab, src_g, N - 1, k, 2).then_inc(node_s_got, 16)
            for k in range(K):
                gather(XD, x, dst_g, N - 1, k).then_inc(xd_got, 16)
            for k in range(XS_FIRST):
                gather(XS, x, src_g, N - 1, k).then_inc(xs_got, 16)
            pool.wait_ge(ptr_ready, 1)

            def gather_round(r, ticks):
                pool.wait_ge(ticked, r + ticks)
                pool.wait_ge(table_stored, r * 16 + 16)
                nc.gpsimd.tensor_tensor(tick[:, 5:6], ident[:, 0:1], ident[:, 0:1], ALU.add).then_inc(ticked, 1)
                for k in range(K):
                    gather(G, agg_tab, ptr, EP - 1, k).then_inc(got[k // KG], 16)

            pool.wait_ge(mode_ready, 1)
            few = pool.value_load(flag[0:1, 0:1], min_val=0, max_val=1)
            with pool.If(few > 0):
                pool.wait_ge(few_zeroed, 32)
                pool.wait_ge(f_seg_ready, 1)
                for r in range(KC):
                    nc.gpsimd.indirect_dma_start(few_pos, bass.IndirectOffsetOnAxis(f_seg.bitcast(i32)[:, r:r + 1], 0),
                                                 f_place[:, r:r + 1], None, bounds_check=EP - 1,
                                                 oob_is_err=False).then_inc(f_seg_put, 16)
                for r in range(KC):
                    gather(few_g, x, f_src.bitcast(i32), N - 1, r).then_inc(f_x_got, 16)
                pool.wait_ge(f_seg_put, 16 * KC)
                for r in range(KC):
                    gather(f_pos, few_pos, f_ptr.bitcast(i32), EP - 1, r, 1).then_inc(f_pos_got, 16)
                pool.wait_ge(f_pos_ready, 1)
                for i in range(L0_ROUNDS - 1):
                    pool.wait_ge(f_stored, i * 16 + 16)
                    for r in range(KC):
                        gather(few_g, few_tab, f_pos.bitcast(i32), EC - 1, r).then_inc(f_got[2 * r // KC], 16)
                    for k in range(XS_FIRST + XS_FILL * i, min(K, XS_FIRST + XS_FILL * (i + 1))):
                        gather(XS, x, src_g, N - 1, k).then_inc(xs_got, 16)
                pool.wait_ge(ticked, 1)
                nc.gpsimd.memset(tick[:, 5:6], 0.0).then_inc(ticked, L0_ROUNDS - 1)
                pool.wait_ge(f_exit, 1)
                for r in range(KC):
                    nc.gpsimd.indirect_dma_start(agg_tab, bass.IndirectOffsetOnAxis(f_seg.bitcast(i32)[:, r:r + 1], 0),
                                                 few_row[:, r * F:(r + 1) * F], None, bounds_check=EP - 1,
                                                 oob_is_err=False).then_inc(f_put, 16)
                pool.wait_ge(f_put, 16 * KC)
                nc.gpsimd.memset(tick[:, 6:7], 0.0).then_inc(table_stored, 16)
            with pool.Else():
                for k in range(XS_FIRST, K):
                    gather(XS, x, src_g, N - 1, k).then_inc(xs_got, 16)
                with pool.Fori(0, L0_ROUNDS - 1) as i:
                    pool.wait_ge(ticked, i + 1)
                    pool.wait_ge(g_stored, i * 16 + 16)
                    nc.gpsimd.tensor_tensor(tick[:, 5:6], ident[:, 0:1], ident[:, 0:1], ALU.add).then_inc(ticked, 1)
                    for k in range(K):
                        gather(G, agg_tab, ptr, EP - 1, k).then_inc(g_got[k // KG], 16)
            gather_round(0, L0_ROUNDS)
            pool.wait_ge(deg_stored, 16)
            pool.wait_ge(deg_idx_ready, 2)
            for n2, idx in ((n2d, s1), (n2s, s2)):
                for k in range(K):
                    gather(n2, deg_tab, idx[:].bitcast(i32), N - 1, k, 1).then_inc(deg_got, 16)
            pool.wait_ge(table_stored, 32)
            pool.wait_ge(ids_back, 16)
            pool.wait_ge(out_zeroed, 32)
            for k in range(K):
                gather(G, agg_tab, ptr, EP - 1, k).then_inc(got[k // KG], 16)
                pool.wait_ge(merged_ready, k + 1)
                if k:
                    pool.wait_ge(added, 16 * k)
                nc.gpsimd.indirect_dma_start(out_tab, bass.IndirectOffsetOnAxis(add_to[:, k:k + 1], 0),
                                             C[:, k * F:(k + 1) * F], None, bounds_check=N + P - 1,
                                             oob_is_err=True, compute_op=ALU.add).then_inc(added, 16)
            pool.wait_ge(added, 16 * K)
            for k in range(K):
                gather(C, out_tab, dst_g, N - 1, k).then_inc(out_d_got, 16)
            pool.wait_ge(dense_go, 1)
            for k in range(K):
                gather(G, out_tab, src_g, N - 1, k).then_inc(out_s_got[k // KG], 16)
            with pool.Fori(2, 6) as r:
                gather_round(r, L0_ROUNDS - 1)
            for u in range(2):
                pool.wait_ge(dense_stored[u], 16 * (ND // 2))
            for k in range(K):
                if k % KG == 0:
                    pool.wait_ge(res_ready, k // KG + 1)
                scatter(out, A, idx_last, k).then_inc(res_stored, 16)

        @block.tensor
        def _(pe):
            pe.wait_ge(iota_done, 7)
            for t in range(2):
                pe.wait_ge(bc_ready, t + 1)
                nc.tensor.matmul(psC[:, P * t:P * (t + 1)], bcm, ident[:], start=True, stop=True).then_inc(bc_done, 1)

            def carry(q, src, matrix, width=F):
                pe.wait_ge(scan_done, q + 1)
                rhs = fm(src)[:, :, K - 1] if matrix is M else fm(src)[:, :, 0]
                nc.tensor.matmul(psC[:, 0:F], matrix[:], rhs, start=True, stop=True).then_inc(carry_done, 1)

            def carry1(q, src, lhs):
                pe.wait_ge(scan_done, q + 1)
                nc.tensor.matmul(psC[:, 0:src.shape[1]], lhs, src, start=True, stop=True).then_inc(carry_done, 1)

            carry1(0, s1[:, K - 1:K], M[:])
            carry1(1, s1[:, 0:1], MT[:])
            pe.wait_ge(zeros_ready, 1)
            zb = zeros.bitcast(bf16)
            for o, w in ((0, 512), (512, RN - 512)):
                nc.tensor.matmul(psW[:, 0, o:o + w], zb[:, 0:P], zb[:, 0:w], start=True, stop=False,
                                 skip_group_check=True)
            with pe.Fori(0, K // 2) as i:
                for u in range(2):
                    pe.wait_ge(hots_ready, i * 2 + u + 1)
                    nc.tensor.matmul(psW[:, 0, 0:512], hot_p[u][:, 0:P], hot_c[u][:, 0:512], start=False,
                                     stop=False, skip_group_check=True)
                    nc.tensor.matmul(psW[:, 0, 512:RN], hot_p[u][:, 0:P], hot_c[u][:, 512:RN], start=False,
                                     stop=False, skip_group_check=True).then_inc(hist_mm, 1)
            for o, w in ((0, 512), (512, RN - 512)):
                mm = nc.tensor.matmul(psW[:, 0, o:o + w], zb[:, 0:P], zb[:, 0:w], start=False, stop=True,
                                      skip_group_check=True)
            mm.then_inc(hist_done, 1)
            pe.wait_ge(iota_done, 7)
            with pe.Fori(0, K) as k:
                pe.wait_ge(diag_ready, k + 1)
                nc.tensor.matmul(psC[:, 0:P], ones[:], diag[:], start=True, stop=True).then_inc(same_done, 1)
            pe.wait_ge(count_ready, 1)
            nc.tensor.matmul(psC[0:1, 0:P], f_one[:, 0:1], ident[:], start=True, stop=True).then_inc(count_done, 1)
            pe.wait_ge(mode_ready, 1)
            few = pe.value_load(flag[0:1, 0:1], min_val=0, max_val=1)
            with pe.If(few > 0):
                pe.wait_ge(f_first_ready, 1)
                nc.tensor.matmul(psC[:, 0:P], bcm, ident[:], start=True, stop=True).then_inc(f_first_done, 1)
                with pe.Fori(0, L0_ROUNDS - 1) as i:
                    pe.wait_ge(f_scan, i + 1)
                    nc.tensor.matmul(psC[:, 0:F], MF, few_acc.rearrange("p (f k) -> p f k", k=KC)[:, :, KC - 1],
                                     start=True, stop=True).then_inc(f_carry, 1)
                pe.wait_ge(scan_done, 3)
                nc.tensor.matmul(psC[:, 0:F], MF, few_acc.rearrange("p (f k) -> p f k", k=KC)[:, :, KC - 1],
                                 start=True, stop=True).then_inc(carry_done, 1)
            with pe.Else():
                with pe.Fori(0, L0_ROUNDS - 1) as i:
                    pe.wait_ge(g_scan, i + 1)
                    nc.tensor.matmul(psC[:, 0:F], M[:], fm(B)[:, :, K - 1], start=True, stop=True).then_inc(g_carry, 1)
                carry(2, B, M)
            carry(3, B, MT)
            pe.wait_ge(s_small, 16 * 18)
            pe.wait_ge(s_w2, 32)
            with pe.Fori(0, N1 // 2) as i:
                for u in range(2):
                    n = i * 2 + u
                    pe.wait_ge(ea_in[u], i * 16 + 16)
                    pe.wait_ge(hid_ready, n + 1)
                    nc.tensor.matmul(psH[0:2 * H, 0:512], w1_sb[:], ea[u][:, 0:512], start=True, stop=True)
                    nc.tensor.matmul(psH[0:2 * H, 512:T1 * P], w1_sb[:], ea[u][:, 512:T1 * P],
                                     start=True, stop=True).then_inc(hid_mm, 1)
                    pe.wait_ge(hid_ready, n + 2)
                    for t in range(T1):
                        m = i * (2 * T1) + (u * T1 + t)
                        slot = (u * T1 + t) % 2
                        pe.wait_ge(wts_ready, m + 1 if (u, t) == (0, 0) else m)
                        nc.tensor.matmul(psW[:, slot, 0:W1C], hid[:, t * P:(t + 1) * P], w2_sb[:, 0:W1C],
                                         start=True, stop=True)
                        nc.tensor.matmul(psW[:, slot, 512:512 + W2C], hid[:, t * P:(t + 1) * P],
                                         w2_sb[:, W1C:WC], start=True, stop=True).then_inc(wts_mm, 1)
            carry(4, C, M)
            carry(5, C, MT)
            with pe.Fori(0, K) as k:
                pe.wait_ge(diag_ready, k + (K + 1))
                nc.tensor.matmul(psC[:, 0:P], ones[:], diag[:], start=True, stop=True).then_inc(same_done, 1)
                pe.wait_ge(equal_ready, k + 1)
                nc.tensor.matmul(psC[:, P:P + F], B[:, 0:P], A[:, bass.ds(k * F, F)], start=True, stop=True).then_inc(merged_mm, 1)

            taken = [0]

            def linear(pairs, chunks=range(LC)):
                for c in chunks:
                    g = taken[0]
                    if g >= 4:
                        pe.wait_ge(lin_out, g - 3)
                    o = psW[:, (g // 2) % 2, 512 * (g % 2):512 * (g % 2) + LW]
                    for i, (t, w) in enumerate(pairs):
                        mm = nc.tensor.matmul(o, w, t[:, c * LW:(c + 1) * LW], start=(i == 0),
                                              stop=(i == len(pairs) - 1))
                    mm.then_inc(lin_mm, 1)
                    taken[0] += 1

            for layer in range(2):
                q = 6 + 2 * layer
                carry(q, B, M)
                pe.wait_ge(lin_in, 3 * layer + 1)
                linear([(C, Wa), (A, Wb)])
                carry(q + 1, C, M)
                pe.wait_ge(lin_in, 3 * layer + 2)
                linear([(C, Wa), (XS, Wb)])
                pe.wait_ge(lin_in, 3 * layer + 3)
                linear([(C, Wc), (XD, ident[:])])
                if layer == 1:
                    pe.wait_ge(lin_out, taken[0])
                    linear([(B, BD[4])])
                    carry(10, XD, MT)
                for g in range(GC):
                    pe.wait_ge(lin_part, layer * GC + g + 1)
                    cc = range(LC // GC * g, LC // GC * (g + 1))
                    linear([(C, Wc), (XS, ident[:])], cc)
                    if layer == 1:
                        pe.wait_ge(lin_out, taken[0])
                        linear([(B, BD[3])], cc)
            q = 10
            carry1(q + 1, ident[:], A[:, 0:P])
            carry1(q + 2, s1[:, 0:1], MT[:])
            carry1(q + 3, s1[:, K - 1:K], M[:])
            carry(q + 4, B, M)

        @block.scalar
        def _(act):
            nstd = [0]

            def sqrt(t):
                act.wait_ge(var_ready, nstd[0] + 1)
                nc.scalar.activation(t, t, ACT.Sqrt).then_inc(std_ready, 1)
                nstd[0] += 1

            def sqrt_groups():
                for g in range(GC):
                    sqrt(s2[:, g * KG:(g + 1) * KG])

            sqrt(s2[:])
            sqrt(norms[:, 0:2, :].rearrange("p a k -> p (a k)"))
            sqrt(f_low)
            sqrt(s2[:])
            sqrt_groups()
            with act.Fori(0, N1 // 2) as i:
                for u in range(2):
                    n = i * 2 + u
                    W = (B, C)[u][:, 0:T1 * WC].rearrange("p (t w) -> p t w", w=WC)
                    act.wait_ge(hid_mm, n + 1)
                    nc.scalar.activation(hid, psH[0:H, 0:T1 * P], ACT.Relu, scale=float(HIN) ** -0.5).then_inc(hid_ready, 1)
                    act.wait_ge(l1_used[u], i + 1)
                    for t in range(T1):
                        m = i * (2 * T1) + (u * T1 + t)
                        slot = (u * T1 + t) % 2
                        act.wait_ge(wts_mm, m + 1)
                        nc.scalar.activation(W[:, t, 0:W1C], psW[:, slot, 0:W1C], ACT.Copy,
                                             scale=0.25 / 32.0 ** 0.5)
                        nc.scalar.activation(W[:, t, W1C:WC], psW[:, slot, 512:512 + W2C], ACT.Copy,
                                             scale=0.25 / 4.0).then_inc(wts_ready, 1)
            sqrt(norms[:, 2:4, :].rearrange("p a k -> p (a k)"))
            act.wait_ge(wts_blank, 1)
            nc.scalar.activation(row(A)[:, :, 0:8], row(A)[:, :, 0:8], ACT.Tanh)
            nc.scalar.activation(gates[:], gates[:], ACT.Tanh).then_inc(l1_tanh, 1)
            sqrt(s2[:])
            sqrt(s2[:])

            def dense_roots(w):
                for t in range(*SPANS[w]):
                    sqrt(s1[0:NP, 0:2 * RC])
                    sqrt(s1[0:NP, 0:RC])
                    sqrt(s1[0:NP, 0:RC])

            dense_roots(0)
            sqrt(s2[:])
            sqrt_groups()

            taken = [0]

            def take(dst, func, bias=None, chunks=range(LC)):
                for c in chunks:
                    g = taken[0]
                    act.wait_ge(lin_mm, g + 1)
                    o = psW[:, (g // 2) % 2, 512 * (g % 2):512 * (g % 2) + LW]
                    if bias is None:
                        nc.scalar.activation(dst[:, c * LW:(c + 1) * LW], o, func).then_inc(lin_out, 1)
                    else:
                        nc.scalar.activation(dst[:, c * LW:(c + 1) * LW], o, func, bias=bias).then_inc(lin_out, 1)
                    taken[0] += 1

            act.wait_ge(x3_spilled, 16)
            for layer in range(2):
                take(XD, ACT.Identity, cb)
                dense_roots(1 + 2 * layer)
                take(XS, ACT.Identity, cb)
                take(B, ACT.Relu)
                if layer == 0:
                    dense_roots(2)
                else:
                    take(C, ACT.Identity, bd_c)
                for g in range(GC):
                    cc = range(LC // GC * g, LC // GC * (g + 1))
                    take(B, ACT.Relu, chunks=cc)
                    if layer == 1:
                        take(A, ACT.Identity, bs_c, chunks=cc)
            act.wait_ge(ex_in, 1)
            nc.scalar.activation(s2[:], s2[:], ACT.Exp).then_inc(ex_out, 1)
            sqrt_groups()

        @block.vector
        def _(dve):
            v = nc.vector
            steps = [0]
            loop = [None, 0, dve_step]

            def link(ins):
                steps[0] += 1
                ins.then_inc(loop[2], 1)
                n = steps[0]
                dve.wait_ge(loop[2], n if loop[0] is None else loop[0] * loop[1] + n)

            nstd = [0]

            def root(ins):
                ins.then_inc(var_ready, 1)
                nstd[0] += 1
                dve.wait_ge(std_ready, nstd[0])

            v.memset(w1_sb[:], 0.0).then_inc(w1_blank, 1)
            dve.wait_ge(s_idx, 32)
            v.tensor_copy(d, dst_i)
            link(v.tensor_copy(srcf, src_i))
            v.tensor_scalar(dst_g, d[:, 1:K + 1], float(N - 1), None, ALU.min).then_inc(dst_g_ready, 1)
            v.tensor_scalar(src_g, srcf, float(N - 1), None, ALU.min).then_inc(dst_g_ready, 1)
            link(v.tensor_tensor(last[:], d[:, 1:K + 1], d[:, 2:K + 2], ALU.not_equal))
            link(v.tensor_scalar(s1[:], d[:, 1:K + 1], float(-NONE), None, ALU.add))
            link(v.tensor_tensor(s1[:], s1[:], last[:], ALU.mult))
            link(v.tensor_scalar(idx_last[:], s1[:], float(NONE), None, ALU.add))
            link(v.tensor_tensor(s2[:], d[:, 1:K + 1], d[:, 0:K], ALU.is_equal))
            link(v.memset(s2[:, 0:1], 0.0))
            link(v.memset(mask_f[:], 0))
            link(v.tensor_copy(fm(mask_f), over_f_fm(s2[:])))
            link(v.tensor_scalar(m_first[:], d[:, 1:K + 1], d[:, 1:2], None, ALU.is_equal))
            link(v.tensor_scalar(m_last[:], d[:, 1:K + 1], d[:, K:K + 1], None, ALU.is_equal))

            dve.wait_ge(c_iota, 5)
            v.tensor_copy(iota_c, iota_i)
            v.tensor_copy(iota_p, iota_q)
            v.tensor_copy(node_row[:, :, 0], node_row[:, :, 0].bitcast(i32))
            link(v.tensor_copy(spare, spare.bitcast(i32)))
            dve.wait_ge(iota_done, 7)
            v.tensor_copy(bcm, d[:, 1:2].broadcast_to([P, P])).then_inc(bc_ready, 1)
            dve.wait_ge(bc_done, 1)
            v.tensor_copy(bcm, d[:, K:K + 1].broadcast_to([P, P])).then_inc(bc_ready, 1)
            dve.wait_ge(bc_done, 2)
            link(v.scalar_tensor_tensor(M[:], psC[:, 0:P], d[:, K:K + 1], M[:], ALU.is_equal, ALU.mult))
            link(v.scalar_tensor_tensor(MT[:], psC[:, P:2 * P], d[:, 1:2], MT[:], ALU.is_equal, ALU.mult))

            def fix(j, m):
                dve.wait_ge(carry_done, j + 1)
                link(v.tensor_copy(cr[:, 0:1], psC[:, 0:1]))
                link(v.scalar_tensor_tensor(s1[:], m[:], cr[:, 0:1], s1[:], ALU.mult, ALU.add))

            link(v.memset(s2[:], 1.0))
            v.tensor_tensor_scan(s1[:], mask_f[:, 0:K], s2[:], 0.0, ALU.mult, ALU.add).then_inc(scan_done, 1)
            dve.wait_ge(scan_done, 1)
            fix(0, m_first)
            v.tensor_copy(node_row[:, :, 1], s1[:]).then_inc(node_row_ready, 1)
            link(v.tensor_scalar(n3d, s1[:], 1.0, None, ALU.max))

            dve.wait_ge(s_small, 16 * 18)
            link(v.reciprocal(rm2, lam_c))
            link(v.tensor_scalar(nre, rm2, -2.0, None, ALU.mult))
            link(v.tensor_scalar(rm1, rm2, 2.0, -1.0, ALU.mult, ALU.add))
            link(v.tensor_scalar(nre2, nre, 2.0, None, ALU.mult))
            link(v.tensor_scalar(rm2, rm1, 2.0, None, ALU.mult))

            r3v = r3[:].rearrange("p (k c) -> p k c", c=3)
            q3 = C[:, 0:3 * K].rearrange("p (k c) -> p k c", c=3)
            link(v.tensor_tensor(q3, r3v, r3v, ALU.mult))
            root(v.tensor_reduce(s2[:], q3, AX, ALU.add))
            link(v.reciprocal(s2[:], s2[:]))
            link(v.tensor_tensor(r3v, r3v, s2[:].unsqueeze(2).broadcast_to([P, K, 3]), ALU.mult))

            def take_carry(q):
                dve.wait_ge(carry_done, q + 1)
                link(v.tensor_copy(cr[:], psC[:, 0:F]))

            def segment_sums(q, msg, acc, res):
                v.tensor_tensor_scan(acc[:], mask_f[:, 0:KF], msg[:], 0.0, ALU.mult, ALU.add).then_inc(scan_done, 1)
                dve.wait_ge(scan_done, q + 1)
                take_carry(q)
                for f in range(F):
                    o = v.scalar_tensor_tensor(row(res)[:, :, f], m_first[:], cr[:, f:f + 1], fm(acc)[:, f, :],
                                               ALU.mult, ALU.add)
                return o

            def spread(q, msg, acc):
                v.tensor_tensor_scan(acc[:, ::-1], mask_f[:, 1:KF + 1][:, ::-1], msg[:, ::-1], 0.0,
                                     ALU.mult, ALU.add).then_inc(scan_done, 1)
                dve.wait_ge(scan_done, q + 1)
                take_carry(q)
                for f in range(F):
                    o = v.scalar_tensor_tensor(fm(acc)[:, f, :], m_last[:], cr[:, f:f + 1], fm(acc)[:, f, :],
                                               ALU.mult, ALU.add)
                link(o)

            def group(g):
                return slice(g * KG, (g + 1) * KG), slice(g * KG * F, (g + 1) * KG * F)

            def layernorm(X, Q, ks=slice(0, K)):
                x, q = row(X)[:, ks, :], row(Q)[:, ks, :]
                link(v.tensor_reduce(s1[:, ks], x, AX, ALU.add))
                link(v.tensor_scalar(s1[:, ks], s1[:, ks], -1.0 / F, None, ALU.mult))
                link(v.tensor_tensor(x, x, over_f(s1[:, ks]), ALU.add))
                link(v.tensor_tensor(q, x, x, ALU.mult))
                link(v.tensor_reduce(s2[:, ks], q, AX, ALU.add))
                root(v.tensor_scalar(s2[:, ks], s2[:, ks], 1.0 / F, EPS, ALU.mult, ALU.add))
                link(v.reciprocal(s2[:, ks], s2[:, ks]))
                return v.tensor_tensor(x, x, over_f(s2[:, ks]), ALU.mult)

            def gathered(r, c=GC - 1):
                for g in range(c + 1) if c == GC - 1 else [c]:
                    dve.wait_ge(got[g], r * (16 * KG) + 16 * KG)

            link(v.tensor_tensor(s2[:], node_row[:, :, 0], last[:], ALU.mult))
            v.tensor_tensor_scan(s1[:, ::-1], mask_f[:, 1:K + 1][:, ::-1], s2[:, ::-1], 0.0,
                                 ALU.mult, ALU.add).then_inc(scan_done, 1)
            dve.wait_ge(scan_done, 2)
            fix(1, m_last)
            link(v.tensor_copy(seg_last, s1[:]))

            link(v.tensor_scalar(s3[:].bitcast(i32), srcf, 1.0 / RN, None, ALU.mult))
            link(v.tensor_copy(s2[:], s3[:].bitcast(i32)))
            link(v.scalar_tensor_tensor(s1[:], s2[:], float(-RN), srcf, ALU.mult, ALU.add))
            for test, by in ((ALU.is_lt, -1.0), (ALU.is_ge, 1.0)):
                link(v.tensor_scalar(s3[:], s1[:], 0.0 if by < 0 else float(RN), None, test))
                link(v.scalar_tensor_tensor(s2[:], s3[:], by, s2[:], ALU.mult, ALU.add))
                link(v.scalar_tensor_tensor(s1[:], s3[:], -by * RN, s1[:], ALU.mult, ALU.add))
            with dve.Fori(0, K // 2) as i:
                for u in range(2):
                    col = bass.ds(i * 2 + u, 1)
                    dve.wait_ge(hist_mm, i * 2 + u + 1)
                    v.tensor_scalar(hot_p[u][:, 0:P], iota_p[:, 0:P], s2[:, col], None, ALU.is_equal)
                    v.tensor_scalar(hot_c[u][:, 0:RN], iota_c[:, 0:RN], s1[:, col], None,
                                    ALU.is_equal).then_inc(hots_ready, 1)
            dve.wait_ge(hist_done, 1)
            v.tensor_copy(stage, psW[0:NP, 0, 0:RN]).then_inc(stage_ready, 1)

            dve.wait_ge(c_far, 2)
            base = steps[0]
            with dve.Fori(0, K) as k:
                loop[0], loop[1] = k, 1
                v.tensor_scalar(diag[:], ident[:], srcf[:, bass.ds(k, 1)], None, ALU.mult).then_inc(diag_ready, 1)
                dve.wait_ge(same_done, k + 1)
                link(v.scalar_tensor_tensor(bcm, psC[:, 0:P], srcf[:, bass.ds(k, 1)], MF, ALU.is_equal, ALU.mult,
                                            accum_out=s3[:, bass.ds(k, 1)]))
            loop[0] = None
            steps[0] = base + K
            link(v.tensor_scalar(s1[:], srcf, float(N), None, ALU.is_lt))
            link(v.scalar_tensor_tensor(s3[:], s3[:], 0.0, s1[:], ALU.is_equal, ALU.mult))
            link(v.scalar_tensor_tensor(s1[:], srcf, spare, s3[:], ALU.subtract, ALU.mult))
            v.tensor_scalar(add_to, s1[:], spare, None, ALU.add).then_inc(ids_ready, 1)
            dve.wait_ge(ids_ready, 1)

            ns = node_s.rearrange("p (k c) -> p k c", c=2)
            dve.wait_ge(node_s_got, 16 * K)
            v.tensor_copy(ptr[:], ns[:, :, 0]).then_inc(ptr_ready, 1)
            link(v.tensor_scalar(live[:], ns[:, :, 0], float(EP), None, ALU.is_lt))
            v.tensor_reduce(f_one[:, 0:1], live[:], AX, ALU.add).then_inc(count_ready, 1)
            dve.wait_ge(count_done, 1)
            link(v.tensor_reduce(f_one[0:1, 1:2], psC[0:1, 0:P], AX, ALU.max))
            v.tensor_scalar(flag[:], f_one[0:1, 1:2], float(FEW_MAX), None, ALU.is_le).then_inc(mode_ready, 1)
            dve.wait_ge(mode_ready, 1)
            root(v.tensor_scalar(n3s, ns[:, :, 1], 1.0, None, ALU.max))
            link(v.reciprocal(norms[:, 0:2, :], norms[:, 0:2, :]))
            link(v.tensor_tensor(n3live[:], n3s, live[:], ALU.mult))
            link(v.tensor_tensor(cs1[:], n3live[:], n3live[:], ALU.mult))
            link(v.tensor_scalar(cs1[:], cs1[:], 0.9, None, ALU.mult))
            dve.wait_ge(node_stored, 16)
            dve.wait_ge(deg_stored, 16)
            dve.wait_ge(out_zeroed, 32)
            dve.wait_ge(few_zeroed, 32)

            few = dve.value_load(flag[0:1, 0:1], min_val=0, max_val=1)
            after = steps[0]
            with dve.If(few > 0):
                steps[0], loop[2] = 0, f_step
                fi, ff = f_int.bitcast(i32), f_tmp

                def packed(value, out, out_col=None):
                    link(v.tensor_tensor(s1[:], kb, value, ALU.add))
                    link(v.tensor_tensor(s1[:], s1[:], live[:], ALU.mult))
                    top()
                    link(v.tensor_copy(fi, f_key))
                    if out_col is not None:
                        link(v.tensor_scalar(f_next.bitcast(i32), fi, 15, None, ALU.arith_shift_right))
                        link(v.tensor_copy(out_col, f_next.bitcast(i32)))
                    link(v.tensor_scalar(fi, fi, PACK - 1, None, ALU.bitwise_and))
                    link(v.tensor_copy(out, fi))

                def top():
                    for j in range(KC // 8):
                        link(v.max(f_key[:, 8 * j:8 * j + 8], s1[:]))
                        if j < KC // 8 - 1:
                            link(v.match_replace(s1[:], f_key[:, 8 * j:8 * j + 8], s1[:], 0.0))

                def index(out, value, where, shift=0.0):
                    link(v.scalar_tensor_tensor(ff, value, shift - NONE, where, ALU.add, ALU.mult))
                    link(v.tensor_scalar(out.bitcast(i32), ff, float(NONE), None, ALU.add))

                kb = s2[:]
                p0 = node_row[:, 0:1, 0]
                link(v.tensor_scalar(kb, node_row[:, :, 0], p0, float(-PACK), ALU.subtract, ALU.mult))
                link(v.tensor_scalar(kb, kb, float(K * PACK), None, ALU.add))
                packed(ns[:, :, 1], f_deg)
                packed(seg_last, f_seg)
                packed(ns[:, :, 0], f_ptr, f_edge)
                link(v.tensor_scalar(f_live, f_key, 0.0, None, ALU.is_gt))
                link(v.tensor_scalar(f_edge, f_edge, -1.0, float(K), ALU.mult, ALU.add))
                link(v.tensor_scalar(f_edge, f_edge, p0, None, ALU.add))
                index(f_edge, f_edge, f_live)
                index(f_ptr, f_ptr, f_live)
                for half, op, by in ((f_low, ALU.bitwise_and, 511), (f_src, ALU.arith_shift_right, 9)):
                    link(v.tensor_scalar(s3[:].bitcast(i32), src_i, by, None, op))
                    link(v.tensor_copy(s3[:], s3[:].bitcast(i32)))
                    packed(s3[:], half)
                link(v.scalar_tensor_tensor(f_src, f_src, 512.0, f_low, ALU.mult, ALU.add))
                index(f_src, f_src, f_live)
                link(v.tensor_scalar(s1[:], d[:, 1:K + 1], 1.0, None, ALU.add))
                link(v.tensor_tensor(s1[:], s1[:], live[:], ALU.mult))
                link(v.tensor_reduce(f_one[:, 2:3], s1[:], AX, ALU.max))
                link(v.tensor_scalar(f_one[:, 2:3], f_one[:, 2:3], -1.0, None, ALU.add))
                link(v.tensor_scalar(s1[:], d[:, 1:K + 1], -1.0, float(2 * NONE), ALU.mult, ALU.add))
                link(v.tensor_tensor(s1[:], s1[:], live[:], ALU.mult))
                top()
                link(v.tensor_scalar(f_dst, f_key, -1.0, float(2 * NONE), ALU.mult, ALU.add))
                link(v.tensor_scalar(f_dst, f_dst, f_one[:, 2:3], None, ALU.min))
                link(v.tensor_scalar(f_m1, f_dst, f_dst[:, 0:1], None, ALU.is_equal))
                link(v.memset(f_same, 0.0))
                link(v.tensor_tensor(f_same[:, 1:KC], f_dst[:, 1:KC], f_dst[:, 0:KC - 1], ALU.is_equal))
                link(v.tensor_copy(few_mask.rearrange("p (f k) -> p f k", k=KC),
                                   f_same.unsqueeze(1).broadcast_to([P, F, KC])))
                dve.wait_ge(c_far, 2)
                v.tensor_copy(bcm, f_dst[:, 0:1].broadcast_to([P, P])).then_inc(f_first_ready, 1)
                dve.wait_ge(f_first_done, 1)
                link(v.scalar_tensor_tensor(MF, psC[:, 0:P], f_one[:, 2:3], MF, ALU.is_equal, ALU.mult))
                link(v.tensor_reduce(f_one[:, 3:4], MF, AX, ALU.max))
                link(v.memset(f_next, 0.0))
                link(v.tensor_copy(f_next[:, 0:KC - 1], f_live[:, 1:KC]))
                link(v.tensor_tensor(f_end[:, 0:KC - 1], f_same[:, 1:KC], f_next[:, 0:KC - 1], ALU.mult))
                link(v.memset(f_end[:, KC - 1:KC], 0.0))
                link(v.tensor_scalar(f_next, f_next, -1.0, 1.0, ALU.mult, ALU.add))
                link(v.tensor_scalar(f_next, f_next, f_one[:, 3:4], None, ALU.mult))
                link(v.tensor_tensor(f_end, f_end, f_next, ALU.max))
                link(v.tensor_scalar(f_end, f_end, -1.0, 1.0, ALU.mult, ALU.add))
                link(v.tensor_tensor(f_end, f_end, f_live, ALU.mult))
                index(f_seg, f_seg, f_end)
                link(v.tensor_copy(f_place, f_place.bitcast(i32)))
                link(v.memset(f_pos, 0.0))
                v.memset(few_g, 0.0).then_inc(f_seg_ready, 1)
                link(v.tensor_scalar(f_cs1, f_deg, 1.0, None, ALU.max))
                link(v.reciprocal(f_cs1, f_cs1))
                link(v.tensor_tensor(f_cs1, f_cs1, f_live, ALU.mult))
                link(v.tensor_scalar(f_cs1, f_cs1, 0.9, None, ALU.mult))
                link(v.memset(G[:], 0.0))
                root(v.tensor_scalar(f_low, f_deg, 1.0, None, ALU.max))
                link(v.reciprocal(f_low, f_low))
                link(v.tensor_tensor(f_low, f_low, f_live, ALU.mult))
                dve.wait_ge(f_x_got, 16 * KC)

                def f_fm(t):
                    return t.rearrange("p (f k) -> p f k", k=KC)

                def f_rt(t):
                    return t.rearrange("p (k f) -> p f k", f=F)

                link(v.tensor_tensor(f_fm(few_w), f_rt(few_g), f_low.unsqueeze(1).broadcast_to([P, F, KC]),
                                     ALU.mult))
                link(v.tensor_scalar(few_c0, few_w, 0.1, None, ALU.mult))
                dve.wait_ge(f_pos_got, 16 * KC)
                link(v.tensor_scalar(f_next, f_pos, 0.0, None, ALU.is_gt))
                index(f_pos, f_pos, f_next, -1.0)
                v.memset(few_g, 0.0).then_inc(f_pos_ready, 1)
                dve.wait_ge(f_pos_ready, 1)
                f_base, F_PASS = steps[0], 7
                with dve.Fori(0, L0_ROUNDS - 1) as i:
                    loop[0], loop[1] = i, F_PASS
                    v.tensor_tensor_scan(few_acc, few_mask, few_w, 0.0, ALU.mult, ALU.add).then_inc(f_scan, 1)
                    dve.wait_ge(f_scan, i + 1)
                    dve.wait_ge(f_carry, i + 1)
                    link(v.tensor_copy(cr[:], psC[:, 0:F]))
                    link(v.tensor_tensor(few_row.rearrange("p (k f) -> p k f", f=F),
                                         f_m1.unsqueeze(2).broadcast_to([P, KC, F]),
                                         cr[:].unsqueeze(1).broadcast_to([P, KC, F]), ALU.mult))
                    link(v.tensor_tensor(f_rt(few_row), f_rt(few_row), f_fm(few_acc), ALU.add))
                    v.tensor_copy(cr[:, 0:1], cr[:, 0:1]).then_inc(f_table, 1)
                    for h in range(2):
                        ks = slice(h * KC // 2, (h + 1) * KC // 2)
                        dve.wait_ge(f_got[h], i * (8 * KC) + 8 * KC)
                        link(v.tensor_tensor(f_fm(few_w)[:, :, ks], f_rt(few_g)[:, :, ks],
                                             f_cs1[:, ks].unsqueeze(1).broadcast_to([P, F, KC // 2]), ALU.mult))
                        link(v.tensor_tensor(f_fm(few_w)[:, :, ks], f_fm(few_w)[:, :, ks], f_fm(few_c0)[:, :, ks],
                                             ALU.add))
                assert steps[0] == f_base + F_PASS, steps[0] - f_base
                loop[0] = None
                steps[0] = f_base + F_PASS * (L0_ROUNDS - 1)
                v.tensor_tensor_scan(few_acc, few_mask, few_w, 0.0, ALU.mult, ALU.add).then_inc(scan_done, 1)
                dve.wait_ge(scan_done, 3)
                take_carry(2)
                link(v.tensor_tensor(few_row.rearrange("p (k f) -> p k f", f=F),
                                     f_m1.unsqueeze(2).broadcast_to([P, KC, F]),
                                     cr[:].unsqueeze(1).broadcast_to([P, KC, F]), ALU.mult))
                v.tensor_tensor(f_rt(few_row), f_rt(few_row), f_fm(few_acc), ALU.add).then_inc(f_exit, 1)
                dve.wait_ge(f_back, 16)
                v.tensor_copy(cr[:, 0:1], cr[:, 0:1]).then_inc(table_ready, 1)
            with dve.Else():
                steps[0], loop[2] = 0, g_step
                nstd[0] -= 1
                root(v.memset(f_low, 1.0))
                dve.wait_ge(xs_got, 16 * K)
                link(v.tensor_tensor(fm(A), row_t(XS), over_f_fm(n3live[:]), ALU.mult))
                link(v.memset(G[:], 1.0))
                link(v.tensor_scalar(C[:], A[:], 0.1, None, ALU.mult))
                base = steps[0]
                PASS = 2 + 2 * GC
                with dve.Fori(0, L0_ROUNDS - 1) as i:
                    loop[0], loop[1] = i, PASS
                    v.tensor_tensor_scan(B[:], mask_f[:, 0:KF], A[:], 0.0, ALU.mult, ALU.add).then_inc(g_scan, 1)
                    dve.wait_ge(g_scan, i + 1)
                    dve.wait_ge(g_carry, i + 1)
                    link(v.tensor_copy(cr[:], psC[:, 0:F]))
                    for f in range(F):
                        o = v.scalar_tensor_tensor(row(A)[:, :, f], m_first[:], cr[:, f:f + 1], fm(B)[:, f, :],
                                                   ALU.mult, ALU.add)
                    link(o)
                    v.tensor_copy(cr[:, 0:1], cr[:, 0:1]).then_inc(g_table, 1)
                    for c in range(GC):
                        dve.wait_ge(g_got[c], i * (16 * KG) + 16 * KG)
                        ks = slice(c * KG, (c + 1) * KG)
                        link(v.tensor_tensor(fm(A)[:, :, ks], row_t(G)[:, :, ks], over_f_fm(cs1[:, ks]), ALU.mult))
                        link(v.tensor_tensor(fm(A)[:, :, ks], fm(A)[:, :, ks], fm(C)[:, :, ks], ALU.add))
                assert steps[0] == base + PASS
                loop[0] = None
                steps[0] = base + PASS * (L0_ROUNDS - 1)
                segment_sums(2, A, B, A).then_inc(table_ready, 1)
            steps[0], loop[2] = after, dve_step
            dve.wait_ge(table_ready, 1)
            dve.wait_ge(xd_got, 16 * K)
            link(v.tensor_tensor(s1[:], n3d, last[:], ALU.mult))
            link(v.tensor_scalar(s1[:], s1[:], 0.9, None, ALU.mult))
            link(v.tensor_tensor(fm(C), row_t(A), over_f_fm(s1[:]), ALU.mult))
            spread(3, C, B)
            link(v.scalar_tensor_tensor(row_t(XD), row_t(XD), 1.1, fm(B), ALU.mult, ALU.add))
            link(layernorm(XD, C))
            dve.wait_ge(xs_got, 16 * K)
            for g in range(GC):
                ks, cs = group(g)
                gathered(0, g)
                link(v.scalar_tensor_tensor(row(G)[:, ks, :], row(G)[:, ks, :], 0.9, over_f(n3live[:, ks]),
                                            ALU.mult, ALU.mult))
                link(v.scalar_tensor_tensor(XS[:, cs], XS[:, cs], 1.1, G[:, cs], ALU.mult, ALU.add))
                link(layernorm(XS, C, ks))

            dve.wait_ge(ids_stored, 16)
            v.tensor_copy(s1[:].bitcast(i32), dst_g).then_inc(deg_idx_ready, 1)
            v.tensor_copy(s2[:].bitcast(i32), src_g).then_inc(deg_idx_ready, 1)
            dve.wait_ge(deg_idx_ready, 2)
            link(v.memset(U[:], 0.0))
            v.memset(w2_sb, 0.0).then_inc(w2_free, 1)
            PR = G[:, 0:T1 * 96 * 8].rearrange("p (t u w) -> p t u w", u=96, w=8)
            PF = G[:, 0:T1 * 96 * 8].rearrange("p (g u w) -> p g w u", u=16, w=8)
            P2 = G[:, 0:T1 * 64 * 8].rearrange("p (t u w) -> p t u w", u=64, w=8)
            P2F = G[:, 0:T1 * 64 * 8].rearrange("p (g u w) -> p g w u", u=8, w=8)
            base = steps[0]
            with dve.Fori(0, N1 // 2) as i:
                loop[0], loop[1] = i, 2 * L1_LINKS
                for u in range(2):
                    k0 = i * (2 * T1) + u * T1
                    W = (B, C)[u][:, 0:T1 * WC].rearrange("p (t w) -> p t w", w=WC)
                    Wm = W[:, :, 0:W1C].rearrange("p t (u w) -> p t u w", w=8)
                    Wn = W[:, :, W1C:WC].rearrange("p t (u w) -> p t u w", w=8)
                    xs = row(XS)[:, bass.ds(k0, T1), :]
                    xd = row(XD)[:, bass.ds(k0, T1), :]
                    rr = r3v[:, bass.ds(k0, T1), :]
                    for j, z in enumerate((xs, xd)):
                        v.tensor_copy(in48[:, :, 8 * j:8 * j + 8], z[:, :, 0:8])
                        v.tensor_copy(in48[:, :, 32 + 8 * j:40 + 8 * j], z[:, :, 0:8])
                        vr = G[:, 0:T1 * 24].rearrange("p (t v c) -> p t v c", v=8, c=3)
                        link(v.tensor_tensor(vr, z[:, :, 8:F].rearrange("p t (v c) -> p t v c", c=3),
                                             rr.unsqueeze(2).broadcast_to([P, T1, 8, 3]), ALU.mult))
                        link(v.tensor_reduce(in48[:, :, 16 + 8 * j:24 + 8 * j], vr, AX, ALU.add))
                    dve.wait_ge(wts_ready, i * (2 * T1) + ((u + 1) * T1 + 1))
                    v.tensor_tensor(PR[:, :, 0:48, :], Wm[:, :, 0:48, :],
                                    in48[:].unsqueeze(3).broadcast_to([P, T1, 48, 8]), ALU.mult)
                    for c in range(3):
                        for j, z in enumerate((xs, xd)):
                            vec = z[:, :, 8:F].rearrange("p t (v c) -> p t v c", c=3)[:, :, :, c]
                            o = v.tensor_tensor(PR[:, :, 48 + 16 * c + 8 * j:56 + 16 * c + 8 * j, :],
                                                Wm[:, :, 48 + 8 * j:56 + 8 * j, :],
                                                vec.unsqueeze(3).broadcast_to([P, T1, 8, 8]), ALU.mult)
                    link(o)
                    S6 = sums[:].rearrange("p t g w -> p (t g) w")[:, 0:T1 * 6, :]
                    link(v.tensor_reduce(S6, PF, AX, ALU.add))
                    S6 = S6.rearrange("p (t g) w -> p t g w", g=6)
                    for j in (0, 16, 32):
                        v.tensor_tensor(in48[:, :, j:j + 8], S6[:, :, 0, :], S6[:, :, 1, :], ALU.add)
                    for c in range(3):
                        o = v.tensor_tensor(vt[:, :, c, :], S6[:, :, 2, :],
                                            rr[:, :, c:c + 1].broadcast_to([P, T1, 8]), ALU.mult)
                    link(o)
                    link(v.scalar_tensor_tensor(vt[:], vt[:], S3, S6[:, :, 3:6, :], ALU.mult, ALU.add))
                    pv = G[:, 0:T1 * 24].rearrange("p (t c w) -> p t c w", c=3, w=8)
                    link(v.tensor_tensor(pv, vt[:], rr.unsqueeze(3).broadcast_to([P, T1, 3, 8]), ALU.mult))
                    for j in (8, 24):
                        o = v.tensor_reduce(in48[:, :, j:j + 8], pv.rearrange("p t c w -> p t w c"), AX, ALU.add)
                    link(o)
                    v.tensor_tensor(P2[:, :, 0:40, :], Wn[:, :, 0:40, :],
                                    in48[:, :, 0:40].unsqueeze(3).broadcast_to([P, T1, 40, 8]), ALU.mult)
                    for c in range(3):
                        o = v.tensor_tensor(P2[:, :, 40 + 8 * c:48 + 8 * c, :], Wn[:, :, 40:48, :],
                                            vt[:, :, c, :].unsqueeze(3).broadcast_to([P, T1, 8, 8]), ALU.mult)
                    o.then_inc(l1_used[u], 1)
                    dve.wait_ge(l1_used[u], i + 2)
                    link(v.tensor_reduce(sums[:].rearrange("p t g w -> p (t g) w"), P2F, AX, ALU.add))
                    a = row(A)[:, bass.ds(k0, T1), :]
                    v.tensor_tensor(a[:, :, 0:8], sums[:, :, 0, :], sums[:, :, 1, :], ALU.add)
                    v.tensor_tensor(gates[:, bass.ds(k0, T1), :], sums[:, :, 2, :], sums[:, :, 3, :], ALU.add)
                    for c in range(3):
                        o = v.tensor_tensor(vt[:, :, c, :], sums[:, :, 4, :],
                                            rr[:, :, c:c + 1].broadcast_to([P, T1, 8]), ALU.mult)
                    link(o)
                    link(v.scalar_tensor_tensor(vt[:], vt[:], S3, sums[:, :, 5:8, :], ALU.mult, ALU.add))
                    link(v.tensor_copy(a[:, :, 8:F].rearrange("p t (w c) -> p t c w", c=3), vt[:]))
            assert steps[0] == base + 2 * L1_LINKS, steps[0] - base
            loop[0] = None
            steps[0] = base + 2 * L1_LINKS * (N1 // 2)
            dve.wait_ge(deg_got, 2 * 16 * K)
            root(v.tensor_scalar(norms[:, 2:4, :], norms[:, 2:4, :], 1.0, None, ALU.add))
            link(v.reciprocal(norms[:, 2:4, :], norms[:, 2:4, :]))
            v.memset(U[:], 0.0).then_inc(wts_blank, 1)
            dve.wait_ge(l1_tanh, 1)
            av = row(A)[:, :, 8:F].rearrange("p k (w c) -> p k w c", c=3)
            link(v.tensor_tensor(av, av, gates[:].unsqueeze(3).broadcast_to([P, K, 8, 3]), ALU.mult))
            link(v.tensor_tensor(fm(B), row_t(A), over_f_fm(ewt[:]), ALU.mult))
            segment_sums(4, B, C, A).then_inc(table_ready, 1)
            dve.wait_ge(table_ready, 2)
            link(v.tensor_tensor(fm(B), row_t(A), over_f_fm(last[:]), ALU.mult))
            spread(5, B, C)
            link(v.tensor_tensor(row_t(XD), row_t(XD), fm(C), ALU.add))
            link(layernorm(XD, B))

            dve.wait_ge(ids_back, 16)
            link(v.tensor_scalar(s1[:], srcf, float(N), None, ALU.is_lt))
            link(v.tensor_tensor(s1[:], s1[:], n2d, ALU.mult))
            dve.wait_ge(table_stored, 32)
            link(v.tensor_tensor(row(A), row(XD), over_f(s1[:]), ALU.mult))
            base = steps[0]
            bcq = B[:, 0:P]
            with dve.Fori(0, K) as k:
                loop[0], loop[1] = k, 0
                v.tensor_scalar(diag[:], ident[:], srcf[:, bass.ds(k, 1)], None, ALU.mult).then_inc(diag_ready, 1)
                dve.wait_ge(same_done, k + (K + 1))
                v.tensor_scalar(bcq, psC[:, 0:P], srcf[:, bass.ds(k, 1)], None, ALU.is_equal).then_inc(equal_ready, 1)
                dve.wait_ge(merged_mm, k + 1)
                v.tensor_copy(C[:, bass.ds(k * F, F)], psC[:, P:P + F]).then_inc(merged_ready, 1)
            loop[0] = None
            gathered(1)
            link(v.tensor_tensor(row(B), row(G), over_f(live[:]), ALU.mult))
            link(v.tensor_tensor(XS[:], XS[:], B[:], ALU.add))
            link(layernorm(XS, B))
            Q = DQ.rearrange("p (r f) -> p r f", f=F)
            S = DS.rearrange("p (r f) -> p r f", f=F)
            z1, z4 = s1[0:NP, 0:RC], s1[0:NP, RC:2 * RC]
            z2, z3 = s2[0:NP, 0:RC], s3[0:NP, 0:RC]

            def wide(z):
                return z.unsqueeze(2).broadcast_to([NP, RC, F])

            def dense_span(w):
                v.tensor_copy(cr[:, 0:1], c_bias[:, 0:1]).then_inc(dense_go, 1)
                for t in range(*SPANS[w]):
                    X = DX[t % 2].rearrange("p (r f) -> p r f", f=F)
                    deg = DN[t % 2]

                    def centre():
                        link(v.tensor_reduce(z1, X, AX, ALU.add))
                        link(v.tensor_scalar(z1, z1, -1.0 / F, None, ALU.mult))
                        link(v.tensor_tensor(X, X, wide(z1), ALU.add))

                    def squares():
                        link(v.tensor_tensor(Q, X, X, ALU.mult))
                        link(v.tensor_reduce(z2, Q, AX, ALU.add))

                    dve.wait_ge(x_in[t % 2], 32 * (t // 2 + 1))
                    centre()
                    squares()
                    link(v.tensor_scalar(z2, z2, 1.0 / F, None, ALU.mult))
                    link(v.tensor_scalar(z1, z2, 1.21, EPS, ALU.mult, ALU.add))
                    link(v.reciprocal(z1, z1))
                    link(v.tensor_scalar(z1, z1, 1.21, None, ALU.mult))
                    link(v.tensor_tensor(z2, z2, z1, ALU.mult))
                    link(v.tensor_scalar(z3, z2, EPS, None, ALU.add))
                    link(v.reciprocal(z3, z3))
                    link(v.tensor_tensor(z1, z1, z3, ALU.mult))
                    link(v.tensor_scalar(z4, deg, 1.0, None, ALU.add))
                    link(v.reciprocal(z4, z4))
                    root(v.tensor_scalar(z3, z4, 1.0, None, ALU.add))
                    link(v.tensor_tensor(z1, z1, z3, ALU.mult))
                    link(v.tensor_tensor(X, X, wide(z1), ALU.mult))
                    dve.wait_ge(sums_in, 16 * (t + 1))
                    link(v.tensor_tensor(S, S, wide(z4), ALU.mult))
                    v.tensor_tensor(X, X, S, ALU.add).then_inc(sums_used, 1)
                    dve.wait_ge(sums_used, t + 1)
                    for layer in (2, 3):
                        centre()
                        squares()
                        root(v.tensor_scalar(z1, z2, 1.0 / F, EPS, ALU.mult, ALU.add))
                        link(v.reciprocal(z1, z1))
                        o = v.tensor_tensor(X, X, wide(z1), ALU.mult)
                        if layer == 2:
                            link(o)
                            link(v.tensor_tensor(X, X, c_bias[0:NP, :].unsqueeze(1).broadcast_to([NP, RC, F]), ALU.add))
                    o.then_inc(dense_ready, 1)
                    dve.wait_ge(dense_ready, t + 1)

            def dense_out(w):
                t1 = SPANS[w][1]
                for u in range(2):
                    dve.wait_ge(dense_stored[u], 16 * ((t1 + 1 - u) // 2))

            def own_row(X, T, own, n, ks, cs):
                link(v.tensor_tensor(row(T)[:, ks, :], row(X)[:, ks, :], over_f(n[:, ks]), ALU.mult))
                link(v.tensor_tensor(T[:, cs], T[:, cs], own[:, cs], ALU.add))
                link(v.tensor_tensor(row(T)[:, ks, :], row(T)[:, ks, :], over_f(n[:, ks]), ALU.mult))
                link(v.tensor_tensor(X[:, cs], X[:, cs], T[:, cs], ALU.add))
                return layernorm(X, T, ks)

            dense_span(0)
            dense_out(0)
            dve.wait_ge(out_d_got, 16 * K)
            own_row(XD, B, C, n2d, slice(0, K), slice(0, KF)).then_inc(x3_ready, 1)
            dve.wait_ge(x3_ready, 1)
            for g in range(GC):
                ks, cs = group(g)
                dve.wait_ge(out_s_got[g], 16 * KG)
                link(own_row(XS, B, G, n2s, ks, cs))
                link(v.tensor_tensor(fm(A)[:, :, ks], row_t(XS)[:, :, ks], over_f_fm(n3s[:, ks]), ALU.mult))

            dve.wait_ge(s_wts, 16 * 20)
            link(v.tensor_tensor(Wa, BD[0], BD[2], ALU.subtract))
            link(v.scalar_tensor_tensor(Wb, BD[2], rm2, BD[1], ALU.mult, ALU.add))
            link(v.tensor_scalar(Wc, BD[2], nre2, None, ALU.mult))
            for layer in range(2):
                r = 2 + 2 * layer
                q = 6 + 2 * layer
                n = 4 * LC * layer
                m = 3 * layer
                segment_sums(q, A, B, A).then_inc(table_ready, 1)
                dve.wait_ge(table_ready, r + 1)
                link(v.scalar_tensor_tensor(row(B), row(A), nre, over_f(n3d), ALU.mult, ALU.mult))
                link(v.scalar_tensor_tensor(B[:], XD[:], rm1, B[:], ALU.mult, ALU.add))
                link(v.transpose(C[:], XD[:]))
                dve.wait_ge(table_stored, 16 * (r + 1))
                v.transpose(A[:], B[:]).then_inc(lin_in, 1)
                dve.wait_ge(lin_in, m + 1)
                dve.wait_ge(lin_out, n + LC)
                dense_span(1 + 2 * layer)
                dense_out(1 + 2 * layer)
                for g in range(GC):
                    ks, cs = group(g)
                    gathered(r, g)
                    link(v.scalar_tensor_tensor(row(B)[:, ks, :], row(G)[:, ks, :], nre, over_f(n3live[:, ks]),
                                                ALU.mult, ALU.mult))
                    link(v.scalar_tensor_tensor(B[:, cs], XS[:, cs], rm1, B[:, cs], ALU.mult, ALU.add))
                    link(v.tensor_tensor(fm(A)[:, :, ks], row_t(B)[:, :, ks], over_f_fm(n3s[:, ks]), ALU.mult))
                segment_sums(q + 1, A, C, A).then_inc(table_ready, 1)
                dve.wait_ge(table_ready, r + 2)
                link(v.transpose(C[:], XS[:]))
                v.transpose(XS[:], B[:]).then_inc(lin_in, 1)
                dve.wait_ge(lin_in, m + 2)
                link(v.tensor_tensor(row(B), row(A), over_f(n3d), ALU.mult))
                dve.wait_ge(lin_out, n + 2 * LC)
                v.transpose(C[:], B[:]).then_inc(lin_in, 1)
                dve.wait_ge(lin_in, m + 3)
                dve.wait_ge(lin_out, n + 3 * LC)
                if layer == 0:
                    link(v.transpose(XD[:], B[:]))
                    dve.wait_ge(table_stored, 16 * (r + 2))
                    dense_span(2)
                    dense_out(2)
                else:
                    dve.wait_ge(lin_out, n + 4 * LC)
                    link(v.transpose(XD[:], C[:]))
                    dve.wait_ge(table_stored, 16 * (r + 2))
                    link(v.tensor_tensor(fm(A), row_t(XD), over_f_fm(last[:]), ALU.mult))
                    spread(10, A, XD)
                for g in range(GC + 1):
                    if g < GC:
                        ks, cs = group(g)
                        gathered(r + 1, g)
                        link(v.tensor_tensor(row(G)[:, ks, :], row(G)[:, ks, :], over_f(n3live[:, ks]), ALU.mult))
                        v.transpose(C[:, cs], G[:, cs]).then_inc(lin_part, 1)
                    if g and layer == 0:
                        ks, cs = group(g - 1)
                        dve.wait_ge(lin_out, n + 3 * LC + LC // GC * g)
                        link(v.transpose(XS[:, cs], B[:, cs]))
                        link(v.tensor_tensor(fm(A)[:, :, ks], row_t(XS)[:, :, ks], over_f_fm(n3s[:, ks]), ALU.mult))
                    if g and layer == 1:
                        ks, cs = group(g - 1)
                        dve.wait_ge(lin_out, n + 4 * LC + 2 * (LC // GC) * g)
                        e = fm(XD)[:, :, ks]
                        link(v.transpose(XS[:, cs], A[:, cs]))
                        link(v.tensor_tensor(e, e, row_t(XS)[:, :, ks], ALU.add))
                        link(v.scalar_tensor_tensor(e, e, 0.2, e, ALU.mult, ALU.max))
                        link(v.tensor_tensor(e, e, c_attn[:].unsqueeze(2).broadcast_to([P, F, KG]), ALU.mult))
                        o = v.tensor_reduce(s3[:, ks], e.rearrange("p f k -> p k f"), AX, ALU.add)
                        if g < GC:
                            link(o)
            o.then_inc(xd_free, 1)
            dve.wait_ge(xd_free, 1)
            q = 10
            msk = mask_f[:, 0:K]
            link(v.tensor_scalar(s1[:], msk, BIG, -BIG, ALU.mult, ALU.add))
            link(v.tensor_tensor_scan(s2[:], s1[:], s3[:], -BIG, ALU.add, ALU.max))
            v.tensor_copy(A[:, 0:P], s2[:, K - 1:K].broadcast_to([P, P])).then_inc(scan_done, 1)
            link(v.tensor_scalar(A[:, P:2 * P], MT[:], BIG, -BIG, ALU.mult, ALU.add))
            dve.wait_ge(carry_done, q + 2)
            link(v.tensor_tensor(A[:, P:2 * P], A[:, P:2 * P], psC[:, 0:P], ALU.add))
            link(v.tensor_reduce(cr[:, 0:1], A[:, P:2 * P], AX, ALU.max))
            link(v.tensor_scalar(s1[:], m_first[:], BIG, -BIG, ALU.mult, ALU.add))
            link(v.scalar_tensor_tensor(s1[:], m_first[:], cr[:, 0:1], s1[:], ALU.mult, ALU.add))
            link(v.tensor_tensor(s2[:], s2[:], s1[:], ALU.max))
            link(v.tensor_tensor(s2[:], s2[:], last[:], ALU.mult))
            v.tensor_tensor_scan(s1[:, ::-1], mask_f[:, 1:K + 1][:, ::-1], s2[:, ::-1], 0.0,
                                 ALU.mult, ALU.add).then_inc(scan_done, 1)
            dve.wait_ge(scan_done, q + 3)

            fix(q + 2, m_last)
            v.tensor_tensor(s2[:], s3[:], s1[:], ALU.subtract).then_inc(ex_in, 1)
            dve.wait_ge(ex_out, 1)
            v.tensor_tensor_scan(s1[:], msk, s2[:], 0.0, ALU.mult, ALU.add).then_inc(scan_done, 1)
            dve.wait_ge(scan_done, q + 4)
            fix(q + 3, m_first)
            link(v.tensor_scalar(s1[:], s1[:], 1e-6, None, ALU.max))
            link(v.reciprocal(s3[:], s1[:]))
            link(v.tensor_tensor(fm(A), row_t(XS), over_f_fm(s2[:]), ALU.mult))
            link(segment_sums(q + 4, A, B, A))
            dve.wait_ge(x3_back, 16)
            for g in range(GC):
                ks, cs = group(g)
                a = row(A)[:, ks, :]
                link(v.tensor_tensor(a, a, over_f(s3[:, ks]), ALU.mult))
                link(v.tensor_tensor(a, a, c_bias[:].unsqueeze(1).broadcast_to([P, KG, F]), ALU.add))
                link(v.tensor_tensor(A[:, cs], A[:, cs], XD[:, cs], ALU.add))
                layernorm(A, C, ks).then_inc(res_ready, 1)


def kernel(x, src, dst, edge_attr_10, edge_attr_3, edge_weight, L1_gnn_fc1_w1, L1_gnn_fc1_w2, L1_gnn_fc2_w1,
           L1_gnn_fc2_w2, L3_gnn_laplacian_lambda_max, L3_gnn_cheb_W, L3_gnn_cheb_b, L3_gnn_gat_Wsrc,
           L3_gnn_gat_bsrc, L3_gnn_gat_Wdst, L3_gnn_gat_bdst, L3_gnn_gat_attn, L3_gnn_gat_bias):
    import numpy as np
    import concourse.bacc as bacc
    from concourse.bass_utils import run_bass_kernel_spmd

    P, E = 128, src.shape[0]
    K = -(-E // P)
    pad = P * K - E

    def padded(a, value):
        a = np.asarray(a)
        return np.concatenate([a, np.full((pad,) + a.shape[1:], value, a.dtype)])

    def tiles(a, value):
        return np.ascontiguousarray(padded(a, value).reshape(P, -1))

    d = np.concatenate([np.full(1, -1, np.int32), padded(dst, 200000), np.full(1, -2, np.int32)])
    dst_ext = np.stack([d[p * K:p * K + K + 2] for p in range(P)])
    ea10 = padded(edge_attr_10, 0).reshape(P, K, -1)
    arrays = {
        "x": np.asarray(x),
        "dst_ext": dst_ext,
        "src_idx": tiles(src, 200000),
        "ea10_t": np.ascontiguousarray(ea10.transpose(2, 1, 0).reshape(ea10.shape[2], K * P)),
        "ea3": tiles(edge_attr_3, 1),
        "ew": tiles(edge_weight, 0),
        "w1cat": np.concatenate([np.asarray(L1_gnn_fc1_w1), np.asarray(L1_gnn_fc2_w1)], axis=1),
        "fc1_w2": np.asarray(L1_gnn_fc1_w2),
        "fc2_w2": np.asarray(L1_gnn_fc2_w2),
        "lam": np.asarray(L3_gnn_laplacian_lambda_max),
        "cheb_wt": np.ascontiguousarray(np.asarray(L3_gnn_cheb_W).T),
        "cheb_b": np.asarray(L3_gnn_cheb_b),
        "wsrc_t": np.ascontiguousarray(np.asarray(L3_gnn_gat_Wsrc).T),
        "bsrc": np.asarray(L3_gnn_gat_bsrc),
        "wdst_t": np.ascontiguousarray(np.asarray(L3_gnn_gat_Wdst).T),
        "bdst": np.asarray(L3_gnn_gat_bdst),
        "attn": np.asarray(L3_gnn_gat_attn).reshape(-1),
        "gat_bias": np.asarray(L3_gnn_gat_bias),
    }
    nc = bacc.Bacc("TRN2", target_bir_lowering=False, num_devices=1)
    aps = [nc.dram_tensor(f"in_{n}", a.shape, mybir.dt.from_np(a.dtype), kind="ExternalInput").ap()
           for n, a in arrays.items()]
    out = nc.dram_tensor("out_rows", x.shape, mybir.dt.float32, kind="ExternalOutput").ap()
    gnn_resnorm_kernel(nc, *aps, out)
    r = run_bass_kernel_spmd(nc, [{f"in_{n}": a for n, a in arrays.items()}], core_ids=[0])
    return r.results[0]["out_rows"]
```

```python
import concourse.bass as bass
from concourse import mybir
from contextlib import ExitStack


def gnn_resnorm_kernel(nc, x, dst_ext, src_idx, ea10_t, ea3, ew, w1cat, fc1_w2, fc2_w2, lam,
                       cheb_wt, cheb_b, wsrc_t, bsrc, wdst_t, bdst, attn, gat_bias, out):
    fp32, i32, u8 = mybir.dt.float32, mybir.dt.int32, mybir.dt.uint8
    ALU = mybir.AluOpType
    ACT = mybir.ActivationFunctionType
    AX = mybir.AxisListType.X

    N, F = x.shape
    P = 128
    K = src_idx.shape[1]
    EP = P * K
    KF = K * F
    NONE = 200000
    EPS = 1e-5
    BIG = 1e30
    NP, NR = 125, N // 125
    ND = 10
    SPANS = ((0, 3), (3, 5), (5, 7), (7, 9), (9, 10))
    RC = NR // ND
    GC = 7
    KG = K // GC
    T1 = 7
    N1 = K // T1
    LC = 14
    LW = KF // LC
    H = w1cat.shape[1]
    HIN = w1cat.shape[0]
    W1C, W2C = fc1_w2.shape[1], fc2_w2.shape[1]
    WC = W1C + W2C
    S3 = 3.0 ** 0.5
    L0_ROUNDS = 10
    KC = 64
    FEW_MAX = KC
    XS_FIRST = 56
    XS_FILL = -(-(K - XS_FIRST) // (L0_ROUNDS - 1))
    EC = P * KC
    KCF = KC * F
    PACK = 32768
    L1_PARTS = ((0, 1), (1, 4), (4, 7))
    L1_LINKS = 13

    node_tab = nc.dram_tensor("node_tab", [N, 2], fp32).ap()
    deg_tab = nc.dram_tensor("deg_tab", [N, 1], fp32).ap()
    out_tab = nc.dram_tensor("out_tab", [N + 2 * P, F], fp32).ap()
    few_tab = nc.dram_tensor("few_tab", [EC, F], fp32).ap()
    few_pos = nc.dram_tensor("few_pos", [EP, 1], fp32).ap()
    ids_tab = nc.dram_tensor("ids_tab", [P, 4 * K], fp32).ap()
    agg_tab = nc.dram_tensor("agg_tab", [EP, F], fp32).ap()
    x3_tab = nc.dram_tensor("x3_tab", [P, KF], fp32).ap()

    ctx = ExitStack()
    with ctx:
        def sb(name, shape, dt=fp32):
            return ctx.enter_context(nc.sbuf_tensor(name, shape, dt))

        def sem(name):
            return ctx.enter_context(nc.semaphore(name))

        gates = sb("gates", [P, K, 8])
        XS, XD, G, A, B, C = (sb(n, [P, KF]) for n in ("XS", "XD", "G", "A", "B", "C"))
        mask_f = sb("mask_f", [P, KF + 4], u8)
        U = sb("U", [P, 3 * T1 * P])
        r3 = sb("r3", [P, K * 3])
        last = sb("last", [P, K])
        m_first = sb("m_first", [P, K])
        m_last = sb("m_last", [P, K])
        ewt = sb("ewt", [P, K])
        live = sb("live", [P, K])
        norms = sb("norms", [P, 4, K])
        n3s, n3d, n2s, n2d = (norms[:, i, :] for i in range(4))
        n3live = sb("n3live", [P, K])
        cs1 = sb("cs1", [P, K])
        idx_last = sb("idx_last", [P, K], i32)
        ptr = sb("ptr", [P, K], i32)
        s1, s2, s3 = (sb(n, [P, K]) for n in ("s1", "s2", "s3"))
        ident = sb("ident", [P, P])
        M = sb("M", [P, P])
        MT = sb("MT", [P, P])
        cr = sb("cr", [P, F])
        flag = sb("flag", [1, 1], i32)
        tick = sb("tick", [P, 16])
        c_bias = sb("c_bias", [P, F])
        c_attn = sb("c_attn", [P, F])
        cols = sb("cols", [P, 8])
        cb, bs_c, bd_c, lam_c, nre, rm1, rm2, nre2 = (cols[:, i:i + 1] for i in range(8))

        dst_i = U[:, 0:K + 2].bitcast(i32)
        src_i = U[:, 200:200 + K].bitcast(i32)
        node_row = U[:, 400:400 + 2 * K].rearrange("p (k c) -> p k c", c=2)
        ids = U[:, 1024:1024 + 4 * K]
        src_g, dst_g, add_to = (U[:, 1024 + K * i:1024 + K * (i + 1)].bitcast(i32) for i in range(3))
        srcf = U[:, 1024 + 3 * K:1024 + 4 * K]
        d = U[:, 2004:2004 + K + 2]
        seg_last = U[:, 2360:2360 + K]
        spare = U[:, 2210:2211]
        spare_odd = U[:, 2212:2213]
        bcm = U[:, 2220:2220 + P]
        RN = NR
        fp16, bf16 = mybir.dt.float16, mybir.dt.bfloat16
        iota_c = G[:, 0:400].bitcast(fp16)
        iota_p = G[:, 400:464].bitcast(fp16)
        hot_c = [G[:, 464 + 400 * u:864 + 400 * u].bitcast(bf16) for u in range(2)]
        hot_p = [G[:, 1264 + 64 * u:1328 + 64 * u].bitcast(bf16) for u in range(2)]
        stage = G[0:NP, 1392:1392 + RN]
        iota_i = G[:, 1392:1392 + RN].bitcast(i32)
        iota_q = G[:, 2192:2192 + P].bitcast(i32)
        zeros = G[:, 3792:3792 + 1024]
        node_s = G[:, 5532:5532 + 2 * K]
        blank = A[0:NP, 0:2 * RN].rearrange("p (c w) -> p c w", w=2)
        few_w, few_acc, few_row = (B[:, KCF * i:KCF * (i + 1)] for i in range(3))
        few_g, few_c0 = (C[:, KCF * i:KCF * (i + 1)] for i in range(2))
        few_mask = C[:, 2 * KCF:2 * KCF + KCF // 4].bitcast(u8)
        gt = gates[:].rearrange("p k w -> p (k w)")
        MF = gt[:, 0:P]
        (f_key, f_int, f_ptr, f_edge, f_dst, f_seg, f_deg, f_live, f_same, f_place, f_pos, f_m1, f_cs1, f_end,
         f_tmp, f_next, f_src, f_low) = (gt[:, P + KC * i:P + KC * (i + 1)] for i in range(18))
        f_one = gt[:, P + 18 * KC:P + 18 * KC + 8]
        diag = sb("diag", [P, P])
        diag_odd = B[:, 512:512 + P]
        ones = sb("ones", [P, P])
        ea = U[0:HIN, 0:T1 * P]
        hid = U[0:H, T1 * P:2 * T1 * P]
        sums = U[:, 2 * T1 * P:2 * T1 * P + 2 * T1 * 64].rearrange("p (t g w) -> p t g w", g=8, w=8)
        BD = [U[:, P * i:P * (i + 1)] for i in range(5)]
        Wa, Wb, Wc = (U[:, P * i:P * (i + 1)] for i in range(5, 8))
        w1_sb = sb("w1_sb", [HIN, 2 * H])
        in48 = sb("in48", [P, 2 * T1, 48])
        vt = sb("vt", [P, 2 * T1, 3, 8])
        w2_sb = G[0:H, KF - WC:KF]

        psW = ctx.enter_context(nc.psum_tensor("psW", [P, 2, 1024], fp32))
        psH = ctx.enter_context(nc.psum_tensor("psH", [P, 1024], fp32))
        psC = ctx.enter_context(nc.psum_tensor("psC", [P, 512], fp32))

        def bank(i):
            return psW[:, i // 2, 512 * (i % 2):512 * (i % 2) + 512]

        def row(t):
            return t[:, 0:KF].rearrange("p (k f) -> p k f", f=F)

        def row_t(t):
            return t[:, 0:KF].rearrange("p (k f) -> p f k", f=F)

        def fm(t):
            return t[:, 0:KF].rearrange("p (f k) -> p f k", k=K)

        def over_f(s):
            return s.unsqueeze(2).broadcast_to([P, s.shape[1], F])

        def over_f_fm(s):
            return s.unsqueeze(1).broadcast_to([P, F, s.shape[1]])

        s_idx = sem("s_idx")
        s_small = sem("s_small")
        s_wts = sem("s_wts")
        s_w2 = sem("s_w2")
        iota_done = sem("iota_done")
        dst_g_ready = sem("dst_g_ready")
        bc_ready = sem("bc_ready")
        bc_done = sem("bc_done")
        c_iota = sem("c_iota")
        hots_ready = sem("hots_ready")
        hist_mm = sem("hist_mm")
        stage_ready = sem("stage_ready")
        zeros_ready = sem("zeros_ready")
        node_stored = sem("node_stored")
        out_zeroed = sem("out_zeroed")
        blank_ready = sem("blank_ready")
        deg_stored = sem("deg_stored")
        deg_idx_ready = sem("deg_idx_ready")
        deg_got = sem("deg_got")
        node_row_ready = sem("node_row_ready")
        node_scattered = sem("node_scattered")
        diag_ready = sem("diag_ready")
        same_done = sem("same_done")
        ids_ready = sem("ids_ready")
        ids_stored = sem("ids_stored")
        ids_back = sem("ids_back")
        equal_ready = sem("equal_ready")
        merged_mm = sem("merged_mm")
        merged_ready = sem("merged_ready")
        added = sem("added")
        out_s_got = [sem(f"out_s_got{i}") for i in range(GC)]
        out_d_got = sem("out_d_got")
        dense_go = sem("dense_go")
        sums_in = sem("sums_in")
        sums_used = sem("sums_used")
        ptr_ready = sem("ptr_ready")
        hist_done = sem("hist_done")
        xd_got = sem("xd_got")
        xs_got = sem("xs_got")
        node_s_got = sem("node_s_got")
        x_in = [sem(f"x_in{i}") for i in range(2)]
        dense_ready = sem("dense_ready")
        dense_stored = [sem(f"dense_stored{i}") for i in range(2)]
        dve_step = sem("dve_step")
        var_ready = sem("var_ready")
        std_ready = sem("std_ready")
        scan_done = sem("scan_done")
        carry_done = sem("carry_done")
        table_ready = sem("table_ready")
        table_stored = sem("table_stored")
        got = [sem(f"got{i}") for i in range(GC)]
        ticked = sem("ticked")
        few_zeroed = sem("few_zeroed")
        mode_ready = sem("mode_ready")
        count_ready = sem("count_ready")
        count_done = sem("count_done")
        g_step = sem("g_step")
        f_step = sem("f_step")
        g_scan = sem("g_scan")
        g_carry = sem("g_carry")
        g_table = sem("g_table")
        g_stored = sem("g_stored")
        f_seg_ready = sem("f_seg_ready")
        f_seg_put = sem("f_seg_put")
        f_pos_got = sem("f_pos_got")
        f_pos_ready = sem("f_pos_ready")
        f_first_ready = sem("f_first_ready")
        f_first_done = sem("f_first_done")
        f_x_got = sem("f_x_got")
        f_scan = sem("f_scan")
        f_carry = sem("f_carry")
        f_table = sem("f_table")
        f_stored = sem("f_stored")
        f_exit = sem("f_exit")
        a_free = sem("a_free")
        f_put = sem("f_put")
        f_back = sem("f_back")
        c_far = sem("c_far")
        g_got = [sem(f"g_got{i}") for i in range(GC)]
        f_got = [sem(f"f_got{i}") for i in range(2)]
        w1_blank = sem("w1_blank")
        w2_free = sem("w2_free")
        ea_in = sem("ea_in")
        hid_mm = sem("hid_mm")
        hid_ready = sem("hid_ready")
        wts_mm = sem("wts_mm")
        wts_ready = sem("wts_ready")
        w1_used = [sem(f"w1_used{i}") for i in range(2)]
        w2_used = [sem(f"w2_used{i}") for i in range(2)]
        l1_tanh = sem("l1_tanh")
        wts_blank = sem("wts_blank")
        x3_ready = sem("x3_ready")
        x3_spilled = sem("x3_spilled")
        xd_free = sem("xd_free")
        x3_back = sem("x3_back")
        lin_in = sem("lin_in")
        lin_part = sem("lin_part")
        lin_mm = sem("lin_mm")
        lin_out = sem("lin_out")
        ex_in = sem("ex_in")
        ex_out = sem("ex_out")
        res_ready = sem("res_ready")
        res_stored = sem("res_stored")

        x_v = x.rearrange("(p c r) f -> p c (r f)", p=NP, c=ND)
        out_v = out.rearrange("(p c r) f -> p c (r f)", p=NP, c=ND)
        agg_v = agg_tab.rearrange("(p k) f -> p (k f)", p=P)
        sum_v = out_tab[0:N, :].rearrange("(p c r) f -> p c (r f)", p=NP, c=ND)
        node_v = deg_tab.rearrange("(p c r) w -> p c (r w)", p=NP, c=ND)
        DX = [B[0:NP, u * RC * F:(u + 1) * RC * F] for u in range(2)]
        DN = [B[0:NP, 2 * RC * F + u * RC:2 * RC * F + (u + 1) * RC] for u in range(2)]
        DS = A[0:NP, 0:RC * F]
        DQ = A[0:NP, RC * F:2 * RC * F]

        block = ctx.enter_context(nc.Block())

        @block.sync
        def _(sp):
            sp.dma_start(dst_i, dst_ext).then_inc(s_idx, 16)
            sp.dma_start(src_i, src_idx).then_inc(s_idx, 16)
            sp.dma_start(c_bias[:], gat_bias.unsqueeze(0).broadcast_to([P, F])).then_inc(s_small, 16)
            sp.dma_start(c_attn[:], attn.unsqueeze(0).broadcast_to([P, F])).then_inc(s_small, 16)
            sp.dma_start(lam_c, lam.unsqueeze(0).broadcast_to([P, 1])).then_inc(s_small, 16)
            for i in range(4):
                for c, v in ((cb, cheb_b), (bs_c, bsrc), (bd_c, bdst)):
                    sp.dma_start(c[F * i:F * (i + 1), :], v.unsqueeze(1)).then_inc(s_small, 16)
            sp.wait_ge(w1_blank, 1)
            sp.dma_start(w1_sb[:, 0:H], w1cat).then_inc(s_small, 16)
            sp.dma_start(ewt[:], ew).then_inc(s_small, 16)
            sp.dma_start(r3[:], ea3).then_inc(s_small, 16)
            sp.wait_ge(blank_ready, 2)
            sp.dma_start(node_tab.rearrange("(p c) w -> p (c w)", p=NP),
                         blank.rearrange("p c w -> p (c w)")).then_inc(node_stored, 16)
            sp.wait_ge(zeros_ready, 1)
            sp.dma_start(out_tab[0:N, :].rearrange("(p a r) f -> p a (r f)", p=NP, a=25),
                         zeros[0:NP, :].unsqueeze(1).broadcast_to([NP, 25, 1024])).then_inc(out_zeroed, 16)
            sp.dma_start(out_tab[N:N + 2 * P, :].rearrange("(p r) f -> p (r f)", r=2), zeros[:, 0:2 * F]).then_inc(out_zeroed, 16)
            sp.dma_start(few_pos.rearrange("(p k) o -> p (k o)", p=P), zeros[:, 0:K]).then_inc(few_zeroed, 16)
            sp.dma_start(agg_tab.rearrange("(p a r) f -> p a (r f)", p=P, a=7),
                         zeros[:, 0:KF // 7].unsqueeze(1).broadcast_to([P, 7, KF // 7])).then_inc(few_zeroed, 16)
            sp.wait_ge(stage_ready, 1)
            sp.dma_start(deg_tab.rearrange("(p c) w -> p (c w)", p=NP), stage).then_inc(deg_stored, 16)
            def store_table(r):
                sp.wait_ge(table_ready, r + 1)
                sp.dma_start(agg_v, A[:]).then_inc(table_stored, 16)

            sp.wait_ge(ids_ready, 1)
            sp.dma_start(ids_tab, ids).then_inc(ids_stored, 16)
            sp.wait_ge(mode_ready, 1)
            few = sp.value_load(flag[0:1, 0:1], min_val=0, max_val=1)
            with sp.If(few > 0):
                with sp.Fori(0, L0_ROUNDS - 1) as i:
                    sp.wait_ge(f_table, i + 1)
                    sp.dma_start(few_tab.rearrange("(p k) f -> p (k f)", p=P), few_row).then_inc(f_stored, 16)
                sp.wait_ge(f_put, 16 * KC)
                sp.dma_start(G[:], agg_v).then_inc(f_back, 16)
            with sp.Else():
                with sp.Fori(0, L0_ROUNDS - 1) as i:
                    sp.wait_ge(g_table, i + 1)
                    sp.dma_start(agg_v, A[:]).then_inc(g_stored, 16)
                store_table(0)
            sp.wait_ge(w2_free, 1)
            sp.dma_start(w2_sb[0:H // 2, 0:W1C], fc1_w2).then_inc(s_w2, 16)
            sp.dma_start(w2_sb[H // 2:H, W1C:WC], fc2_w2).then_inc(s_w2, 16)
            sp.dma_start(ea, ea10_t[:, 0:T1 * P]).then_inc(ea_in, 16)
            with sp.Fori(0, N1 - 1) as n:
                sp.wait_ge(hid_mm, n + 1)
                sp.dma_start(ea, ea10_t[:, bass.ds(n * (T1 * P) + T1 * P, T1 * P)]).then_inc(ea_in, 16)
            store_table(1)
            sp.wait_ge(wts_blank, 1)
            for q in range(4):
                sl = slice(F * q, F * (q + 1))
                for i in range(3):
                    sp.dma_start(BD[i][sl, sl], cheb_wt[F * i:F * (i + 1), :]).then_inc(s_wts, 16)
                sp.dma_start(BD[3][sl, sl], wsrc_t).then_inc(s_wts, 16)
                sp.dma_start(BD[4][sl, sl], wdst_t).then_inc(s_wts, 16)
            sp.wait_ge(ids_stored, 16)
            sp.dma_start(ids, ids_tab).then_inc(ids_back, 16)

            def load_dense(t):
                u = t % 2
                sp.dma_start(DX[u], x_v[:, t, :]).then_inc(x_in[u], 16)
                sp.dma_start(DN[u], node_v[:, t, :]).then_inc(x_in[u], 16)

            def dense_span(w):
                sp.wait_ge(dense_go, w + 1)
                t0, t1 = SPANS[w]
                for t in range(t0, min(t0 + 2, t1)):
                    load_dense(t)
                for t in range(t0, t1):
                    if t > t0:
                        sp.wait_ge(sums_used, t)
                    sp.dma_start(DS, sum_v[:, t, :]).then_inc(sums_in, 16)
                    if t > t0:
                        sp.wait_ge(dense_ready, t)
                        sp.dma_start(out_v[:, t - 1, :], DX[(t - 1) % 2]).then_inc(dense_stored[(t - 1) % 2], 16)
                        if t + 1 < t1:
                            sp.wait_ge(dense_stored[(t - 1) % 2], 16 * ((t - 1) // 2 + 1))
                            load_dense(t + 1)
                sp.wait_ge(dense_ready, t1)
                sp.dma_start(out_v[:, t1 - 1, :], DX[(t1 - 1) % 2]).then_inc(dense_stored[(t1 - 1) % 2], 16)

            sp.wait_ge(added, 16 * K)
            dense_span(0)
            sp.wait_ge(x3_ready, 1)
            sp.dma_start(x3_tab, XD[:]).then_inc(x3_spilled, 16)
            for r in range(4):
                store_table(2 + r)
                if 1 + r < len(SPANS):
                    dense_span(1 + r)
            sp.wait_ge(xd_free, 1)
            sp.dma_start(XD[:], x3_tab).then_inc(x3_back, 16)
            sp.wait_ge(res_stored, 16 * K)
            for u in range(2):
                sp.wait_ge(dense_stored[u], 16 * (ND // 2))

        @block.gpsimd
        def _(pool):
            for j, (sm, n) in enumerate(((hist_mm, 2), (hid_ready, 1), (wts_ready, 1), (ticked, 1),
                                         (w1_used[0], 1), (w1_used[1], 1), (w2_used[0], 1), (w2_used[1], 1))):
                nc.gpsimd.memset(tick[:, j:j + 1], 0.0).then_inc(sm, n)
            nc.gpsimd.memset(blank[:, :, 0], float(NONE)).then_inc(blank_ready, 1)
            nc.gpsimd.memset(blank[:, :, 1], 0.0).then_inc(blank_ready, 1)
            nc.gpsimd.memset(ident[:], 1.0).then_inc(iota_done, 1)
            nc.gpsimd.iota(iota_i, [[1, RN]], base=0, channel_multiplier=0).then_inc(c_iota, 1)
            nc.gpsimd.iota(iota_q, [[1, P]], base=0, channel_multiplier=0).then_inc(c_iota, 1)
            nc.gpsimd.iota(node_row[:, :, 0].bitcast(i32), [[1, K]], base=0, channel_multiplier=K).then_inc(c_iota, 1)
            nc.gpsimd.iota(f_place.bitcast(i32), [[1, KC]], base=1, channel_multiplier=KC).then_inc(c_iota, 1)
            nc.gpsimd.memset(MF, 1.0).then_inc(c_far, 1)
            nc.gpsimd.iota(spare.bitcast(i32), [[1, 1]], base=N, channel_multiplier=1).then_inc(c_iota, 1)
            nc.gpsimd.memset(zeros, 0.0).then_inc(zeros_ready, 1)
            nc.gpsimd.memset(ones[:], 1.0).then_inc(iota_done, 1)
            nc.gpsimd.memset(M[:], 1.0).then_inc(iota_done, 1)
            nc.gpsimd.memset(MT[:], 1.0).then_inc(iota_done, 1)
            pool.wait_ge(iota_done, 4)
            nc.gpsimd.affine_select(ident[:], ident[:], [[-1, P]], ALU.is_equal, 0.0, base=0,
                                    channel_multiplier=1).then_inc(iota_done, 1)
            nc.gpsimd.affine_select(M[:], M[:], [[1, P]], ALU.is_gt, 0.0, base=0,
                                    channel_multiplier=-1).then_inc(iota_done, 1)
            pool.wait_ge(c_far, 1)
            nc.gpsimd.affine_select(MF, MF, [[1, P]], ALU.is_gt, 0.0, base=0, channel_multiplier=-1).then_inc(c_far, 1)
            nc.gpsimd.affine_select(MT[:], MT[:], [[-1, P]], ALU.is_gt, 0.0, base=0,
                                    channel_multiplier=1).then_inc(iota_done, 1)

            def gather(dst, table, idx, bound, k, w=F):
                return nc.gpsimd.indirect_dma_start(dst[:, k * w:(k + 1) * w], None, table,
                                                    bass.IndirectOffsetOnAxis(idx[:, k:k + 1], 0),
                                                    bounds_check=bound, oob_is_err=False)

            def scatter(table, src, idx, k, w=F):
                return nc.gpsimd.indirect_dma_start(table, bass.IndirectOffsetOnAxis(idx[:, k:k + 1], 0),
                                                    src[:, k * w:(k + 1) * w], None, bounds_check=N - 1,
                                                    oob_is_err=False)

            pool.wait_ge(node_stored, 16)
            pool.wait_ge(node_row_ready, 1)
            for k in range(K):
                scatter(node_tab, U[:, 400:400 + 2 * K], idx_last, k, 2).then_inc(node_scattered, 16)
            pool.wait_ge(node_scattered, 16 * K)
            pool.wait_ge(dst_g_ready, 2)
            for k in range(K):
                gather(node_s, node_tab, src_g, N - 1, k, 2).then_inc(node_s_got, 16)
            for k in range(K):
                gather(XD, x, dst_g, N - 1, k).then_inc(xd_got, 16)
            for k in range(XS_FIRST):
                gather(XS, x, src_g, N - 1, k).then_inc(xs_got, 16)
            pool.wait_ge(ptr_ready, 1)

            def gather_round(r, ticks, into=G):
                pool.wait_ge(ticked, r + ticks)
                pool.wait_ge(table_stored, r * 16 + 16)
                nc.gpsimd.tensor_tensor(tick[:, 8:9], ident[:, 0:1], ident[:, 0:1], ALU.add).then_inc(ticked, 1)
                for k in range(K):
                    gather(into, agg_tab, ptr, EP - 1, k).then_inc(got[k // KG], 16)

            pool.wait_ge(mode_ready, 1)
            few = pool.value_load(flag[0:1, 0:1], min_val=0, max_val=1)
            with pool.If(few > 0):
                pool.wait_ge(few_zeroed, 32)
                pool.wait_ge(f_seg_ready, 1)
                for r in range(KC):
                    nc.gpsimd.indirect_dma_start(few_pos, bass.IndirectOffsetOnAxis(f_seg.bitcast(i32)[:, r:r + 1], 0),
                                                 f_place[:, r:r + 1], None, bounds_check=EP - 1,
                                                 oob_is_err=False).then_inc(f_seg_put, 16)
                for r in range(KC):
                    gather(few_g, x, f_src.bitcast(i32), N - 1, r).then_inc(f_x_got, 16)
                pool.wait_ge(f_seg_put, 16 * KC)
                for r in range(KC):
                    gather(f_pos, few_pos, f_ptr.bitcast(i32), EP - 1, r, 1).then_inc(f_pos_got, 16)
                pool.wait_ge(f_pos_ready, 1)
                for i in range(L0_ROUNDS - 1):
                    pool.wait_ge(f_stored, i * 16 + 16)
                    for r in range(KC):
                        gather(few_g, few_tab, f_pos.bitcast(i32), EC - 1, r).then_inc(f_got[2 * r // KC], 16)
                    for k in range(XS_FIRST + XS_FILL * i, min(K, XS_FIRST + XS_FILL * (i + 1))):
                        gather(XS, x, src_g, N - 1, k).then_inc(xs_got, 16)
                pool.wait_ge(ticked, 1)
                nc.gpsimd.memset(tick[:, 8:9], 0.0).then_inc(ticked, L0_ROUNDS - 1)
                pool.wait_ge(f_exit, 1)
                for r in range(KC):
                    nc.gpsimd.indirect_dma_start(agg_tab, bass.IndirectOffsetOnAxis(f_seg.bitcast(i32)[:, r:r + 1], 0),
                                                 few_row[:, r * F:(r + 1) * F], None, bounds_check=EP - 1,
                                                 oob_is_err=False).then_inc(f_put, 16)
                pool.wait_ge(f_put, 16 * KC)
                nc.gpsimd.memset(tick[:, 9:10], 0.0).then_inc(table_stored, 16)
                nc.gpsimd.memset(tick[:, 10:11], 0.0).then_inc(a_free, 1)
            with pool.Else():
                for k in range(XS_FIRST, K):
                    gather(XS, x, src_g, N - 1, k).then_inc(xs_got, 16)
                with pool.Fori(0, L0_ROUNDS - 1) as i:
                    pool.wait_ge(ticked, i + 1)
                    pool.wait_ge(g_stored, i * 16 + 16)
                    nc.gpsimd.tensor_tensor(tick[:, 8:9], ident[:, 0:1], ident[:, 0:1], ALU.add).then_inc(ticked, 1)
                    for k in range(K):
                        gather(G, agg_tab, ptr, EP - 1, k).then_inc(g_got[k // KG], 16)
            pool.wait_ge(a_free, 1)
            gather_round(0, L0_ROUNDS, into=A)
            pool.wait_ge(deg_stored, 16)
            pool.wait_ge(deg_idx_ready, 2)
            for n2, idx in ((n2d, s1), (n2s, s2)):
                for k in range(K):
                    gather(n2, deg_tab, idx[:].bitcast(i32), N - 1, k, 1).then_inc(deg_got, 16)
            pool.wait_ge(table_stored, 32)
            pool.wait_ge(ids_back, 16)
            pool.wait_ge(out_zeroed, 32)
            for k in range(0, K, 2):
                pool.wait_ge(merged_ready, k // 2 + 1)
                if k:
                    pool.wait_ge(added, 16 * k)
                for c in (k, k + 1):
                    nc.gpsimd.indirect_dma_start(out_tab, bass.IndirectOffsetOnAxis(add_to[:, c:c + 1], 0),
                                                 C[:, c * F:(c + 1) * F], None, bounds_check=N + 2 * P - 1,
                                                 oob_is_err=True, compute_op=ALU.add).then_inc(added, 16)
                for c in (k, k + 1):
                    gather(G, agg_tab, ptr, EP - 1, c).then_inc(got[c // KG], 16)
            pool.wait_ge(added, 16 * K)
            for k in range(K):
                gather(C, out_tab, dst_g, N - 1, k).then_inc(out_d_got, 16)
            pool.wait_ge(dense_go, 1)
            for k in range(K):
                gather(G, out_tab, src_g, N - 1, k).then_inc(out_s_got[k // KG], 16)
            with pool.Fori(2, 6) as r:
                gather_round(r, L0_ROUNDS - 1)
            for u in range(2):
                pool.wait_ge(dense_stored[u], 16 * (ND // 2))
            for k in range(K):
                if k % KG == 0:
                    pool.wait_ge(res_ready, k // KG + 1)
                scatter(out, A, idx_last, k).then_inc(res_stored, 16)

        @block.tensor
        def _(pe):
            pe.wait_ge(iota_done, 7)
            for t in range(2):
                pe.wait_ge(bc_ready, t + 1)
                nc.tensor.matmul(psC[:, P * t:P * (t + 1)], bcm, ident[:], start=True, stop=True).then_inc(bc_done, 1)

            def carry(q, src, matrix, width=F):
                pe.wait_ge(scan_done, q + 1)
                rhs = fm(src)[:, :, K - 1] if matrix is M else fm(src)[:, :, 0]
                nc.tensor.matmul(psC[:, 0:F], matrix[:], rhs, start=True, stop=True).then_inc(carry_done, 1)

            def carry1(q, src, lhs):
                pe.wait_ge(scan_done, q + 1)
                nc.tensor.matmul(psC[:, 0:src.shape[1]], lhs, src, start=True, stop=True).then_inc(carry_done, 1)

            carry1(0, s1[:, K - 1:K], M[:])
            carry1(1, s1[:, 0:1], MT[:])
            pe.wait_ge(zeros_ready, 1)
            zb = zeros.bitcast(bf16)
            for o, w in ((0, 512), (512, RN - 512)):
                nc.tensor.matmul(psW[:, 0, o:o + w], zb[:, 0:P], zb[:, 0:w], start=True, stop=False,
                                 skip_group_check=True)
            with pe.Fori(0, K // 2) as i:
                for u in range(2):
                    pe.wait_ge(hots_ready, i * 2 + u + 1)
                    nc.tensor.matmul(psW[:, 0, 0:512], hot_p[u][:, 0:P], hot_c[u][:, 0:512], start=False,
                                     stop=False, skip_group_check=True)
                    nc.tensor.matmul(psW[:, 0, 512:RN], hot_p[u][:, 0:P], hot_c[u][:, 512:RN], start=False,
                                     stop=False, skip_group_check=True).then_inc(hist_mm, 1)
            for o, w in ((0, 512), (512, RN - 512)):
                mm = nc.tensor.matmul(psW[:, 0, o:o + w], zb[:, 0:P], zb[:, 0:w], start=False, stop=True,
                                      skip_group_check=True)
            mm.then_inc(hist_done, 1)
            pe.wait_ge(iota_done, 7)
            def sources(i):
                pe.wait_ge(diag_ready, i)
                nc.tensor.matmul(psC[:, 0:P], ones[:], diag[:], start=True, stop=True)
                nc.tensor.matmul(psC[:, P:2 * P], ones[:], diag_odd, start=True, stop=True).then_inc(same_done, 1)

            with pe.Fori(0, K // 2) as i:
                sources(i + 1)
            pe.wait_ge(count_ready, 1)
            nc.tensor.matmul(psC[0:1, 0:P], f_one[:, 0:1], ident[:], start=True, stop=True).then_inc(count_done, 1)
            pe.wait_ge(mode_ready, 1)
            few = pe.value_load(flag[0:1, 0:1], min_val=0, max_val=1)
            with pe.If(few > 0):
                pe.wait_ge(f_first_ready, 1)
                nc.tensor.matmul(psC[:, 0:P], bcm, ident[:], start=True, stop=True).then_inc(f_first_done, 1)
                with pe.Fori(0, L0_ROUNDS - 1) as i:
                    pe.wait_ge(f_scan, i + 1)
                    nc.tensor.matmul(psC[:, 0:F], MF, few_acc.rearrange("p (f k) -> p f k", k=KC)[:, :, KC - 1],
                                     start=True, stop=True).then_inc(f_carry, 1)
                pe.wait_ge(scan_done, 3)
                nc.tensor.matmul(psC[:, 0:F], MF, few_acc.rearrange("p (f k) -> p f k", k=KC)[:, :, KC - 1],
                                 start=True, stop=True).then_inc(carry_done, 1)
            with pe.Else():
                with pe.Fori(0, L0_ROUNDS - 1) as i:
                    pe.wait_ge(g_scan, i + 1)
                    nc.tensor.matmul(psC[:, 0:F], M[:], fm(B)[:, :, K - 1], start=True, stop=True).then_inc(g_carry, 1)
                carry(2, B, M)
            carry(3, B, MT)
            pe.wait_ge(s_small, 16 * 18)
            pe.wait_ge(s_w2, 32)
            with pe.Fori(0, N1 // 2) as i:
                for u in range(2):
                    n = i * 2 + u
                    pe.wait_ge(ea_in, i * 32 + 16 * (u + 1))
                    pe.wait_ge(hid_ready, n + 1)
                    nc.tensor.matmul(psH[0:2 * H, 0:512], w1_sb[:], ea[:, 0:512], start=True, stop=True)
                    nc.tensor.matmul(psH[0:2 * H, 512:T1 * P], w1_sb[:], ea[:, 512:T1 * P],
                                     start=True, stop=True).then_inc(hid_mm, 1)
                    pe.wait_ge(hid_ready, n + 2)
                    for j in range(2 * T1):
                        m = i * (4 * T1) + (u * 2 * T1 + j)
                        t, part = j % T1, (slice(0, W1C), slice(W1C, WC))[j // T1]
                        if (u, j) == (0, 0):
                            pe.wait_ge(wts_ready, m + 1)
                        elif (u, j) >= (0, 4):
                            pe.wait_ge(wts_ready, m - 2)
                        nc.tensor.matmul(bank((u * 2 * T1 + j) % 4)[:, 0:part.stop - part.start],
                                         hid[:, t * P:(t + 1) * P], w2_sb[:, part],
                                         start=True, stop=True).then_inc(wts_mm, 1)
            carry(4, C, M)
            carry(5, C, MT)
            def merge(i):
                pe.wait_ge(equal_ready, i + 1)
                rows = [A[:, bass.ds(i * (2 * F) + F * u, F)] for u in range(2)]
                nc.tensor.matmul(psH[:, 0:F], B[:, 0:P], rows[0], start=True, stop=True)
                nc.tensor.matmul(psH[:, F:2 * F], B[:, P:2 * P], rows[0], start=True, stop=False)
                nc.tensor.matmul(psH[:, F:2 * F], B[:, 2 * P:3 * P], rows[1], start=False,
                                 stop=True).then_inc(merged_mm, 1)

            sources(K // 2 + 1)
            with pe.Fori(0, K // 2 - 1) as i:
                merge(i)
                sources(i + (K // 2 + 2))
            merge(K // 2 - 1)

            taken = [0]

            def linear(pairs, chunks=range(LC)):
                for c in chunks:
                    g = taken[0]
                    if g >= 4:
                        pe.wait_ge(lin_out, g - 3)
                    o = psW[:, (g // 2) % 2, 512 * (g % 2):512 * (g % 2) + LW]
                    for i, (t, w) in enumerate(pairs):
                        mm = nc.tensor.matmul(o, w, t[:, c * LW:(c + 1) * LW], start=(i == 0),
                                              stop=(i == len(pairs) - 1))
                    mm.then_inc(lin_mm, 1)
                    taken[0] += 1

            for layer in range(2):
                q = 6 + 2 * layer
                carry(q, B, M)
                pe.wait_ge(lin_in, 3 * layer + 1)
                linear([(C, Wa), (A, Wb)])
                carry(q + 1, C, M)
                pe.wait_ge(lin_in, 3 * layer + 2)
                linear([(C, Wa), (XS, Wb)])
                pe.wait_ge(lin_in, 3 * layer + 3)
                linear([(C, Wc), (XD, ident[:])])
                if layer == 1:
                    pe.wait_ge(lin_out, taken[0])
                    linear([(B, BD[4])])
                    carry(10, XD, MT)
                for g in range(GC):
                    pe.wait_ge(lin_part, layer * GC + g + 1)
                    cc = range(LC // GC * g, LC // GC * (g + 1))
                    linear([(C, Wc), (XS, ident[:])], cc)
                    if layer == 1:
                        pe.wait_ge(lin_out, taken[0])
                        linear([(B, BD[3])], cc)
            q = 10
            carry1(q + 1, ident[:], A[:, 0:P])
            carry1(q + 2, s1[:, 0:1], MT[:])
            carry1(q + 3, s1[:, K - 1:K], M[:])
            carry(q + 4, B, M)

        @block.scalar
        def _(act):
            nstd = [0]

            def sqrt(t):
                act.wait_ge(var_ready, nstd[0] + 1)
                nc.scalar.activation(t, t, ACT.Sqrt).then_inc(std_ready, 1)
                nstd[0] += 1

            def sqrt_groups():
                for g in range(GC):
                    sqrt(s2[:, g * KG:(g + 1) * KG])

            sqrt(s2[:])
            sqrt(norms[:, 0:2, :].rearrange("p a k -> p (a k)"))
            sqrt(f_low)
            sqrt(s2[:])
            def weights(i):
                for u in range(2):
                    n = i * 2 + u
                    W = (B, C)[u][:, 0:T1 * WC].rearrange("p (t w) -> p t w", w=WC)
                    act.wait_ge(hid_mm, n + 1)
                    nc.scalar.activation(hid, psH[0:H, 0:T1 * P], ACT.Relu, scale=float(HIN) ** -0.5).then_inc(hid_ready, 1)
                    for j in range(2 * T1):
                        m = i * (4 * T1) + (u * 2 * T1 + j)
                        t, part = j % T1, (slice(0, W1C), slice(W1C, WC))[j // T1]
                        if t == 0:
                            act.wait_ge((w1_used, w2_used)[j // T1][u], i + 1)
                        act.wait_ge(wts_mm, m + 1)
                        nc.scalar.activation(W[:, t, part], bank((u * 2 * T1 + j) % 4)[:, 0:part.stop - part.start],
                                             ACT.Copy, scale=0.25 / (32.0 ** 0.5, 4.0)[j // T1]).then_inc(wts_ready, 1)
            for g0, g1 in L1_PARTS:
                w = (g1 - g0) * KG
                sqrt(s3[:, w:2 * w])
                with act.Fori(g0 * KG // (2 * T1), g1 * KG // (2 * T1)) as i:
                    weights(i)
            sqrt(norms[:, 2:4, :].rearrange("p a k -> p (a k)"))
            act.wait_ge(wts_blank, 1)
            nc.scalar.activation(row(A)[:, :, 0:8], row(A)[:, :, 0:8], ACT.Tanh)
            nc.scalar.activation(gates[:], gates[:], ACT.Tanh).then_inc(l1_tanh, 1)
            sqrt(s2[:])
            sqrt(s2[:])

            def dense_roots(w):
                for t in range(*SPANS[w]):
                    sqrt(s1[0:NP, 0:2 * RC])
                    sqrt(s1[0:NP, 0:RC])
                    sqrt(s1[0:NP, 0:RC])

            dense_roots(0)
            sqrt(s2[:])
            sqrt_groups()

            taken = [0]

            def take(dst, func, bias=None, chunks=range(LC)):
                for c in chunks:
                    g = taken[0]
                    act.wait_ge(lin_mm, g + 1)
                    o = psW[:, (g // 2) % 2, 512 * (g % 2):512 * (g % 2) + LW]
                    if bias is None:
                        nc.scalar.activation(dst[:, c * LW:(c + 1) * LW], o, func).then_inc(lin_out, 1)
                    else:
                        nc.scalar.activation(dst[:, c * LW:(c + 1) * LW], o, func, bias=bias).then_inc(lin_out, 1)
                    taken[0] += 1

            act.wait_ge(x3_spilled, 16)
            for layer in range(2):
                take(XD, ACT.Identity, cb)
                dense_roots(1 + 2 * layer)
                take(XS, ACT.Identity, cb)
                take(B, ACT.Relu)
                if layer == 0:
                    dense_roots(2)
                else:
                    take(C, ACT.Identity, bd_c)
                    dense_roots(4)
                for g in range(GC):
                    cc = range(LC // GC * g, LC // GC * (g + 1))
                    take(B, ACT.Relu, chunks=cc)
                    if layer == 1:
                        take(A, ACT.Identity, bs_c, chunks=cc)
            act.wait_ge(ex_in, 1)
            nc.scalar.activation(s2[:], s2[:], ACT.Exp).then_inc(ex_out, 1)
            sqrt_groups()

        @block.vector
        def _(dve):
            v = nc.vector
            steps = [0]
            loop = [None, 0, dve_step]

            def link(ins):
                steps[0] += 1
                ins.then_inc(loop[2], 1)
                n = steps[0]
                dve.wait_ge(loop[2], n if loop[0] is None else loop[0] * loop[1] + n)

            nstd = [0]

            def root(ins):
                ins.then_inc(var_ready, 1)
                nstd[0] += 1
                dve.wait_ge(std_ready, nstd[0])

            v.memset(w1_sb[:], 0.0).then_inc(w1_blank, 1)
            dve.wait_ge(s_idx, 32)
            v.tensor_copy(d, dst_i)
            link(v.tensor_copy(srcf, src_i))
            v.tensor_scalar(dst_g, d[:, 1:K + 1], float(N - 1), None, ALU.min).then_inc(dst_g_ready, 1)
            v.tensor_scalar(src_g, srcf, float(N - 1), None, ALU.min).then_inc(dst_g_ready, 1)
            link(v.tensor_tensor(last[:], d[:, 1:K + 1], d[:, 2:K + 2], ALU.not_equal))
            link(v.tensor_scalar(s1[:], d[:, 1:K + 1], float(-NONE), None, ALU.add))
            link(v.tensor_tensor(s1[:], s1[:], last[:], ALU.mult))
            link(v.tensor_scalar(idx_last[:], s1[:], float(NONE), None, ALU.add))
            link(v.tensor_tensor(s2[:], d[:, 1:K + 1], d[:, 0:K], ALU.is_equal))
            link(v.memset(s2[:, 0:1], 0.0))
            link(v.memset(mask_f[:], 0))
            link(v.tensor_copy(fm(mask_f), over_f_fm(s2[:])))
            link(v.tensor_scalar(m_first[:], d[:, 1:K + 1], d[:, 1:2], None, ALU.is_equal))
            link(v.tensor_scalar(m_last[:], d[:, 1:K + 1], d[:, K:K + 1], None, ALU.is_equal))

            dve.wait_ge(c_iota, 5)
            v.tensor_copy(iota_c, iota_i)
            v.tensor_copy(iota_p, iota_q)
            v.tensor_copy(node_row[:, :, 0], node_row[:, :, 0].bitcast(i32))
            link(v.tensor_copy(spare, spare.bitcast(i32)))
            dve.wait_ge(iota_done, 7)
            v.tensor_copy(bcm, d[:, 1:2].broadcast_to([P, P])).then_inc(bc_ready, 1)
            dve.wait_ge(bc_done, 1)
            v.tensor_copy(bcm, d[:, K:K + 1].broadcast_to([P, P])).then_inc(bc_ready, 1)
            dve.wait_ge(bc_done, 2)
            link(v.scalar_tensor_tensor(M[:], psC[:, 0:P], d[:, K:K + 1], M[:], ALU.is_equal, ALU.mult))
            link(v.scalar_tensor_tensor(MT[:], psC[:, P:2 * P], d[:, 1:2], MT[:], ALU.is_equal, ALU.mult))

            def fix(j, m):
                dve.wait_ge(carry_done, j + 1)
                link(v.tensor_copy(cr[:, 0:1], psC[:, 0:1]))
                link(v.scalar_tensor_tensor(s1[:], m[:], cr[:, 0:1], s1[:], ALU.mult, ALU.add))

            link(v.memset(s2[:], 1.0))
            v.tensor_tensor_scan(s1[:], mask_f[:, 0:K], s2[:], 0.0, ALU.mult, ALU.add).then_inc(scan_done, 1)
            dve.wait_ge(scan_done, 1)
            fix(0, m_first)
            v.tensor_copy(node_row[:, :, 1], s1[:]).then_inc(node_row_ready, 1)
            link(v.tensor_scalar(n3d, s1[:], 1.0, None, ALU.max))

            dve.wait_ge(s_small, 16 * 18)
            link(v.reciprocal(rm2, lam_c))
            link(v.tensor_scalar(nre, rm2, -2.0, None, ALU.mult))
            link(v.tensor_scalar(rm1, rm2, 2.0, -1.0, ALU.mult, ALU.add))
            link(v.tensor_scalar(nre2, nre, 2.0, None, ALU.mult))
            link(v.tensor_scalar(rm2, rm1, 2.0, None, ALU.mult))

            r3v = r3[:].rearrange("p (k c) -> p k c", c=3)
            q3 = C[:, 0:3 * K].rearrange("p (k c) -> p k c", c=3)
            link(v.tensor_tensor(q3, r3v, r3v, ALU.mult))
            root(v.tensor_reduce(s2[:], q3, AX, ALU.add))
            link(v.reciprocal(s2[:], s2[:]))
            link(v.tensor_tensor(r3v, r3v, s2[:].unsqueeze(2).broadcast_to([P, K, 3]), ALU.mult))

            def take_carry(q):
                dve.wait_ge(carry_done, q + 1)
                link(v.tensor_copy(cr[:], psC[:, 0:F]))

            def segment_sums(q, msg, acc, res):
                v.tensor_tensor_scan(acc[:], mask_f[:, 0:KF], msg[:], 0.0, ALU.mult, ALU.add).then_inc(scan_done, 1)
                dve.wait_ge(scan_done, q + 1)
                take_carry(q)
                for f in range(F):
                    o = v.scalar_tensor_tensor(row(res)[:, :, f], m_first[:], cr[:, f:f + 1], fm(acc)[:, f, :],
                                               ALU.mult, ALU.add)
                return o

            def spread(q, msg, acc):
                v.tensor_tensor_scan(acc[:, ::-1], mask_f[:, 1:KF + 1][:, ::-1], msg[:, ::-1], 0.0,
                                     ALU.mult, ALU.add).then_inc(scan_done, 1)
                dve.wait_ge(scan_done, q + 1)
                take_carry(q)
                for f in range(F):
                    o = v.scalar_tensor_tensor(fm(acc)[:, f, :], m_last[:], cr[:, f:f + 1], fm(acc)[:, f, :],
                                               ALU.mult, ALU.add)
                link(o)

            def group(g):
                return slice(g * KG, (g + 1) * KG), slice(g * KG * F, (g + 1) * KG * F)

            def layernorm(X, Q, ks=slice(0, K), qs=None, t=None):
                x, q = row(X)[:, ks, :], row(Q)[:, qs or ks, :]
                t1, t2 = t or (s1[:, ks], s2[:, ks])
                link(v.tensor_reduce(t1, x, AX, ALU.add))
                link(v.tensor_scalar(t1, t1, -1.0 / F, None, ALU.mult))
                link(v.tensor_tensor(x, x, over_f(t1), ALU.add))
                link(v.tensor_tensor(q, x, x, ALU.mult))
                link(v.tensor_reduce(t2, q, AX, ALU.add))
                root(v.tensor_scalar(t2, t2, 1.0 / F, EPS, ALU.mult, ALU.add))
                link(v.reciprocal(t2, t2))
                return v.tensor_tensor(x, x, over_f(t2), ALU.mult)

            def gathered(r, c=GC - 1):
                for g in range(c + 1) if c == GC - 1 else [c]:
                    dve.wait_ge(got[g], r * (16 * KG) + 16 * KG)

            link(v.tensor_tensor(s2[:], node_row[:, :, 0], last[:], ALU.mult))
            v.tensor_tensor_scan(s1[:, ::-1], mask_f[:, 1:K + 1][:, ::-1], s2[:, ::-1], 0.0,
                                 ALU.mult, ALU.add).then_inc(scan_done, 1)
            dve.wait_ge(scan_done, 2)
            fix(1, m_last)
            link(v.tensor_copy(seg_last, s1[:]))

            link(v.tensor_scalar(s3[:].bitcast(i32), srcf, 1.0 / RN, None, ALU.mult))
            link(v.tensor_copy(s2[:], s3[:].bitcast(i32)))
            link(v.scalar_tensor_tensor(s1[:], s2[:], float(-RN), srcf, ALU.mult, ALU.add))
            for test, by in ((ALU.is_lt, -1.0), (ALU.is_ge, 1.0)):
                link(v.tensor_scalar(s3[:], s1[:], 0.0 if by < 0 else float(RN), None, test))
                link(v.scalar_tensor_tensor(s2[:], s3[:], by, s2[:], ALU.mult, ALU.add))
                link(v.scalar_tensor_tensor(s1[:], s3[:], -by * RN, s1[:], ALU.mult, ALU.add))
            with dve.Fori(0, K // 2) as i:
                for u in range(2):
                    col = bass.ds(i * 2 + u, 1)
                    dve.wait_ge(hist_mm, i * 2 + u + 1)
                    v.tensor_scalar(hot_p[u][:, 0:P], iota_p[:, 0:P], s2[:, col], None, ALU.is_equal)
                    v.tensor_scalar(hot_c[u][:, 0:RN], iota_c[:, 0:RN], s1[:, col], None,
                                    ALU.is_equal).then_inc(hots_ready, 1)
            dve.wait_ge(hist_done, 1)
            v.tensor_copy(stage, psW[0:NP, 0, 0:RN]).then_inc(stage_ready, 1)

            dve.wait_ge(c_far, 2)
            def diagonals(i):
                v.tensor_scalar(diag[:], ident[:], srcf[:, bass.ds(i * 2, 1)], None, ALU.mult)
                v.tensor_scalar(diag_odd, ident[:], srcf[:, bass.ds(i * 2 + 1, 1)], None, ALU.mult).then_inc(diag_ready, 1)

            same = [B[:, P * j:P * (j + 1)] for j in range(3)]
            base = steps[0]
            with dve.Fori(0, K // 2) as i:
                loop[0], loop[1] = i, 1
                diagonals(i)
                dve.wait_ge(same_done, i + 1)
                even, odd = bass.ds(i * 2, 1), bass.ds(i * 2 + 1, 1)
                v.scalar_tensor_tensor(same[0], psC[:, 0:P], srcf[:, even], MF, ALU.is_equal, ALU.mult,
                                       accum_out=s3[:, even])
                v.scalar_tensor_tensor(same[1], psC[:, P:2 * P], srcf[:, even], ones[:], ALU.is_equal, ALU.mult,
                                       accum_out=s2[:, even])
                link(v.scalar_tensor_tensor(same[2], psC[:, P:2 * P], srcf[:, odd], MF, ALU.is_equal, ALU.mult,
                                            accum_out=s3[:, odd]))
            loop[0] = None
            steps[0] = base + K // 2
            link(v.tensor_tensor(s3[:, 0:K:2], s3[:, 0:K:2], s2[:, 0:K:2], ALU.add))
            link(v.tensor_scalar(s1[:], srcf, float(N), None, ALU.is_lt))
            link(v.scalar_tensor_tensor(s3[:], s3[:], 0.0, s1[:], ALU.is_equal, ALU.mult))
            link(v.tensor_scalar(spare_odd, spare, float(P), None, ALU.add))
            for u, row_of in enumerate((spare, spare_odd)):
                cols_u = slice(u, K, 2)
                link(v.scalar_tensor_tensor(s1[:, cols_u], srcf[:, cols_u], row_of, s3[:, cols_u], ALU.subtract,
                                            ALU.mult))
                o = v.tensor_scalar(add_to[:, cols_u], s1[:, cols_u], row_of, None, ALU.add)
            o.then_inc(ids_ready, 1)
            dve.wait_ge(ids_ready, 1)

            ns = node_s.rearrange("p (k c) -> p k c", c=2)
            dve.wait_ge(node_s_got, 16 * K)
            v.tensor_copy(ptr[:], ns[:, :, 0]).then_inc(ptr_ready, 1)
            link(v.tensor_scalar(live[:], ns[:, :, 0], float(EP), None, ALU.is_lt))
            v.tensor_reduce(f_one[:, 0:1], live[:], AX, ALU.add).then_inc(count_ready, 1)
            dve.wait_ge(count_done, 1)
            link(v.tensor_reduce(f_one[0:1, 1:2], psC[0:1, 0:P], AX, ALU.max))
            v.tensor_scalar(flag[:], f_one[0:1, 1:2], float(FEW_MAX), None, ALU.is_le).then_inc(mode_ready, 1)
            dve.wait_ge(mode_ready, 1)
            root(v.tensor_scalar(n3s, ns[:, :, 1], 1.0, None, ALU.max))
            link(v.reciprocal(norms[:, 0:2, :], norms[:, 0:2, :]))
            link(v.tensor_tensor(n3live[:], n3s, live[:], ALU.mult))
            link(v.tensor_tensor(cs1[:], n3live[:], n3live[:], ALU.mult))
            link(v.tensor_scalar(cs1[:], cs1[:], 0.9, None, ALU.mult))
            dve.wait_ge(node_stored, 16)
            dve.wait_ge(deg_stored, 16)
            dve.wait_ge(out_zeroed, 32)
            dve.wait_ge(few_zeroed, 32)

            few = dve.value_load(flag[0:1, 0:1], min_val=0, max_val=1)
            after = steps[0]
            with dve.If(few > 0):
                steps[0], loop[2] = 0, f_step
                fi, ff = f_int.bitcast(i32), f_tmp

                def packed(value, out, out_col=None):
                    link(v.tensor_tensor(s1[:], kb, value, ALU.add))
                    link(v.tensor_tensor(s1[:], s1[:], live[:], ALU.mult))
                    top()
                    link(v.tensor_copy(fi, f_key))
                    if out_col is not None:
                        link(v.tensor_scalar(f_next.bitcast(i32), fi, 15, None, ALU.arith_shift_right))
                        link(v.tensor_copy(out_col, f_next.bitcast(i32)))
                    link(v.tensor_scalar(fi, fi, PACK - 1, None, ALU.bitwise_and))
                    link(v.tensor_copy(out, fi))

                def top():
                    for j in range(KC // 8):
                        link(v.max(f_key[:, 8 * j:8 * j + 8], s1[:]))
                        if j < KC // 8 - 1:
                            link(v.match_replace(s1[:], f_key[:, 8 * j:8 * j + 8], s1[:], 0.0))

                def index(out, value, where, shift=0.0):
                    link(v.scalar_tensor_tensor(ff, value, shift - NONE, where, ALU.add, ALU.mult))
                    link(v.tensor_scalar(out.bitcast(i32), ff, float(NONE), None, ALU.add))

                kb = s2[:]
                p0 = node_row[:, 0:1, 0]
                link(v.tensor_scalar(kb, node_row[:, :, 0], p0, float(-PACK), ALU.subtract, ALU.mult))
                link(v.tensor_scalar(kb, kb, float(K * PACK), None, ALU.add))
                packed(ns[:, :, 1], f_deg)
                packed(seg_last, f_seg)
                packed(ns[:, :, 0], f_ptr, f_edge)
                link(v.tensor_scalar(f_live, f_key, 0.0, None, ALU.is_gt))
                link(v.tensor_scalar(f_edge, f_edge, -1.0, float(K), ALU.mult, ALU.add))
                link(v.tensor_scalar(f_edge, f_edge, p0, None, ALU.add))
                index(f_edge, f_edge, f_live)
                index(f_ptr, f_ptr, f_live)
                for half, op, by in ((f_low, ALU.bitwise_and, 511), (f_src, ALU.arith_shift_right, 9)):
                    link(v.tensor_scalar(s3[:].bitcast(i32), src_i, by, None, op))
                    link(v.tensor_copy(s3[:], s3[:].bitcast(i32)))
                    packed(s3[:], half)
                link(v.scalar_tensor_tensor(f_src, f_src, 512.0, f_low, ALU.mult, ALU.add))
                index(f_src, f_src, f_live)
                link(v.tensor_scalar(s1[:], d[:, 1:K + 1], 1.0, None, ALU.add))
                link(v.tensor_tensor(s1[:], s1[:], live[:], ALU.mult))
                link(v.tensor_reduce(f_one[:, 2:3], s1[:], AX, ALU.max))
                link(v.tensor_scalar(f_one[:, 2:3], f_one[:, 2:3], -1.0, None, ALU.add))
                link(v.tensor_scalar(s1[:], d[:, 1:K + 1], -1.0, float(2 * NONE), ALU.mult, ALU.add))
                link(v.tensor_tensor(s1[:], s1[:], live[:], ALU.mult))
                top()
                link(v.tensor_scalar(f_dst, f_key, -1.0, float(2 * NONE), ALU.mult, ALU.add))
                link(v.tensor_scalar(f_dst, f_dst, f_one[:, 2:3], None, ALU.min))
                link(v.tensor_scalar(f_m1, f_dst, f_dst[:, 0:1], None, ALU.is_equal))
                link(v.memset(f_same, 0.0))
                link(v.tensor_tensor(f_same[:, 1:KC], f_dst[:, 1:KC], f_dst[:, 0:KC - 1], ALU.is_equal))
                link(v.tensor_copy(few_mask.rearrange("p (f k) -> p f k", k=KC),
                                   f_same.unsqueeze(1).broadcast_to([P, F, KC])))
                dve.wait_ge(c_far, 2)
                v.tensor_copy(bcm, f_dst[:, 0:1].broadcast_to([P, P])).then_inc(f_first_ready, 1)
                dve.wait_ge(f_first_done, 1)
                link(v.scalar_tensor_tensor(MF, psC[:, 0:P], f_one[:, 2:3], MF, ALU.is_equal, ALU.mult))
                link(v.tensor_reduce(f_one[:, 3:4], MF, AX, ALU.max))
                link(v.memset(f_next, 0.0))
                link(v.tensor_copy(f_next[:, 0:KC - 1], f_live[:, 1:KC]))
                link(v.tensor_tensor(f_end[:, 0:KC - 1], f_same[:, 1:KC], f_next[:, 0:KC - 1], ALU.mult))
                link(v.memset(f_end[:, KC - 1:KC], 0.0))
                link(v.tensor_scalar(f_next, f_next, -1.0, 1.0, ALU.mult, ALU.add))
                link(v.tensor_scalar(f_next, f_next, f_one[:, 3:4], None, ALU.mult))
                link(v.tensor_tensor(f_end, f_end, f_next, ALU.max))
                link(v.tensor_scalar(f_end, f_end, -1.0, 1.0, ALU.mult, ALU.add))
                link(v.tensor_tensor(f_end, f_end, f_live, ALU.mult))
                index(f_seg, f_seg, f_end)
                link(v.tensor_copy(f_place, f_place.bitcast(i32)))
                link(v.memset(f_pos, 0.0))
                v.memset(few_g, 0.0).then_inc(f_seg_ready, 1)
                link(v.tensor_scalar(f_cs1, f_deg, 1.0, None, ALU.max))
                link(v.reciprocal(f_cs1, f_cs1))
                link(v.tensor_tensor(f_cs1, f_cs1, f_live, ALU.mult))
                link(v.tensor_scalar(f_cs1, f_cs1, 0.9, None, ALU.mult))
                link(v.memset(A[:], 0.0))
                root(v.tensor_scalar(f_low, f_deg, 1.0, None, ALU.max))
                link(v.reciprocal(f_low, f_low))
                link(v.tensor_tensor(f_low, f_low, f_live, ALU.mult))
                dve.wait_ge(f_x_got, 16 * KC)

                def f_fm(t):
                    return t.rearrange("p (f k) -> p f k", k=KC)

                def f_rt(t):
                    return t.rearrange("p (k f) -> p f k", f=F)

                link(v.tensor_tensor(f_fm(few_w), f_rt(few_g), f_low.unsqueeze(1).broadcast_to([P, F, KC]),
                                     ALU.mult))
                link(v.tensor_scalar(few_c0, few_w, 0.1, None, ALU.mult))
                dve.wait_ge(f_pos_got, 16 * KC)
                link(v.tensor_scalar(f_next, f_pos, 0.0, None, ALU.is_gt))
                index(f_pos, f_pos, f_next, -1.0)
                v.memset(few_g, 0.0).then_inc(f_pos_ready, 1)
                dve.wait_ge(f_pos_ready, 1)
                f_base, F_PASS = steps[0], 7
                with dve.Fori(0, L0_ROUNDS - 1) as i:
                    loop[0], loop[1] = i, F_PASS
                    v.tensor_tensor_scan(few_acc, few_mask, few_w, 0.0, ALU.mult, ALU.add).then_inc(f_scan, 1)
                    dve.wait_ge(f_scan, i + 1)
                    dve.wait_ge(f_carry, i + 1)
                    link(v.tensor_copy(cr[:], psC[:, 0:F]))
                    link(v.tensor_tensor(few_row.rearrange("p (k f) -> p k f", f=F),
                                         f_m1.unsqueeze(2).broadcast_to([P, KC, F]),
                                         cr[:].unsqueeze(1).broadcast_to([P, KC, F]), ALU.mult))
                    link(v.tensor_tensor(f_rt(few_row), f_rt(few_row), f_fm(few_acc), ALU.add))
                    v.tensor_copy(cr[:, 0:1], cr[:, 0:1]).then_inc(f_table, 1)
                    for h in range(2):
                        ks = slice(h * KC // 2, (h + 1) * KC // 2)
                        dve.wait_ge(f_got[h], i * (8 * KC) + 8 * KC)
                        link(v.tensor_tensor(f_fm(few_w)[:, :, ks], f_rt(few_g)[:, :, ks],
                                             f_cs1[:, ks].unsqueeze(1).broadcast_to([P, F, KC // 2]), ALU.mult))
                        link(v.tensor_tensor(f_fm(few_w)[:, :, ks], f_fm(few_w)[:, :, ks], f_fm(few_c0)[:, :, ks],
                                             ALU.add))
                assert steps[0] == f_base + F_PASS, steps[0] - f_base
                loop[0] = None
                steps[0] = f_base + F_PASS * (L0_ROUNDS - 1)
                v.tensor_tensor_scan(few_acc, few_mask, few_w, 0.0, ALU.mult, ALU.add).then_inc(scan_done, 1)
                dve.wait_ge(scan_done, 3)
                take_carry(2)
                link(v.tensor_tensor(few_row.rearrange("p (k f) -> p k f", f=F),
                                     f_m1.unsqueeze(2).broadcast_to([P, KC, F]),
                                     cr[:].unsqueeze(1).broadcast_to([P, KC, F]), ALU.mult))
                v.tensor_tensor(f_rt(few_row), f_rt(few_row), f_fm(few_acc), ALU.add).then_inc(f_exit, 1)
                dve.wait_ge(f_back, 16)
                v.tensor_copy(cr[:, 0:1], cr[:, 0:1]).then_inc(table_ready, 1)
            with dve.Else():
                steps[0], loop[2] = 0, g_step
                nstd[0] -= 1
                root(v.memset(f_low, 1.0))
                dve.wait_ge(xs_got, 16 * K)
                link(v.tensor_tensor(fm(A), row_t(XS), over_f_fm(n3live[:]), ALU.mult))
                link(v.memset(G[:], 1.0))
                link(v.tensor_scalar(C[:], A[:], 0.1, None, ALU.mult))
                base = steps[0]
                PASS = 2 + 2 * GC
                with dve.Fori(0, L0_ROUNDS - 1) as i:
                    loop[0], loop[1] = i, PASS
                    v.tensor_tensor_scan(B[:], mask_f[:, 0:KF], A[:], 0.0, ALU.mult, ALU.add).then_inc(g_scan, 1)
                    dve.wait_ge(g_scan, i + 1)
                    dve.wait_ge(g_carry, i + 1)
                    link(v.tensor_copy(cr[:], psC[:, 0:F]))
                    for f in range(F):
                        o = v.scalar_tensor_tensor(row(A)[:, :, f], m_first[:], cr[:, f:f + 1], fm(B)[:, f, :],
                                                   ALU.mult, ALU.add)
                    link(o)
                    v.tensor_copy(cr[:, 0:1], cr[:, 0:1]).then_inc(g_table, 1)
                    for c in range(GC):
                        dve.wait_ge(g_got[c], i * (16 * KG) + 16 * KG)
                        ks = slice(c * KG, (c + 1) * KG)
                        link(v.tensor_tensor(fm(A)[:, :, ks], row_t(G)[:, :, ks], over_f_fm(cs1[:, ks]), ALU.mult))
                        link(v.tensor_tensor(fm(A)[:, :, ks], fm(A)[:, :, ks], fm(C)[:, :, ks], ALU.add))
                assert steps[0] == base + PASS
                loop[0] = None
                steps[0] = base + PASS * (L0_ROUNDS - 1)
                segment_sums(2, A, B, A).then_inc(table_ready, 1)
                dve.wait_ge(table_ready, 1)
                v.tensor_copy(G[:], A[:]).then_inc(a_free, 1)
                dve.wait_ge(a_free, 1)
            steps[0], loop[2] = after, dve_step
            dve.wait_ge(table_ready, 1)
            dve.wait_ge(xd_got, 16 * K)
            link(v.tensor_tensor(s1[:], n3d, last[:], ALU.mult))
            link(v.tensor_scalar(s1[:], s1[:], 0.9, None, ALU.mult))
            link(v.tensor_tensor(fm(C), row_t(G), over_f_fm(s1[:]), ALU.mult))
            spread(3, C, B)
            link(v.scalar_tensor_tensor(row_t(XD), row_t(XD), 1.1, fm(B), ALU.mult, ALU.add))
            link(layernorm(XD, C))
            dve.wait_ge(xs_got, 16 * K)

            dve.wait_ge(ids_stored, 16)
            v.tensor_copy(s1[:].bitcast(i32), dst_g).then_inc(deg_idx_ready, 1)
            v.tensor_copy(s2[:].bitcast(i32), src_g).then_inc(deg_idx_ready, 1)
            dve.wait_ge(deg_idx_ready, 2)
            link(v.memset(U[:], 0.0))
            v.memset(w2_sb, 0.0).then_inc(w2_free, 1)
            T2 = 2 * T1
            PR = G[:, 0:T1 * 96 * 8].rearrange("p (t u w) -> p t u w", u=96, w=8)
            PF = G[:, 0:T1 * 96 * 8].rearrange("p (g u w) -> p g w u", u=16, w=8)
            P2 = G[:, 0:T1 * 64 * 8].rearrange("p (t u w) -> p t u w", u=64, w=8)
            P2F = G[:, 0:T1 * 64 * 8].rearrange("p (g u w) -> p g w u", u=8, w=8)
            S8 = sums.rearrange("p t g w -> p (t g) w")
            S6 = S8[:, 0:T2 * 6, :]
            s6 = S6.rearrange("p (t g) w -> p t g w", g=6)

            def update_sources(g0, g1):
                ks, cs = slice(g0 * KG, g1 * KG), slice(g0 * KG * F, g1 * KG * F)
                w = (g1 - g0) * KG
                for g in range(g0, g1):
                    dve.wait_ge(got[g], 16 * KG)
                link(v.scalar_tensor_tensor(row(A)[:, ks, :], row(A)[:, ks, :], 0.9, over_f(n3live[:, ks]),
                                            ALU.mult, ALU.mult))
                link(v.scalar_tensor_tensor(XS[:, cs], XS[:, cs], 1.1, A[:, cs], ALU.mult, ALU.add))
                link(layernorm(XS, G, ks, slice(0, w), (s3[:, 0:w], s3[:, w:2 * w])))

            def tensor_products(i):
                xs = row(XS)[:, bass.ds(i * T2, T2), :]
                xd = row(XD)[:, bass.ds(i * T2, T2), :]
                rr = r3v[:, bass.ds(i * T2, T2), :]
                vr = [G[:, T2 * 24 * j:T2 * 24 * (j + 1)].rearrange("p (t v c) -> p t v c", v=8, c=3) for j in range(2)]
                for j, z in enumerate((xs, xd)):
                    v.tensor_copy(in48[:, :, 8 * j:8 * j + 8], z[:, :, 0:8])
                    v.tensor_copy(in48[:, :, 32 + 8 * j:40 + 8 * j], z[:, :, 0:8])
                    o = v.tensor_tensor(vr[j], z[:, :, 8:F].rearrange("p t (v c) -> p t v c", c=3),
                                        rr.unsqueeze(2).broadcast_to([P, T2, 8, 3]), ALU.mult)
                link(o)
                for j in range(2):
                    o = v.tensor_reduce(in48[:, :, 16 + 8 * j:24 + 8 * j], vr[j], AX, ALU.add)
                link(o)
                for u in range(2):
                    W = (B, C)[u][:, 0:T1 * WC].rearrange("p (t w) -> p t w", w=WC)
                    Wm = W[:, :, 0:W1C].rearrange("p t (u w) -> p t u w", w=8)
                    ts = slice(u * T1, (u + 1) * T1)
                    dve.wait_ge(wts_ready, i * (4 * T1) + (u * 2 * T1 + T1 + 1))
                    v.tensor_tensor(PR[:, :, 0:48, :], Wm[:, :, 0:48, :],
                                    in48[:, ts, :].unsqueeze(3).broadcast_to([P, T1, 48, 8]), ALU.mult)
                    for c in range(3):
                        for j, x_u in enumerate((XS, XD)):
                            vec = row(x_u)[:, bass.ds(i * T2 + u * T1, T1), 8 + c:F:3]
                            o = v.tensor_tensor(PR[:, :, 48 + 16 * c + 8 * j:56 + 16 * c + 8 * j, :],
                                                Wm[:, :, 48 + 8 * j:56 + 8 * j, :],
                                                vec.unsqueeze(3).broadcast_to([P, T1, 8, 8]), ALU.mult)
                    o.then_inc(w1_used[u], 1)
                    dve.wait_ge(w1_used[u], i + 2)
                    link(v.tensor_reduce(S6[:, u * T1 * 6:(u + 1) * T1 * 6, :], PF, AX, ALU.add))
                for j in (0, 16, 32):
                    v.tensor_tensor(in48[:, :, j:j + 8], s6[:, :, 0, :], s6[:, :, 1, :], ALU.add)
                for c in range(3):
                    o = v.tensor_tensor(vt[:, :, c, :], s6[:, :, 2, :],
                                        rr[:, :, c:c + 1].broadcast_to([P, T2, 8]), ALU.mult)
                link(o)
                link(v.scalar_tensor_tensor(vt[:], vt[:], S3, s6[:, :, 3:6, :], ALU.mult, ALU.add))
                pv = G[:, 0:T2 * 24].rearrange("p (t c w) -> p t c w", c=3, w=8)
                link(v.tensor_tensor(pv, vt[:], rr.unsqueeze(3).broadcast_to([P, T2, 3, 8]), ALU.mult))
                for j in (8, 24):
                    o = v.tensor_reduce(in48[:, :, j:j + 8], pv.rearrange("p t c w -> p t w c"), AX, ALU.add)
                link(o)
                for u in range(2):
                    W = (B, C)[u][:, 0:T1 * WC].rearrange("p (t w) -> p t w", w=WC)
                    Wn = W[:, :, W1C:WC].rearrange("p t (u w) -> p t u w", w=8)
                    ts = slice(u * T1, (u + 1) * T1)
                    dve.wait_ge(wts_ready, i * (4 * T1) + (u * 2 * T1 + 2 * T1 + 1))
                    v.tensor_tensor(P2[:, :, 0:40, :], Wn[:, :, 0:40, :],
                                    in48[:, ts, 0:40].unsqueeze(3).broadcast_to([P, T1, 40, 8]), ALU.mult)
                    for c in range(3):
                        o = v.tensor_tensor(P2[:, :, 40 + 8 * c:48 + 8 * c, :], Wn[:, :, 40:48, :],
                                            vt[:, ts, c, :].unsqueeze(3).broadcast_to([P, T1, 8, 8]), ALU.mult)
                    o.then_inc(w2_used[u], 1)
                    dve.wait_ge(w2_used[u], i + 2)
                    link(v.tensor_reduce(S8[:, u * T1 * 8:(u + 1) * T1 * 8, :], P2F, AX, ALU.add))
                a = row(A)[:, bass.ds(i * T2, T2), :]
                v.tensor_tensor(a[:, :, 0:8], sums[:, :, 0, :], sums[:, :, 1, :], ALU.add)
                v.tensor_tensor(gates[:, bass.ds(i * T2, T2), :], sums[:, :, 2, :], sums[:, :, 3, :], ALU.add)
                for c in range(3):
                    o = v.tensor_tensor(vt[:, :, c, :], sums[:, :, 4, :],
                                        rr[:, :, c:c + 1].broadcast_to([P, T2, 8]), ALU.mult)
                link(o)
                link(v.scalar_tensor_tensor(vt[:], vt[:], S3, sums[:, :, 5:8, :], ALU.mult, ALU.add))
                link(v.tensor_copy(a[:, :, 8:F].rearrange("p t (w c) -> p t c w", c=3), vt[:]))

            for g0, g1 in L1_PARTS:
                update_sources(g0, g1)
                base = steps[0]
                i0, i1 = g0 * KG // T2, g1 * KG // T2
                with dve.Fori(i0, i1) as i:
                    loop[0], loop[1] = i, L1_LINKS
                    steps[0] = base - i0 * L1_LINKS
                    tensor_products(i)
                    assert steps[0] == base - i0 * L1_LINKS + L1_LINKS
                loop[0] = None
                steps[0] = base + L1_LINKS * (i1 - i0)
            dve.wait_ge(deg_got, 2 * 16 * K)
            root(v.tensor_scalar(norms[:, 2:4, :], norms[:, 2:4, :], 1.0, None, ALU.add))
            link(v.reciprocal(norms[:, 2:4, :], norms[:, 2:4, :]))
            v.memset(U[:], 0.0).then_inc(wts_blank, 1)
            dve.wait_ge(l1_tanh, 1)
            av = row(A)[:, :, 8:F].rearrange("p k (w c) -> p k w c", c=3)
            link(v.tensor_tensor(av, av, gates[:].unsqueeze(3).broadcast_to([P, K, 8, 3]), ALU.mult))
            link(v.tensor_tensor(fm(B), row_t(A), over_f_fm(ewt[:]), ALU.mult))
            segment_sums(4, B, C, A).then_inc(table_ready, 1)
            dve.wait_ge(table_ready, 2)
            link(v.tensor_tensor(fm(B), row_t(A), over_f_fm(last[:]), ALU.mult))
            spread(5, B, C)
            link(v.tensor_tensor(row_t(XD), row_t(XD), fm(C), ALU.add))
            link(layernorm(XD, B))

            dve.wait_ge(ids_back, 16)
            link(v.tensor_scalar(s1[:], srcf, float(N), None, ALU.is_lt))
            link(v.tensor_tensor(s1[:], s1[:], n2d, ALU.mult))
            dve.wait_ge(table_stored, 32)
            link(v.tensor_tensor(row(A), row(XD), over_f(s1[:]), ALU.mult))
            def equal(i, more):
                even, odd = srcf[:, bass.ds(i * 2, 1)], srcf[:, bass.ds(i * 2 + 1, 1)]
                dve.wait_ge(same_done, i + (K // 2 + 1))
                v.tensor_scalar(same[0], psC[:, 0:P], even, None, ALU.is_equal)
                v.tensor_scalar(same[1], psC[:, P:2 * P], even, None, ALU.is_equal)
                v.tensor_scalar(same[2], psC[:, P:2 * P], odd, None, ALU.is_equal).then_inc(equal_ready, 1)
                if more:
                    diagonals(i + 1)
                dve.wait_ge(merged_mm, i + 1)
                v.tensor_copy(C[:, bass.ds(i * (2 * F), 2 * F)], psH[:, 0:2 * F]).then_inc(merged_ready, 1)

            diagonals(0)
            with dve.Fori(0, K // 2 - 1) as i:
                equal(i, True)
            equal(K // 2 - 1, False)
            gathered(1)
            link(v.tensor_tensor(row(B), row(G), over_f(live[:]), ALU.mult))
            link(v.tensor_tensor(XS[:], XS[:], B[:], ALU.add))
            link(layernorm(XS, B))
            Q = DQ.rearrange("p (r f) -> p r f", f=F)
            S = DS.rearrange("p (r f) -> p r f", f=F)
            z1, z4 = s1[0:NP, 0:RC], s1[0:NP, RC:2 * RC]
            z2, z3 = s2[0:NP, 0:RC], s3[0:NP, 0:RC]

            def wide(z):
                return z.unsqueeze(2).broadcast_to([NP, RC, F])

            def dense_span(w):
                v.tensor_copy(cr[:, 0:1], c_bias[:, 0:1]).then_inc(dense_go, 1)
                for t in range(*SPANS[w]):
                    X = DX[t % 2].rearrange("p (r f) -> p r f", f=F)
                    deg = DN[t % 2]

                    def centre():
                        link(v.tensor_reduce(z1, X, AX, ALU.add))
                        link(v.tensor_scalar(z1, z1, -1.0 / F, None, ALU.mult))
                        link(v.tensor_tensor(X, X, wide(z1), ALU.add))

                    def squares():
                        link(v.tensor_tensor(Q, X, X, ALU.mult))
                        link(v.tensor_reduce(z2, Q, AX, ALU.add))

                    dve.wait_ge(x_in[t % 2], 32 * (t // 2 + 1))
                    centre()
                    squares()
                    link(v.tensor_scalar(z2, z2, 1.0 / F, None, ALU.mult))
                    link(v.tensor_scalar(z1, z2, 1.21, EPS, ALU.mult, ALU.add))
                    link(v.reciprocal(z1, z1))
                    link(v.tensor_scalar(z1, z1, 1.21, None, ALU.mult))
                    link(v.tensor_tensor(z2, z2, z1, ALU.mult))
                    link(v.tensor_scalar(z3, z2, EPS, None, ALU.add))
                    link(v.reciprocal(z3, z3))
                    link(v.tensor_tensor(z1, z1, z3, ALU.mult))
                    link(v.tensor_scalar(z4, deg, 1.0, None, ALU.add))
                    link(v.reciprocal(z4, z4))
                    root(v.tensor_scalar(z3, z4, 1.0, None, ALU.add))
                    link(v.tensor_tensor(z1, z1, z3, ALU.mult))
                    link(v.tensor_tensor(X, X, wide(z1), ALU.mult))
                    dve.wait_ge(sums_in, 16 * (t + 1))
                    link(v.tensor_tensor(S, S, wide(z4), ALU.mult))
                    v.tensor_tensor(X, X, S, ALU.add).then_inc(sums_used, 1)
                    dve.wait_ge(sums_used, t + 1)
                    for layer in (2, 3):
                        centre()
                        squares()
                        root(v.tensor_scalar(z1, z2, 1.0 / F, EPS, ALU.mult, ALU.add))
                        link(v.reciprocal(z1, z1))
                        o = v.tensor_tensor(X, X, wide(z1), ALU.mult)
                        if layer == 2:
                            link(o)
                            link(v.tensor_tensor(X, X, c_bias[0:NP, :].unsqueeze(1).broadcast_to([NP, RC, F]), ALU.add))
                    o.then_inc(dense_ready, 1)
                    dve.wait_ge(dense_ready, t + 1)

            def dense_out(w):
                t1 = SPANS[w][1]
                for u in range(2):
                    dve.wait_ge(dense_stored[u], 16 * ((t1 + 1 - u) // 2))

            def own_row(X, T, own, n, ks, cs):
                link(v.tensor_tensor(row(T)[:, ks, :], row(X)[:, ks, :], over_f(n[:, ks]), ALU.mult))
                link(v.tensor_tensor(T[:, cs], T[:, cs], own[:, cs], ALU.add))
                link(v.tensor_tensor(row(T)[:, ks, :], row(T)[:, ks, :], over_f(n[:, ks]), ALU.mult))
                link(v.tensor_tensor(X[:, cs], X[:, cs], T[:, cs], ALU.add))
                return layernorm(X, T, ks)

            dense_span(0)
            dense_out(0)
            dve.wait_ge(out_d_got, 16 * K)
            own_row(XD, B, C, n2d, slice(0, K), slice(0, KF)).then_inc(x3_ready, 1)
            dve.wait_ge(x3_ready, 1)
            for g in range(GC):
                ks, cs = group(g)
                dve.wait_ge(out_s_got[g], 16 * KG)
                link(own_row(XS, B, G, n2s, ks, cs))
                link(v.tensor_tensor(fm(A)[:, :, ks], row_t(XS)[:, :, ks], over_f_fm(n3s[:, ks]), ALU.mult))

            dve.wait_ge(s_wts, 16 * 20)
            link(v.tensor_tensor(Wa, BD[0], BD[2], ALU.subtract))
            link(v.scalar_tensor_tensor(Wb, BD[2], rm2, BD[1], ALU.mult, ALU.add))
            link(v.tensor_scalar(Wc, BD[2], nre2, None, ALU.mult))
            for layer in range(2):
                r = 2 + 2 * layer
                q = 6 + 2 * layer
                n = 4 * LC * layer
                m = 3 * layer
                segment_sums(q, A, B, A).then_inc(table_ready, 1)
                dve.wait_ge(table_ready, r + 1)
                link(v.scalar_tensor_tensor(row(B), row(A), nre, over_f(n3d), ALU.mult, ALU.mult))
                link(v.scalar_tensor_tensor(B[:], XD[:], rm1, B[:], ALU.mult, ALU.add))
                link(v.transpose(C[:], XD[:]))
                dve.wait_ge(table_stored, 16 * (r + 1))
                v.transpose(A[:], B[:]).then_inc(lin_in, 1)
                dve.wait_ge(lin_in, m + 1)
                dve.wait_ge(lin_out, n + LC)
                dense_span(1 + 2 * layer)
                dense_out(1 + 2 * layer)
                for g in range(GC):
                    ks, cs = group(g)
                    gathered(r, g)
                    link(v.scalar_tensor_tensor(row(B)[:, ks, :], row(G)[:, ks, :], nre, over_f(n3live[:, ks]),
                                                ALU.mult, ALU.mult))
                    link(v.scalar_tensor_tensor(B[:, cs], XS[:, cs], rm1, B[:, cs], ALU.mult, ALU.add))
                    link(v.tensor_tensor(fm(A)[:, :, ks], row_t(B)[:, :, ks], over_f_fm(n3s[:, ks]), ALU.mult))
                segment_sums(q + 1, A, C, A).then_inc(table_ready, 1)
                dve.wait_ge(table_ready, r + 2)
                link(v.transpose(C[:], XS[:]))
                v.transpose(XS[:], B[:]).then_inc(lin_in, 1)
                dve.wait_ge(lin_in, m + 2)
                link(v.tensor_tensor(row(B), row(A), over_f(n3d), ALU.mult))
                dve.wait_ge(lin_out, n + 2 * LC)
                v.transpose(C[:], B[:]).then_inc(lin_in, 1)
                dve.wait_ge(lin_in, m + 3)
                dve.wait_ge(lin_out, n + 3 * LC)
                if layer == 0:
                    link(v.transpose(XD[:], B[:]))
                    dve.wait_ge(table_stored, 16 * (r + 2))
                    dense_span(2)
                    dense_out(2)
                else:
                    dve.wait_ge(lin_out, n + 4 * LC)
                    link(v.transpose(XD[:], C[:]))
                    dve.wait_ge(table_stored, 16 * (r + 2))
                    link(v.tensor_tensor(fm(A), row_t(XD), over_f_fm(last[:]), ALU.mult))
                    spread(10, A, XD)
                    dense_span(4)
                    dense_out(4)
                for g in range(GC + 1):
                    if g < GC:
                        ks, cs = group(g)
                        gathered(r + 1, g)
                        link(v.tensor_tensor(row(G)[:, ks, :], row(G)[:, ks, :], over_f(n3live[:, ks]), ALU.mult))
                        v.transpose(C[:, cs], G[:, cs]).then_inc(lin_part, 1)
                    if g and layer == 0:
                        ks, cs = group(g - 1)
                        dve.wait_ge(lin_out, n + 3 * LC + LC // GC * g)
                        link(v.transpose(XS[:, cs], B[:, cs]))
                        link(v.tensor_tensor(fm(A)[:, :, ks], row_t(XS)[:, :, ks], over_f_fm(n3s[:, ks]), ALU.mult))
                    if g and layer == 1:
                        ks, cs = group(g - 1)
                        dve.wait_ge(lin_out, n + 4 * LC + 2 * (LC // GC) * g)
                        e = fm(XD)[:, :, ks]
                        link(v.transpose(XS[:, cs], A[:, cs]))
                        link(v.tensor_tensor(e, e, row_t(XS)[:, :, ks], ALU.add))
                        link(v.scalar_tensor_tensor(e, e, 0.2, e, ALU.mult, ALU.max))
                        link(v.tensor_tensor(e, e, c_attn[:].unsqueeze(2).broadcast_to([P, F, KG]), ALU.mult))
                        o = v.tensor_reduce(s3[:, ks], e.rearrange("p f k -> p k f"), AX, ALU.add)
                        if g < GC:
                            link(o)
            o.then_inc(xd_free, 1)
            dve.wait_ge(xd_free, 1)
            q = 10
            msk = mask_f[:, 0:K]
            link(v.tensor_scalar(s1[:], msk, BIG, -BIG, ALU.mult, ALU.add))
            link(v.tensor_tensor_scan(s2[:], s1[:], s3[:], -BIG, ALU.add, ALU.max))
            v.tensor_copy(A[:, 0:P], s2[:, K - 1:K].broadcast_to([P, P])).then_inc(scan_done, 1)
            link(v.tensor_scalar(A[:, P:2 * P], MT[:], BIG, -BIG, ALU.mult, ALU.add))
            dve.wait_ge(carry_done, q + 2)
            link(v.tensor_tensor(A[:, P:2 * P], A[:, P:2 * P], psC[:, 0:P], ALU.add))
            link(v.tensor_reduce(cr[:, 0:1], A[:, P:2 * P], AX, ALU.max))
            link(v.tensor_scalar(s1[:], m_first[:], BIG, -BIG, ALU.mult, ALU.add))
            link(v.scalar_tensor_tensor(s1[:], m_first[:], cr[:, 0:1], s1[:], ALU.mult, ALU.add))
            link(v.tensor_tensor(s2[:], s2[:], s1[:], ALU.max))
            link(v.tensor_tensor(s2[:], s2[:], last[:], ALU.mult))
            v.tensor_tensor_scan(s1[:, ::-1], mask_f[:, 1:K + 1][:, ::-1], s2[:, ::-1], 0.0,
                                 ALU.mult, ALU.add).then_inc(scan_done, 1)
            dve.wait_ge(scan_done, q + 3)

            fix(q + 2, m_last)
            v.tensor_tensor(s2[:], s3[:], s1[:], ALU.subtract).then_inc(ex_in, 1)
            dve.wait_ge(ex_out, 1)
            v.tensor_tensor_scan(s1[:], msk, s2[:], 0.0, ALU.mult, ALU.add).then_inc(scan_done, 1)
            dve.wait_ge(scan_done, q + 4)
            fix(q + 3, m_first)
            link(v.tensor_scalar(s1[:], s1[:], 1e-6, None, ALU.max))
            link(v.reciprocal(s3[:], s1[:]))
            link(v.tensor_tensor(fm(A), row_t(XS), over_f_fm(s2[:]), ALU.mult))
            link(segment_sums(q + 4, A, B, A))
            dve.wait_ge(x3_back, 16)
            for g in range(GC):
                ks, cs = group(g)
                a = row(A)[:, ks, :]
                link(v.tensor_tensor(a, a, over_f(s3[:, ks]), ALU.mult))
                link(v.tensor_tensor(a, a, c_bias[:].unsqueeze(1).broadcast_to([P, KG, F]), ALU.add))
                link(v.tensor_tensor(A[:, cs], A[:, cs], XD[:, cs], ALU.add))
                layernorm(A, C, ks).then_inc(res_ready, 1)


def kernel(x, src, dst, edge_attr_10, edge_attr_3, edge_weight, L1_gnn_fc1_w1, L1_gnn_fc1_w2, L1_gnn_fc2_w1,
           L1_gnn_fc2_w2, L3_gnn_laplacian_lambda_max, L3_gnn_cheb_W, L3_gnn_cheb_b, L3_gnn_gat_Wsrc,
           L3_gnn_gat_bsrc, L3_gnn_gat_Wdst, L3_gnn_gat_bdst, L3_gnn_gat_attn, L3_gnn_gat_bias):
    import numpy as np
    import concourse.bacc as bacc
    from concourse.bass_utils import run_bass_kernel_spmd

    P, E = 128, src.shape[0]
    K = -(-E // P)
    pad = P * K - E

    def padded(a, value):
        a = np.asarray(a)
        return np.concatenate([a, np.full((pad,) + a.shape[1:], value, a.dtype)])

    def tiles(a, value):
        return np.ascontiguousarray(padded(a, value).reshape(P, -1))

    d = np.concatenate([np.full(1, -1, np.int32), padded(dst, 200000), np.full(1, -2, np.int32)])
    dst_ext = np.stack([d[p * K:p * K + K + 2] for p in range(P)])
    ea10 = padded(edge_attr_10, 0).reshape(P, K, -1)
    arrays = {
        "x": np.asarray(x),
        "dst_ext": dst_ext,
        "src_idx": tiles(src, 200000),
        "ea10_t": np.ascontiguousarray(ea10.transpose(2, 1, 0).reshape(ea10.shape[2], K * P)),
        "ea3": tiles(edge_attr_3, 1),
        "ew": tiles(edge_weight, 0),
        "w1cat": np.concatenate([np.asarray(L1_gnn_fc1_w1), np.asarray(L1_gnn_fc2_w1)], axis=1),
        "fc1_w2": np.asarray(L1_gnn_fc1_w2),
        "fc2_w2": np.asarray(L1_gnn_fc2_w2),
        "lam": np.asarray(L3_gnn_laplacian_lambda_max),
        "cheb_wt": np.ascontiguousarray(np.asarray(L3_gnn_cheb_W).T),
        "cheb_b": np.asarray(L3_gnn_cheb_b),
        "wsrc_t": np.ascontiguousarray(np.asarray(L3_gnn_gat_Wsrc).T),
        "bsrc": np.asarray(L3_gnn_gat_bsrc),
        "wdst_t": np.ascontiguousarray(np.asarray(L3_gnn_gat_Wdst).T),
        "bdst": np.asarray(L3_gnn_gat_bdst),
        "attn": np.asarray(L3_gnn_gat_attn).reshape(-1),
        "gat_bias": np.asarray(L3_gnn_gat_bias),
    }
    nc = bacc.Bacc("TRN2", target_bir_lowering=False, num_devices=1)
    aps = [nc.dram_tensor(f"in_{n}", a.shape, mybir.dt.from_np(a.dtype), kind="ExternalInput").ap()
           for n, a in arrays.items()]
    out = nc.dram_tensor("out_rows", x.shape, mybir.dt.float32, kind="ExternalOutput").ap()
    gnn_resnorm_kernel(nc, *aps, out)
    r = run_bass_kernel_spmd(nc, [{f"in_{n}": a for n, a in arrays.items()}], core_ids=[0])
    return r.results[0]["out_rows"]
```
